# Optimizing a Trainium2 kernel written in Bass

```python
import numpy as np
import jax
import jax.numpy as jnp

def _softmax(x, axis=-1):
    return jax.nn.softmax(x, axis=axis)

def _gelu(x):
    return jax.nn.gelu(x, approximate=True)

def _silu(x):
    return jax.nn.silu(x)

def _sigmoid(x):
    return jax.nn.sigmoid(x)

def _layernorm(x, axis=-1, eps=1e-05):
    m = jnp.mean(x, axis=axis, keepdims=True)
    v = jnp.var(x, axis=axis, keepdims=True)
    return (x - m) / jnp.sqrt(v + eps)

def _scatter_add(tgt, idx, src, axis=0):
    return tgt.at[idx].add(src)

def _segment_sum(src, seg, n):
    return jax.ops.segment_sum(src, seg, n)
kernel_name = 'mk_sandwich_d1_jaxref_r4_c8a413'

def setup_inputs(seed: int=0):
    np.random.seed(seed)
    _w = jnp.asarray

    def _L0_attn_setup():
        import jax, jax.numpy as jnp
        import numpy as np
        import math
        B, L, D, H = (2, 256, 256, 16)
        d = D // H
        key = jax.random.key(seed)
        ks = jax.random.split(key, 7)
        s = 1.0 / math.sqrt(D)
        sd = 1.0 / math.sqrt(d)
        return {'X': jax.random.normal(ks[0], (B, L, D), jnp.float32), 'q1_w': jax.random.normal(ks[1], (D, D), jnp.float32) * s, 'k1_w': jax.random.normal(ks[2], (D, D), jnp.float32) * s, 'k2_w': jax.random.normal(ks[3], (D, D), jnp.float32) * s, 'gw_w': jax.random.normal(ks[4], (1, d), jnp.float32) * sd, 'sw_w': jax.random.normal(ks[5], (1, d), jnp.float32) * sd, 'c_proj_w': jax.random.normal(ks[6], (D, D), jnp.float32) * s}
    _L0_attn_in = _L0_attn_setup()

    def _L0_ffn_setup():
        import jax, jax.numpy as jnp
        import numpy as np
        DIM = 256
        DEPTH = 2
        HEADS = 8
        DIM_HEAD = 64
        WINDOW = 128
        INNER = HEADS * DIM_HEAD
        HID = int(DIM * 4 * 2 / 3)
        B, N = (2, 2048)
        QK_SCALE = 8.0

        def shift_token(t):
            t1, t2 = jnp.split(t, 2, axis=-1)
            t2 = jnp.pad(t2, ((0, 0), (1, 0), (0, 0)))[:, :-1]
            return jnp.concatenate([t1, t2], axis=-1)

        def l2norm(t):
            return t / jnp.clip(jnp.linalg.norm(t, axis=-1, keepdims=True), 1e-12)

        def rotate_half(x):
            x1, x2 = jnp.split(x, 2, axis=-1)
            return jnp.concatenate([-x2, x1], axis=-1)

        def rotary_xpos(q, k):
            n = q.shape[-2]
            half_idx = jnp.arange(0, DIM_HEAD, 2, dtype=jnp.float32)
            inv_freq = 1.0 / 10000.0 ** (half_idx / DIM_HEAD)
            t = jnp.arange(n, dtype=jnp.float32)
            freqs = t[:, None] * inv_freq[None, :]
            freqs = jnp.concatenate([freqs, freqs], axis=-1)
            base = (half_idx + 0.4 * DIM_HEAD) / (1.4 * DIM_HEAD)
            power = (t - n // 2) / float(WINDOW // 2)
            scale = base[None, :] ** power[:, None]
            scale = jnp.concatenate([scale, scale], axis=-1)
            cos, sin = (jnp.cos(freqs), jnp.sin(freqs))
            q = q * cos * scale + rotate_half(q) * sin * scale
            k = k * cos / scale + rotate_half(k) * sin / scale
            return (q, k)

        def local_attention(q, k, v):
            b, h, n, d = q.shape
            w = n // WINDOW
            bq = q.reshape(b, h, w, WINDOW, d) * QK_SCALE
            bk = k.reshape(b, h, w, WINDOW, d)
            bv = v.reshape(b, h, w, WINDOW, d)

            def look_around(t):
                p = jnp.pad(t, ((0, 0), (0, 0), (1, 0), (0, 0), (0, 0)))
                return jnp.concatenate([p[:, :, :w], p[:, :, 1:]], axis=3)
            bk, bv = (look_around(bk), look_around(bv))
            bt = jnp.arange(n).reshape(w, WINDOW)
            btp = jnp.pad(bt, ((1, 0), (0, 0)), constant_values=-1)
            btk = jnp.concatenate([btp[:w], btp[1:]], axis=1)
            sim = jnp.einsum('bhwid,bhwjd->bhwij', bq, bk)
            i = bt[:, :, None]
            j = btk[:, None, :]
            mask = (i < j) | (i > j + WINDOW) | (j == -1)
            sim = jnp.where(mask, -jnp.finfo(sim.dtype).max, sim)
            attn = jax.nn.softmax(sim, axis=-1)
            out = jnp.einsum('bhwij,bhwjd->bhwid', attn, bv)
            return out.reshape(b, h, n, d)

        def _layer(x, wqkv, qs, ksc, wo, lg, lb, w1, b1, w2, b2):
            b, n, _ = x.shape
            h = shift_token(x)
            qkv = h @ wqkv
            q, k, v = jnp.split(qkv, 3, axis=-1)
            to_heads = lambda t: t.reshape(b, n, HEADS, DIM_HEAD).transpose(0, 2, 1, 3)
            q, k, v = (to_heads(q), to_heads(k), to_heads(v))
            q = l2norm(q) * qs
            k = l2norm(k) * ksc
            q, k = rotary_xpos(q, k)
            o = local_attention(q, k, v)
            o = o.transpose(0, 2, 1, 3).reshape(b, n, INNER)
            x = x + o @ wo
            h = shift_token(x)
            mu = h.mean(-1, keepdims=True)
            var = h.var(-1, keepdims=True)
            h = (h - mu) / jnp.sqrt(var + 1e-05) * lg + lb
            h = h @ w1 + b1
            a, g = jnp.split(h, 2, axis=-1)
            h = a * jax.nn.gelu(g, approximate=False)
            x = x + h @ w2 + b2
            return x
        key = jax.random.key(seed)
        ks = jax.random.split(key, 6)
        return {'x': jax.random.normal(ks[0], (B, N, DIM), jnp.float32), 'wqkv': jax.random.normal(ks[1], (DEPTH, DIM, 3 * INNER), jnp.float32) * 0.02, 'q_scale': jnp.ones((DEPTH, DIM_HEAD), jnp.float32), 'k_scale': jnp.ones((DEPTH, DIM_HEAD), jnp.float32), 'wo': jax.random.normal(ks[2], (DEPTH, INNER, DIM), jnp.float32) * 0.02, 'ln_g': jnp.ones((DEPTH, DIM), jnp.float32), 'ln_b': jnp.zeros((DEPTH, DIM), jnp.float32), 'w1': jax.random.normal(ks[3], (DEPTH, DIM, 2 * HID), jnp.float32) * 0.02, 'b1': jnp.zeros((DEPTH, 2 * HID), jnp.float32), 'w2': jax.random.normal(ks[4], (DEPTH, HID, DIM), jnp.float32) * 0.02, 'b2': jnp.zeros((DEPTH, DIM), jnp.float32)}
    _L0_ffn_in = _L0_ffn_setup()
    _d = {'L0_attn_X': _L0_attn_in['X'], 'L0_attn_q1_w': _L0_attn_in['q1_w'], 'L0_attn_k1_w': _L0_attn_in['k1_w'], 'L0_attn_k2_w': _L0_attn_in['k2_w'], 'L0_attn_gw_w': _L0_attn_in['gw_w'], 'L0_attn_sw_w': _L0_attn_in['sw_w'], 'L0_attn_c_proj_w': _L0_attn_in['c_proj_w'], 'L0_ffn_wqkv': _L0_ffn_in['wqkv'], 'L0_ffn_q_scale': _L0_ffn_in['q_scale'], 'L0_ffn_k_scale': _L0_ffn_in['k_scale'], 'L0_ffn_wo': _L0_ffn_in['wo'], 'L0_ffn_ln_g': _L0_ffn_in['ln_g'], 'L0_ffn_ln_b': _L0_ffn_in['ln_b'], 'L0_ffn_w1': _L0_ffn_in['w1'], 'L0_ffn_b1': _L0_ffn_in['b1'], 'L0_ffn_w2': _L0_ffn_in['w2'], 'L0_ffn_b2': _L0_ffn_in['b2']}
    _x0 = _d['L0_attn_X']
    _d['L0_attn_X'] = jax.random.normal(jax.random.fold_in(jax.random.key(seed), 1), (4, 1024, 256), dtype=_x0.dtype)
    del _x0
    return _d

def reference(L0_attn_X, L0_attn_q1_w, L0_attn_k1_w, L0_attn_k2_w, L0_attn_gw_w, L0_attn_sw_w, L0_attn_c_proj_w, L0_ffn_wqkv, L0_ffn_q_scale, L0_ffn_k_scale, L0_ffn_wo, L0_ffn_ln_g, L0_ffn_ln_b, L0_ffn_w1, L0_ffn_b1, L0_ffn_w2, L0_ffn_b2):

    def _L0_attn_ref(X, q1_w, k1_w, k2_w, gw_w, sw_w, c_proj_w):
        import jax, jax.numpy as jnp
        import numpy as np
        import math
        B, L, D, H = (2, 256, 256, 16)
        d = D // H
        b, l, dim = X.shape
        Q = (X @ q1_w.T).reshape(b, l, H, d)
        K = (X @ k1_w.T).reshape(b, l, H, d)
        V = X.reshape(b, l, H, d)
        W = K[..., :, None] * V[..., None, :]
        G = jax.nn.sigmoid(X.reshape(b, l, H, d) @ gw_w.T)
        G = jnp.clip(G, 1e-06, None)
        Gc = jnp.exp(jnp.clip(jnp.cumsum(jnp.log(G), axis=1), -30.0, 30.0)) + 1e-06
        Gc = Gc[..., None]
        R = jax.nn.silu(K @ sw_w.T)[..., None]
        Wc = jnp.cumsum(W * R / Gc, axis=1) * Gc
        O1 = jnp.einsum('blhd,blhde->blhe', Q, Wc)
        E = V[:, 1:] - O1[:, :-1]
        sqd = math.sqrt(d)
        Qm = Q[:, :-1] * (-1.0 / sqd)
        Qm = -jnp.where(Qm >= 0, Qm, 0.02 * Qm)
        K2 = X[:, :-1] @ k2_w.T
        K2 = jax.nn.sigmoid(K2 / math.sqrt(dim) * 0.02).reshape(b, l - 1, H, d)
        W2 = jnp.cumsum(K2[..., :, None] * E[..., None, :], axis=1)
        O2 = jnp.einsum('blhd,blhde->blhe', Qm, W2)
        O2 = jnp.concatenate([jnp.zeros_like(O2[:, :1]), O2], axis=1)
        out = (O1.reshape(b, l, dim) + O2.reshape(b, l, dim)) @ c_proj_w.T
        return out

    def _L0_ffn_ref(x, wqkv, q_scale, k_scale, wo, ln_g, ln_b, w1, b1, w2, b2):
        import jax, jax.numpy as jnp
        import numpy as np
        DIM = 256
        DEPTH = 2
        HEADS = 8
        DIM_HEAD = 64
        WINDOW = 128
        INNER = HEADS * DIM_HEAD
        HID = int(DIM * 4 * 2 / 3)
        B, N = (2, 2048)
        QK_SCALE = 8.0

        def shift_token(t):
            t1, t2 = jnp.split(t, 2, axis=-1)
            t2 = jnp.pad(t2, ((0, 0), (1, 0), (0, 0)))[:, :-1]
            return jnp.concatenate([t1, t2], axis=-1)

        def l2norm(t):
            return t / jnp.clip(jnp.linalg.norm(t, axis=-1, keepdims=True), 1e-12)

        def rotate_half(x):
            x1, x2 = jnp.split(x, 2, axis=-1)
            return jnp.concatenate([-x2, x1], axis=-1)

        def rotary_xpos(q, k):
            n = q.shape[-2]
            half_idx = jnp.arange(0, DIM_HEAD, 2, dtype=jnp.float32)
            inv_freq = 1.0 / 10000.0 ** (half_idx / DIM_HEAD)
            t = jnp.arange(n, dtype=jnp.float32)
            freqs = t[:, None] * inv_freq[None, :]
            freqs = jnp.concatenate([freqs, freqs], axis=-1)
            base = (half_idx + 0.4 * DIM_HEAD) / (1.4 * DIM_HEAD)
            power = (t - n // 2) / float(WINDOW // 2)
            scale = base[None, :] ** power[:, None]
            scale = jnp.concatenate([scale, scale], axis=-1)
            cos, sin = (jnp.cos(freqs), jnp.sin(freqs))
            q = q * cos * scale + rotate_half(q) * sin * scale
            k = k * cos / scale + rotate_half(k) * sin / scale
            return (q, k)

        def local_attention(q, k, v):
            b, h, n, d = q.shape
            w = n // WINDOW
            bq = q.reshape(b, h, w, WINDOW, d) * QK_SCALE
            bk = k.reshape(b, h, w, WINDOW, d)
            bv = v.reshape(b, h, w, WINDOW, d)

            def look_around(t):
                p = jnp.pad(t, ((0, 0), (0, 0), (1, 0), (0, 0), (0, 0)))
                return jnp.concatenate([p[:, :, :w], p[:, :, 1:]], axis=3)
            bk, bv = (look_around(bk), look_around(bv))
            bt = jnp.arange(n).reshape(w, WINDOW)
            btp = jnp.pad(bt, ((1, 0), (0, 0)), constant_values=-1)
            btk = jnp.concatenate([btp[:w], btp[1:]], axis=1)
            sim = jnp.einsum('bhwid,bhwjd->bhwij', bq, bk)
            i = bt[:, :, None]
            j = btk[:, None, :]
            mask = (i < j) | (i > j + WINDOW) | (j == -1)
            sim = jnp.where(mask, -jnp.finfo(sim.dtype).max, sim)
            attn = jax.nn.softmax(sim, axis=-1)
            out = jnp.einsum('bhwij,bhwjd->bhwid', attn, bv)
            return out.reshape(b, h, n, d)

        def _layer(x, wqkv, qs, ksc, wo, lg, lb, w1, b1, w2, b2):
            b, n, _ = x.shape
            h = shift_token(x)
            qkv = h @ wqkv
            q, k, v = jnp.split(qkv, 3, axis=-1)
            to_heads = lambda t: t.reshape(b, n, HEADS, DIM_HEAD).transpose(0, 2, 1, 3)
            q, k, v = (to_heads(q), to_heads(k), to_heads(v))
            q = l2norm(q) * qs
            k = l2norm(k) * ksc
            q, k = rotary_xpos(q, k)
            o = local_attention(q, k, v)
            o = o.transpose(0, 2, 1, 3).reshape(b, n, INNER)
            x = x + o @ wo
            h = shift_token(x)
            mu = h.mean(-1, keepdims=True)
            var = h.var(-1, keepdims=True)
            h = (h - mu) / jnp.sqrt(var + 1e-05) * lg + lb
            h = h @ w1 + b1
            a, g = jnp.split(h, 2, axis=-1)
            h = a * jax.nn.gelu(g, approximate=False)
            x = x + h @ w2 + b2
            return x
        for l in range(DEPTH):
            x = _layer(x, wqkv[l], q_scale[l], k_scale[l], wo[l], ln_g[l], ln_b[l], w1[l], b1[l], w2[l], b2[l])
        return x
    x = L0_attn_X
    x = x + _layernorm(_L0_attn_ref(_layernorm(x, axis=-1), L0_attn_q1_w, L0_attn_k1_w, L0_attn_k2_w, L0_attn_gw_w, L0_attn_sw_w, L0_attn_c_proj_w), axis=-1)
    x = x + _layernorm(_L0_ffn_ref(_layernorm(x, axis=-1), L0_ffn_wqkv, L0_ffn_q_scale, L0_ffn_k_scale, L0_ffn_wo, L0_ffn_ln_g, L0_ffn_ln_b, L0_ffn_w1, L0_ffn_b1, L0_ffn_w2, L0_ffn_b2), axis=-1)
    return x

_drawn_inputs = setup_inputs


def setup_inputs(seed=0):
    import zlib

    import numpy as np

    out = dict(_drawn_inputs(seed))
    spreads = {'L0_ffn_q_scale': (1.0, 0.6),
     'L0_ffn_k_scale': (1.0, 0.6),
     'L0_ffn_ln_g': (1.0, 0.6),
     'L0_ffn_ln_b': (0.0, 0.8),
     'L0_ffn_b1': (0.0, 0.8),
     'L0_ffn_b2': (0.0, 0.388)}
    factors = {'L0_attn_k2_w': 173.575, 'L0_ffn_w1': 2.791, 'L0_ffn_w2': 2.769}
    for name, (base, spread) in spreads.items():
        noise = np.random.default_rng([zlib.crc32(name.encode()), seed]).standard_normal(out[name].shape)
        drawn = base * np.exp(spread * noise) if base else spread * noise
        out[name] = jnp.asarray(drawn.astype(out[name].dtype))
    for name, factor in factors.items():
        out[name] = (out[name] * factor).astype(out[name].dtype)
    return out
```

```python
from contextlib import ExitStack

import concourse.bass as bass
from concourse import mybir

F32 = mybir.dt.float32
ALU = mybir.AluOpType
ACT = mybir.ActivationFunctionType
AX = mybir.AxisListType

P = 128
D = 256
KD = D // P
BATCH, SEQ = 4, 1024
CHUNKS = SEQ // P
UNITS = 2
PAIRS = BATCH // UNITS
LH, LD = 16, 16
LPAD = 32
LT = LH * LPAD // P
LPT = LH // LT
DEPTH = 2
AH, AD = 8, 64
INNER = AH * AD
AT = INNER // P
HID = 682
HT = (HID + P - 1) // P
HLAST = HID - (HT - 1) * P
QK_SCALE = 8.0
SLOT_OF = (0, 2, 1, 3)
MASKED = -1e30
EPS = 1e-5

LAYER_PE = ["hT", "qk", "v", "qkT", "sa", "sb", "pa", "pb", "av", "oT", "wo", "xs", "h2T", "w1g", "w1a", "w2"]
LAYER_ACT = ["hT", "xph", "qk", "sq", "v", "qkT", "ea", "eb", "pa", "oT", "xph2", "h2T", "gelu"]
LAYER_DVE = ["ss", "ss_clip", "t2", "rot", "sc8", "ma", "nba", "mb", "nbb", "pb", "rden", "on", "x",
             "st_a", "st_b", "ln_agg", "ln_eps", "hn", "hid", "x2"]
LAYER_POOL = ["tab", "t1", "rnorm", "kn", "ln_rstd", "xb2"]


def layered(names):
    return [f"{n}{l}" for l in range(DEPTH) for n in names]


PE_STEPS = ["xT", "qT", "kT", "tok", "cum", "s1a", "s1b", "o1", "shift", "s2a", "s2b", "o2", "OT", "cproj"] \
    + layered(LAYER_PE)
ACT_STEPS = ["XT_halo", "XT", "QT", "QmT", "KT", "K2T", "K2tok", "egate", "lnG", "eL", "O1p", "OT"] \
    + layered(LAYER_ACT)
DVE_STEPS = ["ln0_stats", "ln0_agg", "ln0_eps", "X", "Qm", "K2T", "Ktok", "rdot", "rsum", "K2tok", "gsum", "e1", "sig",
             "G", "R", "Lmin", "Lclip", "Gc", "rGc", "u", "A1a", "A1b", "O1", "dS1", "S1", "En", "En0",
             "A2a", "A2b", "O", "dS2", "S2", "lnc_stats", "lnc_agg", "lnc_eps", "lnc", "mid_x",
             "lnz_stats", "lnz_agg", "lnz_eps", "z"] + layered(LAYER_DVE) \
    + ["lnf_stats", "lnf_agg", "lnf_eps", "lnf", "out"]
POOL_STEPS = ["ln0_rstd", "gdot", "Vu", "acc", "lnc_rstd", "lnz_rstd"] + layered(LAYER_POOL) + ["lnf_rstd"]

LAYER_STAGES = ["h", "qk", "v", "rot", "qkT", "sa", "sb", "pa", "pb", "av", "oT", "wo", "xs", "h2T",
                "w1g", "w1a", "w2"]
STAGES = [(s, None) for s in ("ln0", "xT", "qT", "kT", "tok", "cum", "s1a", "s1b", "o1", "shift",
                              "s2a", "s2b", "o2", "OT", "cproj")] \
    + [(s, l) for l in range(DEPTH) for s in LAYER_STAGES] + [("out", None)]
ORDER = [(s, l, u) for s, l in STAGES for u in range(UNITS)]


class Done:

    def __init__(self, sems, steps):
        assert len(set(steps)) == len(steps)
        self.sems, self.steps, self.at = sems, steps, {n: i + 1 for i, n in enumerate(steps)}

    def value(self, step, chunk):
        return chunk * len(self.steps) + self.at[step]


def build(nc, x, xpos, q1T, k1T, k2T, gw, sw, cT, wqkv, qs, ks, wo, lg, lb, w1, b1, w2, b2, out):
    with ExitStack() as ctx:
        def sb(name, *shape):
            return ctx.enter_context(nc.sbuf_tensor(name, [P, *shape], F32))

        def sem(name):
            return ctx.enter_context(nc.semaphore(name))

        ident, shift, last, tri, ones = (sb(n, P) for n in ("ident", "shift", "last", "tri", "ones"))
        band = sb("band", 2 * P)
        heads = sb("heads", LPT * LD)
        row0 = sb("row0", 1)
        zero = sb("zero", 2 * LH)
        mhalf = sb("mhalf", LH)
        gwb, swb = sb("gwb", LD), sb("swb", LD)
        q1w, k1w, k2w = (sb(n, KD, LH, LPAD) for n in ("q1w", "k1w", "k2w"))
        cw = sb("cw", KD, D)
        wqkv_s = [sb(f"wqkv{l}", KD, 3 * INNER) for l in range(DEPTH)]
        wo_s = [sb(f"wo{l}", AT, D) for l in range(DEPTH)]
        w1_s = [sb(f"w1_{l}", KD, 2 * HID) for l in range(DEPTH)]
        w2_s = [sb(f"w2_{l}", HT, D) for l in range(DEPTH)]
        scales = [sb(f"scales{l}", 4, AD) for l in range(DEPTH)]
        lgc, lbc = ([sb(f"{n}{l}", KD) for l in range(DEPTH)] for n in ("lgc", "lbc"))
        b1a, b1g = ([sb(f"{n}{l}", HT) for l in range(DEPTH)] for n in ("b1a", "b1g"))
        b2b = [sb(f"b2b{l}", D) for l in range(DEPTH)]

        def per_unit(name, *shape):
            return [sb(f"{name}{u}", *shape) for u in range(UNITS)]

        xin, x1, X = per_unit("xin", D), per_unit("x1", D), per_unit("X", D)
        tab, tabl = per_unit("tab", 4, AD), per_unit("tabl", 4, AD)
        XT = per_unit("XT", KD, P + 1)
        big, mid = per_unit("big", 2048), per_unit("mid", 4 * (P + 1) * 2 + 2 * LT * P)
        Ktok, K2tok = per_unit("Ktok", LH, LPAD), per_unit("K2tok", LH, LPAD)
        Vu, O1, O1p, En = (per_unit(n, D) for n in ("Vu", "O1", "O1p", "En"))
        S1, S2 = per_unit("S1", LT, LPT * LD), per_unit("S2", LT, LPT * LD)
        acc = per_unit("acc", LH)
        vcur, hT, hn, scr, scr2, xo = (per_unit(n, w) for n, w in (
            ("vcur", INNER), ("hT", D), ("hn", D), ("scr", D), ("scr2", D), ("xo", D)))
        prevK = [[sb(f"prevK{l}_{u}", AT, P) for u in range(UNITS)] for l in range(DEPTH)]
        prevV = [[sb(f"prevV{l}_{u}", INNER) for u in range(UNITS)] for l in range(DEPTH)]
        xph = [[sb(f"xph{l}_{u}", P) for u in range(UNITS)] for l in range(DEPTH)]
        xph2 = [[sb(f"xph2{l}_{u}", P) for u in range(UNITS)] for l in range(DEPTH)]
        st6 = per_unit("st6", 2, 6)
        mv = per_unit("mv", 2)
        carry = per_unit("carry", 1)
        ve, rstd = per_unit("ve", 1), per_unit("rstd", 1)
        zz = per_unit("zz", 2 * LH)
        ez, sig = per_unit("ez", 2 * LH), per_unit("sig", 2 * LH)
        gr = per_unit("gr", 2 * LH)
        logG, lc, gc, rgc, uu = (per_unit(n, LH) for n in ("logG", "lc", "gc", "rgc", "uu"))
        ssq, rnorm = per_unit("ssq", 2 * AH), per_unit("rnorm", 2 * AH)
        sc8, mx, nb, den, rden = (per_unit(n, AH) for n in ("sc8", "mx", "nb", "den", "rden"))

        QT = [m[:, 0:516].rearrange("p (t n) -> p t n", t=LT) for m in mid]
        QmT = [m[:, 516:1032].rearrange("p (t n) -> p t n", t=LT) for m in mid]
        KT = [m[:, 1032:1544].rearrange("p (t n) -> p t n", t=LT) for m in mid]
        K2T = [m[:, 1544:2056].rearrange("p (t n) -> p t n", t=LT) for m in mid]
        qkraw = [m[:, 0:1024] for m in mid]
        qkrot = [m[:, 1024:2048] for m in mid]
        qkT = [m[:, 0:1024].rearrange("p (s t n) -> p s t n", s=2, t=AT) for m in mid]
        on = [m[:, 1024:1536] for m in mid]
        oT = [m[:, 1536:2048].rearrange("p (t n) -> p t n", t=AT) for m in mid]

        slA = [ctx.enter_context(nc.psum_tensor(f"slA{u}", [P, 1024], F32)) for u in range(UNITS)]
        slB = [ctx.enter_context(nc.psum_tensor(f"slB{u}", [P, 1024], F32)) for u in range(UNITS)]

        pe_done = Done([sem(f"pe_done{u}") for u in range(UNITS)], PE_STEPS)
        act_done = Done([sem(f"act_done{u}") for u in range(UNITS)], ACT_STEPS)
        dve_done = Done([sem(f"dve_done{u}") for u in range(UNITS)], DVE_STEPS)
        pool_done = Done([sem(f"pool_done{u}") for u in range(UNITS)], POOL_STEPS)
        x_in, tab_in = ([sem(f"{n}{u}") for u in range(UNITS)] for n in ("x_in", "tab_in"))
        kv_kept = [[sem(f"kv_kept{l}_{u}") for u in range(UNITS)] for l in range(DEPTH)]
        stored = [sem(f"stored{u}") for u in range(UNITS)]
        w_first, w_rest, stage_in, padded, made, made2 = (sem(n) for n in (
            "w_first", "w_rest", "stage_in", "padded", "made", "made2"))

        class Prog:

            def __init__(self, eng, done):
                self.eng, self.done, self.n = eng, done, [0] * UNITS

            def start(self, chunk, first):
                self.chunk, self.first, self.n = chunk, first, [0] * UNITS

            def wait(self, done, u, step):
                self.eng.wait_ge(done.sems[u], done.value(step, self.chunk))

            def wait_before(self, done, u, step):
                if not self.first:
                    self.eng.wait_ge(done.sems[u], done.value(step, self.chunk) - len(done.steps))

            def inc(self, u, step):
                assert self.done.steps[self.n[u]] == step, (self.done.steps[self.n[u]], step)
                self.n[u] += 1
                return self.done.sems[u], 1

        def walk(eng, prog, stage):
            with eng.Fori(0, PAIRS) as pair:
                prog.start(pair * CHUNKS, True)
                prog.pair, prog.c = pair, 0
                for s, l, u in ORDER:
                    stage(s, l, u)
                with eng.Fori(1, CHUNKS) as c:
                    prog.start(pair * CHUNKS + c, False)
                    prog.pair, prog.c = pair, c
                    for s, l, u in ORDER:
                        stage(s, l, u)
                for u in range(UNITS):
                    eng.wait_ge(stored[u], pair * (CHUNKS * 16) + CHUNKS * 16)
                    for l in range(DEPTH):
                        eng.wait_ge(kv_kept[l][u], pair * (CHUNKS * 32) + CHUNKS * 32)

        block = ctx.enter_context(nc.Block())

        @block.sync
        def _(sp):
            def load(dst, src, s):
                sp.dma_start(dst, src).then_inc(s, 16)

            for i, w in enumerate((q1T, k1T, k2T)):
                load(big[0][:, 512 * i:512 * i + 512].rearrange("p (k n) -> p k n", k=KD),
                     w.rearrange("(k p) n -> p k n", p=P), stage_in)
            load(gwb[:, :], gw.partition_broadcast(P), w_first)
            load(swb[:, :], sw.partition_broadcast(P), w_first)
            load(cw[:, :, :], cT.rearrange("(k p) n -> p k n", p=P), w_first)
            for l in range(DEPTH):
                load(wqkv_s[l][:, :, :], wqkv[l].rearrange("(k p) n -> p k n", p=P), w_rest)
                load(wo_s[l][:, :, :], wo[l].rearrange("(k p) n -> p k n", p=P), w_rest)
                load(w1_s[l][:, :, :], w1[l].rearrange("(k p) n -> p k n", p=P), w_rest)
                load(w2_s[l][:, 0:HT - 1, :], w2[l, 0:(HT - 1) * P].rearrange("(k p) n -> p k n", p=P), w_rest)
                load(w2_s[l][0:HLAST, HT - 1, :], w2[l, (HT - 1) * P:HID], w_rest)
                for i, s in ((0, qs), (2, ks)):
                    row = s[l].rearrange("(a n) -> a n", a=1)
                    half = AD // 2
                    load(scales[l][:, i, :], row.partition_broadcast(P), w_rest)
                    load(scales[l][:, i + 1, 0:half], row[:, half:AD].partition_broadcast(P), w_rest)
                    load(scales[l][:, i + 1, half:AD], row[:, 0:half].partition_broadcast(P), w_rest)
                load(b2b[l][:, :], b2[l].rearrange("(a n) -> a n", a=1).partition_broadcast(P), w_rest)
                with nc.allow_non_contiguous_dma("bias columns, once"):
                    load(lgc[l][:, :], lg[l].rearrange("(k p) -> p k", p=P), w_rest)
                    load(lbc[l][:, :], lb[l].rearrange("(k p) -> p k", p=P), w_rest)
                    for dst, o in ((b1a, 0), (b1g, HID)):
                        load(dst[l][:, 0:HT - 1], b1[l, o:o + (HT - 1) * P].rearrange("(k p) -> p k", p=P), w_rest)
                        load(dst[l][0:HLAST, HT - 1:HT],
                             b1[l, o + (HT - 1) * P:o + HID].rearrange("(p k) -> p k", k=1), w_rest)

            prog = Prog(sp, None)

            def load_x(u, pair, c):
                sp.dma_start(xin[u][:, :], x[bass.ds((pair * UNITS + u) * SEQ + c * P, P), :]).then_inc(x_in[u], 16)

            def load_tab(u, c):
                sp.dma_start(tab[u][:, :, :].rearrange("p a n -> p (a n)"),
                             xpos[bass.ds(c * P, P), :]).then_inc(tab_in[u], 16)

            def chunk(pair, c, following):
                prog.start(pair * CHUNKS + c, False)
                for l in range(DEPTH):
                    if l == 0 and following:
                        for u in range(UNITS):
                            prog.wait(dve_done, u, "mid_x")
                            load_x(u, *following)
                    for u in range(UNITS):
                        prog.wait(pe_done, u, f"av{l}")
                        sp.dma_start(prevK[l][u][:, :, :], qkT[u][:, 1, :, :]).then_inc(kv_kept[l][u], 16)
                        sp.dma_start(prevV[l][u][:, :], vcur[u][:, :]).then_inc(kv_kept[l][u], 16)
                        if l == DEPTH - 1 and following:
                            prog.wait(pool_done, u, f"tab{l}")
                            load_tab(u, following[1])

            for u in range(UNITS):
                load_x(u, 0, 0)
                load_tab(u, 0)
            for pair in range(PAIRS):
                with sp.Fori(0, CHUNKS - 1) as c:
                    chunk(pair, c, (pair, c + 1))
                chunk(pair, CHUNKS - 1, (pair + 1, 0) if pair < PAIRS - 1 else None)
            for u in range(UNITS):
                sp.wait_ge(stored[u], PAIRS * CHUNKS * 16)
                for l in range(DEPTH):
                    sp.wait_ge(kv_kept[l][u], PAIRS * CHUNKS * 32)

        @block.gpsimd
        def _(pool):
            g = nc.gpsimd
            for t, v in ((ident, 0.0), (shift, 0.0), (last, 0.0), (tri, 1.0), (ones, 1.0), (band, 0.0),
                         (row0, 1.0), (zero, 0.0), (mhalf, -0.5), (heads, 1.0)):
                g.memset(t[:, :], v).then_inc(made, 1)
            for t in (*Ktok, *K2tok, q1w, k1w, k2w):
                g.memset(t[:], 0.0).then_inc(made, 1)
            pool.wait_ge(made, 10 + 2 * UNITS + 3)

            def sel(t, pattern, base, mult, op, fill):
                g.affine_select(out=t, in_=t, pattern=pattern, base=base, channel_multiplier=mult,
                                compare_op=op, fill=fill).then_inc(made2, 1)
            sel(ident[:, :], [[-1, P]], 0, 1, ALU.not_equal, 1.0)
            sel(shift[:, :], [[-1, P]], 1, 1, ALU.not_equal, 1.0)
            sel(last[:, :], [[-1, P]], -(P - 1), 1, ALU.not_equal, 1.0)
            sel(tri[:, :], [[1, P]], 0, -1, ALU.is_ge, 0.0)
            sel(band[:, 0:P], [[1, P]], 0, -1, ALU.is_ge, MASKED)
            sel(band[:, P:2 * P], [[-1, P]], 0, 1, ALU.is_ge, MASKED)
            sel(row0[:, :], [[0, 1]], 0, 1, ALU.not_equal, 0.0)
            hv = heads[:, :].rearrange("p (h e) -> p h e", h=LPT)
            sel(hv, [[-LPAD, LPT], [0, LD]], 0, 1, ALU.is_ge, 0.0)
            pool.wait_ge(made2, 8)
            sel(hv, [[LPAD, LPT], [0, LD]], LPAD - 1, -1, ALU.is_ge, 0.0)
            pool.wait_ge(w_first, 16 * 3)
            pool.wait_ge(w_rest, 16 * 2 * 18)
            prog = Prog(pool, pool_done)
            W, WB, I = prog.wait, prog.wait_before, prog.inc

            def rstd_of(u, name):
                W(dve_done, u, name + "_eps")
                g.tensor_tensor(rstd[u][:, :], ve[u][:, :], mhalf[:, 0:1], ALU.pow).then_inc(*I(u, name + "_rstd"))

            def stage(s, l, u):
                if s == "ln0":
                    rstd_of(u, "ln0")
                elif s == "tok":
                    W(dve_done, u, "X")
                    g.tensor_tensor(scr2[u][:, :].rearrange("p (h d) -> p h d", h=LH),
                                    X[u][:, :].rearrange("p (h d) -> p h d", h=LH),
                                    gwb[:, None, :].to_broadcast([P, LH, LD]), ALU.mult).then_inc(*I(u, "gdot"))
                elif s == "cum":
                    W(dve_done, u, "u")
                    g.tensor_tensor(Vu[u][:, :].rearrange("p (h d) -> p h d", h=LH),
                                    X[u][:, :].rearrange("p (h d) -> p h d", h=LH),
                                    uu[u][:, :, None].to_broadcast([P, LH, LD]), ALU.mult).then_inc(*I(u, "Vu"))
                    prev = zero[:, 0:LH] if prog.first else acc[u][:, :]
                    g.tensor_tensor(acc[u][:, :], prev, logG[u][:, :], ALU.add).then_inc(*I(u, "acc"))
                elif s == "cproj":
                    rstd_of(u, "lnc")
                    rstd_of(u, "lnz")
                elif s == "h":
                    pool.wait_ge(tab_in[u], (prog.chunk + 1) * 16)
                    g.tensor_tensor(tabl[u][:, :, :], tab[u][:, :, :], scales[l][:, :, :],
                                    ALU.mult).then_inc(*I(u, f"tab{l}"))
                elif s == "rot":
                    W(pool_done, u, f"tab{l}")
                    W(act_done, u, f"qk{l}")
                    g.tensor_tensor(qkrot[u].rearrange("p (s h d) -> p s h d", s=2, h=AH),
                                    qkraw[u].rearrange("p (s h d) -> p s h d", s=2, h=AH),
                                    tabl[u][:, 0:4:2, None, :].to_broadcast([P, 2, AH, AD]),
                                    ALU.mult).then_inc(*I(u, f"t1{l}"))
                    W(dve_done, u, f"ss_clip{l}")
                    g.tensor_tensor(rnorm[u][:, :], ssq[u][:, :], mhalf[:, :], ALU.pow).then_inc(*I(u, f"rnorm{l}"))
                    W(pool_done, u, f"rnorm{l}")
                    W(dve_done, u, f"rot{l}")
                    k = qkrot[u][:, INNER:2 * INNER].rearrange("p (h d) -> p h d", h=AH)
                    g.tensor_tensor(k, k, rnorm[u][:, AH:2 * AH, None].to_broadcast([P, AH, AD]),
                                    ALU.mult).then_inc(*I(u, f"kn{l}"))
                elif s == "xs":
                    W(dve_done, u, f"ln_eps{l}")
                    g.tensor_tensor(rstd[u][:, :], ve[u][:, :], mhalf[:, 0:1], ALU.pow).then_inc(*I(u, f"ln_rstd{l}"))
                elif s == "w1g":
                    W(act_done, u, f"xph2{l}")
                    W(dve_done, u, f"hn{l}")
                    g.tensor_tensor(X[u][:, :], X[u][:, :], b2b[l][:, :], ALU.add).then_inc(*I(u, f"xb2{l}"))
                elif s == "out":
                    rstd_of(u, "lnf")

            walk(pool, prog, stage)

        @block.scalar
        def _(act):
            def A(out_, in_, func, **kw):
                return nc.scalar.activation(out_, in_, func, **kw)

            act.wait_ge(stage_in, 48)
            act.wait_ge(made, 10 + 2 * UNITS + 3)
            for i, w in enumerate((q1w, k1w, k2w)):
                A(w[:, :, :, 0:LD], big[0][:, 512 * i:512 * i + 512].rearrange("p (k h d) -> p k h d", k=KD, h=LH),
                  ACT.Copy).then_inc(padded, 1)
            act.wait_ge(padded, 3)
            act.wait_ge(made2, 9)
            act.wait_ge(w_rest, 16 * 2 * 18)
            prog = Prog(act, act_done)
            W, WB, I = prog.wait, prog.wait_before, prog.inc

            def stage(s, l, u):
                if s == "ln0":
                    WB(pe_done, u, "tok")
                    halo = zero[:, 0:KD, None] if prog.first else XT[u][:, :, P:P + 1]
                    A(XT[u][:, :, 0:1], halo, ACT.Copy).then_inc(*I(u, "XT_halo"))
                elif s == "xT":
                    W(pe_done, u, "xT")
                    W(act_done, u, "XT_halo")
                    A(XT[u][:, :, 1:P + 1], slA[u][:, 0:D].rearrange("p (k n) -> p k n", k=KD),
                      ACT.Copy).then_inc(*I(u, "XT"))
                elif s == "qT":
                    W(pe_done, u, "qT")
                    if not prog.first:
                        act.wait_ge(kv_kept[DEPTH - 1][u], prog.chunk * 32)
                    q = slB[u][:, :].rearrange("p (t n) -> p t n", t=LT)[:, :, 0:P + 1]
                    A(QT[u], q, ACT.Copy).then_inc(*I(u, "QT"))
                    A(QmT[u], q, ACT.Copy, scale=-1.0 / LD ** 0.5).then_inc(*I(u, "QmT"))
                elif s == "kT":
                    W(pe_done, u, "kT")
                    A(KT[u], slA[u][:, 0:512].rearrange("p (t n) -> p t n", t=LT), ACT.Copy).then_inc(*I(u, "KT"))
                    A(K2T[u], slA[u][:, 512:1024].rearrange("p (t n) -> p t n", t=LT), ACT.Tanh,
                      scale=0.01 / D ** 0.5).then_inc(*I(u, "K2T"))
                elif s == "tok":
                    W(pe_done, u, "tok")
                    A(K2tok[u][:, :, 0:LD], slB[u][:, 512:512 + D].rearrange("p (h d) -> p h d", h=LH), ACT.Tanh,
                      scale=0.01 / D ** 0.5).then_inc(*I(u, "K2tok"))
                    W(dve_done, u, "gsum")
                    A(ez[u][:, :], zz[u][:, :], ACT.Exp, scale=-1.0).then_inc(*I(u, "egate"))
                elif s == "cum":
                    W(dve_done, u, "G")
                    A(logG[u][:, :], gr[u][:, 0:LH], ACT.Ln).then_inc(*I(u, "lnG"))
                elif s == "s1a":
                    W(dve_done, u, "Lclip")
                    A(gc[u][:, :], lc[u][:, :], ACT.Exp).then_inc(*I(u, "eL"))
                elif s == "shift":
                    W(pe_done, u, "shift")
                    A(O1p[u][:, :], O1[u][:, :], ACT.Copy).then_inc(*I(u, "O1p"))
                elif s == "OT":
                    W(pe_done, u, "OT")
                    A(hT[u][:, :], slB[u][:, 0:D], ACT.Copy).then_inc(*I(u, "OT"))
                elif s == "h":
                    W(pe_done, u, f"hT{l}")
                    A(hT[u][:, :], slB[u][:, 0:D], ACT.Copy).then_inc(*I(u, f"hT{l}"))
                    A(xph[l][u][:, :], X[u][:, P:D], ACT.Copy).then_inc(*I(u, f"xph{l}"))
                elif s == "qk":
                    W(pe_done, u, f"qk{l}")
                    if l:
                        act.wait_ge(kv_kept[l - 1][u], (prog.chunk + 1) * 32)
                    A(qkraw[u], slA[u][:, :], ACT.Copy).then_inc(*I(u, f"qk{l}"))
                    A(big[u][:, 0:1024], slA[u][:, :], ACT.Square).then_inc(*I(u, f"sq{l}"))
                elif s == "v":
                    W(pe_done, u, f"v{l}")
                    if l:
                        act.wait_ge(kv_kept[l - 1][u], (prog.chunk + 1) * 32)
                    elif not prog.first:
                        act.wait_ge(kv_kept[DEPTH - 1][u], prog.chunk * 32)
                    A(vcur[u][:, :], slB[u][:, 0:INNER], ACT.Copy).then_inc(*I(u, f"v{l}"))
                elif s == "qkT":
                    W(pe_done, u, f"qkT{l}")
                    A(qkT[u].rearrange("p s t n -> p (s t n)"), slA[u][:, :], ACT.Copy).then_inc(*I(u, f"qkT{l}"))
                elif s in ("pa", "pb") or s in ("sa", "sb"):
                    if s in ("sa", "sb"):
                        W(dve_done, u, f"nb{s[1]}{l}")
                        lo = P if prog.first else 0
                        for h in range(4 * (s == "sb"), 4 * (s == "sb") + 4):
                            p = big[u][:, 256 * h + lo:256 * h + 256]
                            ins = A(p, p, ACT.Exp, bias=nb[u][:, h:h + 1], scale=sc8[u][:, h:h + 1],
                                    accum_out=den[u][:, h:h + 1])
                        ins.then_inc(*I(u, f"e{s[1]}{l}"))
                    if s == "pa":
                        W(pe_done, u, f"pa{l}")
                        lo = P if prog.first else 0
                        A(big[u][:, 0:1024].rearrange("p (h n) -> p h n", h=4)[:, :, lo:256],
                          slA[u][:, :].rearrange("p (h n) -> p h n", h=4)[:, :, lo:256],
                          ACT.Copy).then_inc(*I(u, f"pa{l}"))
                elif s == "oT":
                    W(pe_done, u, f"oT{l}")
                    A(oT[u].rearrange("p t n -> p (t n)"), slB[u][:, 0:INNER], ACT.Copy).then_inc(*I(u, f"oT{l}"))
                elif s == "xs":
                    W(pe_done, u, f"xs{l}")
                    A(xph2[l][u][:, :], X[u][:, P:D], ACT.Copy).then_inc(*I(u, f"xph2{l}"))
                elif s == "h2T":
                    W(pe_done, u, f"h2T{l}")
                    for k in range(KD):
                        ins = A(hT[u][:, k * P:(k + 1) * P], slA[u][:, k * P:(k + 1) * P], ACT.Identity,
                                scale=lgc[l][:, k:k + 1], bias=lbc[l][:, k:k + 1])
                    ins.then_inc(*I(u, f"h2T{l}"))
                elif s == "w1g":
                    W(pe_done, u, f"w1g{l}")
                    for j in range(HT):
                        m = P if j < HT - 1 else HLAST
                        ins = A(big[u][0:m, j * P:(j + 1) * P], slB[u][0:m, j * P:(j + 1) * P], ACT.Gelu,
                                bias=b1g[l][0:m, j:j + 1])
                    ins.then_inc(*I(u, f"gelu{l}"))
                elif s == "out":
                    W(dve_done, u, "out")
                    row = (prog.pair * UNITS + u) * SEQ + prog.c * P
                    act.dma_start(out[bass.ds(row, P), :], xo[u][:, :]).then_inc(stored[u], 16)

            walk(act, prog, stage)

        @block.tensor
        def _(pe):
            mm, tr = nc.tensor.matmul, nc.tensor.transpose
            pe.wait_ge(padded, 3)
            pe.wait_ge(made2, 9)
            pe.wait_ge(w_first, 16 * 3)
            pe.wait_ge(w_rest, 16 * 2 * 18)
            prog = Prog(pe, pe_done)
            W, WB, I = prog.wait, prog.wait_before, prog.inc

            def scores(u, slot, k_rows, q_rows, q0, groups):
                for t in range(LT):
                    for i, g in enumerate(groups):
                        r = g * LPAD
                        ins = mm(slot[u][:, (i * LT + t) * P:(i * LT + t + 1) * P], k_rows[u][r:r + LPAD, t, :],
                                 q_rows[u][r:r + LPAD, t, q0:q0 + P], start=True, stop=True)
                return ins

            def read_out(u, slot, q_rows, q0, state, v, k_tok):
                first = True
                if not prog.first:
                    for t in range(LT):
                        mm(slot[u][:, t * 64:t * 64 + 64], q_rows[u][:, t, q0:q0 + P], state[u][:, t, :],
                           start=first, stop=False, skip_group_check=True)
                        first = False
                for h in range(LH):
                    at = (h % LPT * LT + h // LPT) * P
                    mm(slot[u][:, h * LD:(h + 1) * LD], big[u][:, at:at + P], v[u][:, h * LD:(h + 1) * LD],
                       start=first, stop=h == LH - 1, skip_group_check=True)
                    first = False
                for t in range(LT):
                    ins = mm(slot[u][:, 512 + t * 64:576 + t * 64],
                             k_tok[u][:, t * LPT:(t + 1) * LPT, :].rearrange("p h d -> p (h d)"),
                             v[u][:, t * 64:(t + 1) * 64], start=True, stop=True)
                return ins

            def stage(s, l, u):
                A, B = slA[u], slB[u]
                if s == "xT":
                    W(dve_done, u, "X")
                    WB(dve_done, u, f"hid{DEPTH - 1}")
                    for k in range(KD):
                        ins = tr(A[:, k * P:(k + 1) * P], X[u][:, k * P:(k + 1) * P], ident[:, :])
                    ins.then_inc(*I(u, "xT"))
                elif s == "qT":
                    W(act_done, u, "XT")
                    WB(dve_done, u, f"x2{DEPTH - 1}")
                    for t in range(LT):
                        for k in range(KD):
                            ins = mm(B[:, t * 256:t * 256 + P + 1],
                                     q1w[:, k, t * LPT:(t + 1) * LPT, :].rearrange("p h d -> p (h d)"),
                                     XT[u][:, k, :], start=k == 0, stop=k == KD - 1)
                    ins.then_inc(*I(u, "qT"))
                elif s == "kT":
                    for i, (w, c0) in enumerate(((k1w, 1), (k2w, 0))):
                        for t in range(LT):
                            for k in range(KD):
                                ins = mm(A[:, 512 * i + t * P:512 * i + (t + 1) * P],
                                         w[:, k, t * LPT:(t + 1) * LPT, :].rearrange("p h d -> p (h d)"),
                                         XT[u][:, k, c0:c0 + P], start=k == 0, stop=k == KD - 1)
                    ins.then_inc(*I(u, "kT"))
                elif s == "tok":
                    W(dve_done, u, "Qm")
                    for i, (w, c0) in enumerate(((k1w, 1), (k2w, 0))):
                        for k in range(KD):
                            ins = mm(B[:, 512 * i:512 * i + D], XT[u][:, k, c0:c0 + P], w[:, k, :, 0:LD],
                                     start=k == 0, stop=k == KD - 1)
                    ins.then_inc(*I(u, "tok"))
                elif s == "cum":
                    W(act_done, u, "lnG")
                    W(act_done, u, "K2T")
                    ins = mm(A[:, 0:LH], tri[:, :], logG[u][:, :], start=True, stop=prog.first)
                    if not prog.first:
                        WB(pool_done, u, "acc")
                        ins = mm(A[:, 0:LH], ones[:, :], acc[u][:, :], start=False, stop=True)
                    ins.then_inc(*I(u, "cum"))
                elif s == "s1a":
                    W(dve_done, u, "Lmin")
                    scores(u, slA, KT, QT, 1, (0, 1)).then_inc(*I(u, "s1a"))
                elif s == "s1b":
                    W(dve_done, u, "K2tok")
                    scores(u, slB, KT, QT, 1, (2, 3)).then_inc(*I(u, "s1b"))
                elif s == "o1":
                    W(dve_done, u, "A1b")
                    W(pool_done, u, "Vu")
                    read_out(u, slA, QT, 1, S1, Vu, Ktok).then_inc(*I(u, "o1"))
                elif s == "shift":
                    W(dve_done, u, "O1")
                    ins = mm(B[:, 0:D], shift[:, :], O1[u][:, :], start=True, stop=prog.first)
                    if not prog.first:
                        ins = mm(B[:, 0:D], last[:, :], O1p[u][:, :], start=False, stop=True)
                    ins.then_inc(*I(u, "shift"))
                elif s == "s2a":
                    W(dve_done, u, "dS1")
                    W(dve_done, u, "K2T")
                    scores(u, slA, K2T, QmT, 0, (0, 1)).then_inc(*I(u, "s2a"))
                elif s == "s2b":
                    W(dve_done, u, "En")
                    scores(u, slB, K2T, QmT, 0, (2, 3)).then_inc(*I(u, "s2b"))
                elif s == "o2":
                    W(dve_done, u, "A2b")
                    read_out(u, slA, QmT, 0, S2, En, K2tok).then_inc(*I(u, "o2"))
                elif s == "OT":
                    W(dve_done, u, "O")
                    for k in range(KD):
                        ins = tr(B[:, k * P:(k + 1) * P], En[u][:, k * P:(k + 1) * P], ident[:, :])
                    ins.then_inc(*I(u, "OT"))
                elif s == "cproj":
                    W(act_done, u, "OT")
                    W(dve_done, u, "dS2")
                    for k in range(KD):
                        ins = mm(A[:, 0:D], hT[u][:, k * P:(k + 1) * P], cw[:, k, :], start=k == 0, stop=k == KD - 1)
                    ins.then_inc(*I(u, "cproj"))
                elif s == "h":
                    W(dve_done, u, f"x2{l - 1}" if l else "z")
                    tr(B[:, 0:P], X[u][:, 0:P], ident[:, :])
                    ins = mm(B[:, P:D], X[u][:, P:D], shift[:, :], start=True, stop=prog.first)
                    if not prog.first:
                        WB(act_done, u, f"xph{l}")
                        ins = mm(B[:, P:D], xph[l][u][:, :], last[:, :], start=False, stop=True)
                    ins.then_inc(*I(u, f"hT{l}"))
                elif s == "qk":
                    W(act_done, u, f"hT{l}")
                    W(dve_done, u, f"hid{l - 1}" if l else "lnc")
                    for n in range(2):
                        for k in range(KD):
                            ins = mm(A[:, n * 512:(n + 1) * 512], hT[u][:, k * P:(k + 1) * P],
                                     wqkv_s[l][:, k, n * 512:(n + 1) * 512], start=k == 0, stop=k == KD - 1)
                    ins.then_inc(*I(u, f"qk{l}"))
                elif s == "v":
                    for k in range(KD):
                        ins = mm(B[:, 0:512], hT[u][:, k * P:(k + 1) * P], wqkv_s[l][:, k, 1024:1536],
                                 start=k == 0, stop=k == KD - 1)
                    ins.then_inc(*I(u, f"v{l}"))
                elif s == "qkT":
                    W(pool_done, u, f"kn{l}")
                    W(act_done, u, f"sq{l}")
                    for i in range(2 * AT):
                        ins = tr(A[:, i * P:(i + 1) * P], qkrot[u][:, i * P:(i + 1) * P], ident[:, :])
                    ins.then_inc(*I(u, f"qkT{l}"))
                elif s in ("sa", "sb"):
                    if s == "sa":
                        W(act_done, u, f"qkT{l}")
                        if not prog.first:
                            pe.wait_ge(kv_kept[l][u], prog.chunk * 32)
                    else:
                        W(act_done, u, f"v{l}")
                    slot = A if s == "sa" else B
                    for i in range(4):
                        h = 4 * (s == "sb") + i
                        r = AD * (h % 2)
                        at = 256 * SLOT_OF[i]
                        q = qkT[u][r:r + AD, 0, h // 2, :]
                        if not prog.first:
                            mm(slot[:, at:at + P], q, prevK[l][u][r:r + AD, h // 2, :],
                               start=True, stop=True)
                        ins = mm(slot[:, at + P:at + 256], q, qkT[u][r:r + AD, 1, h // 2, :],
                                 start=True, stop=True)
                    ins.then_inc(*I(u, f"{s}{l}"))
                elif s in ("pa", "pb"):
                    W(act_done, u, f"e{s[1]}{l}")
                    W(dve_done, u, f"m{s[1]}{l}")
                    slot = A if s == "pa" else B
                    for i in range(4):
                        h = 4 * (s == "pb") + i
                        for j in range(prog.first, 2):
                            ins = tr(slot[:, 256 * i + j * P:256 * i + (j + 1) * P],
                                     big[u][:, 256 * h + j * P:256 * h + (j + 1) * P], ident[:, :])
                    ins.then_inc(*I(u, f"{s}{l}"))
                elif s == "av":
                    W(act_done, u, f"pa{l}")
                    W(dve_done, u, f"pb{l}")
                    for h in range(AH):
                        o = A[:, h * AD:(h + 1) * AD]
                        if not prog.first:
                            mm(o, big[u][:, 256 * h:256 * h + P], prevV[l][u][:, h * AD:(h + 1) * AD],
                               start=True, stop=False)
                        ins = mm(o, big[u][:, 256 * h + P:256 * h + 256], vcur[u][:, h * AD:(h + 1) * AD],
                                 start=prog.first, stop=True)
                    ins.then_inc(*I(u, f"av{l}"))
                elif s == "oT":
                    W(dve_done, u, f"on{l}")
                    for t in range(AT):
                        ins = tr(B[:, t * P:(t + 1) * P], on[u][:, t * P:(t + 1) * P], ident[:, :])
                    ins.then_inc(*I(u, f"oT{l}"))
                elif s == "wo":
                    W(act_done, u, f"oT{l}")
                    for t in range(AT):
                        ins = mm(A[:, 0:D], oT[u][:, t, :], wo_s[l][:, t, :], start=t == 0, stop=t == AT - 1)
                    ins.then_inc(*I(u, f"wo{l}"))
                elif s == "xs":
                    W(dve_done, u, f"x{l}")
                    ins = mm(B[:, 0:P], shift[:, :], X[u][:, P:D], start=True, stop=prog.first)
                    if not prog.first:
                        WB(act_done, u, f"xph2{l}")
                        ins = mm(B[:, 0:P], last[:, :], xph2[l][u][:, :], start=False, stop=True)
                    ins.then_inc(*I(u, f"xs{l}"))
                elif s == "h2T":
                    W(dve_done, u, f"hn{l}")
                    for k in range(KD):
                        ins = tr(A[:, k * P:(k + 1) * P], hn[u][:, k * P:(k + 1) * P], ident[:, :])
                    ins.then_inc(*I(u, f"h2T{l}"))
                elif s in ("w1g", "w1a"):
                    W(act_done, u, f"h2T{l}")
                    slot, o = (B, HID) if s == "w1g" else (A, 0)
                    for j in range(HT):
                        m = P if j < HT - 1 else HLAST
                        for k in range(KD):
                            ins = mm(slot[0:m, j * P:(j + 1) * P], w1_s[l][:, k, o + j * P:o + j * P + m],
                                     hT[u][:, k * P:(k + 1) * P], start=k == 0, stop=k == KD - 1)
                    ins.then_inc(*I(u, f"{s}{l}"))
                elif s == "w2":
                    W(dve_done, u, f"hid{l}")
                    for j in range(HT):
                        m = P if j < HT - 1 else HLAST
                        ins = mm(B[:, 0:D], big[u][0:m, 768 + j * P:768 + (j + 1) * P], w2_s[l][0:m, j, :],
                                 start=j == 0, stop=j == HT - 1)
                    ins.then_inc(*I(u, f"w2{l}"))

            walk(pe, prog, stage)

        @block.vector
        def _(dve):
            v = nc.vector
            dve.wait_ge(made2, 9)
            dve.wait_ge(padded, 3)
            dve.wait_ge(w_first, 16 * 3)
            dve.wait_ge(w_rest, 16 * 2 * 18)
            prog = Prog(dve, dve_done)
            W, WB, I = prog.wait, prog.wait_before, prog.inc

            def heads_of(t, n):
                return t.rearrange("p (h d) -> p h d", h=n)

            def settle(u):
                v.memset(carry[u][:, :], 0.0)

            def ln_stats(u, src, name):
                v.bn_stats(st6[u][:, 0, :], src).then_inc(*I(u, name + "_stats"))
                W(dve_done, u, name + "_stats")
                settle(u)
                v.bn_aggr(mv[u][:, :], st6[u][:, 0, :]).then_inc(*I(u, name + "_agg"))
                W(dve_done, u, name + "_agg")
                v.tensor_scalar(ve[u][:, :], mv[u][:, 1:2], EPS, None, ALU.add).then_inc(*I(u, name + "_eps"))

            def ln_apply(u, dst, src, name, step):
                W(dve_done, u, name + "_eps")
                W(pool_done, u, name + "_rstd")
                v.tensor_scalar(dst, src, mv[u][:, 0:1], rstd[u][:, 0:1], ALU.subtract,
                                ALU.mult).then_inc(*I(u, step))

            def masked(u, slot, half, step):
                v.tensor_tensor(big[u][:, 1024 * half:1024 * half + 1024].rearrange("p (h n) -> p h n", h=8),
                                slot[u][:, :].rearrange("p (h n) -> p h n", h=8),
                                tri[:, None, :].to_broadcast([P, 8, P]), ALU.mult).then_inc(*I(u, step))

            def grow_state(u, state, n):
                ds = slA[u][:, 512:768].rearrange("p (t n) -> p t n", t=LT)
                hm = heads[:, None, :].to_broadcast([P, LT, LPT * LD])
                tmp = scr[u][:, :].rearrange("p (t n) -> p t n", t=LT)
                v.tensor_tensor(tmp, ds, hm, ALU.mult).then_inc(*I(u, f"dS{n}"))
                W(dve_done, u, f"dS{n}")
                if prog.first:
                    v.tensor_copy(state[u][:, :, :], tmp).then_inc(*I(u, f"S{n}"))
                else:
                    v.tensor_tensor(state[u][:, :, :], state[u][:, :, :], tmp, ALU.add).then_inc(*I(u, f"S{n}"))

            def stage(s, l, u):
                A, B = slA[u], slB[u]
                if s == "ln0":
                    dve.wait_ge(x_in[u], (prog.chunk + 1) * 16)
                    WB(dve_done, u, "lnf")
                    WB(act_done, u, f"gelu{DEPTH - 1}")
                    ln_stats(u, xin[u][:, :], "ln0")
                    ln_apply(u, X[u][:, :], xin[u][:, :], "ln0", "X")
                elif s == "qT":
                    W(act_done, u, "QmT")
                    q = B[:, :].rearrange("p (t n) -> p t n", t=LT)[:, :, 0:P + 1]
                    v.scalar_tensor_tensor(QmT[u], q, -0.02 / LD ** 0.5, QmT[u], ALU.mult,
                                           ALU.max).then_inc(*I(u, "Qm"))
                elif s == "kT":
                    W(act_done, u, "K2T")
                    k2 = K2T[u]
                    v.tensor_scalar(k2, k2, 0.5, 0.5, ALU.mult, ALU.add).then_inc(*I(u, "K2T"))
                elif s == "tok":
                    W(pe_done, u, "tok")
                    k = heads_of(B[:, 0:D], LH)
                    v.tensor_copy(Ktok[u][:, :, 0:LD], k).then_inc(*I(u, "Ktok"))
                    v.tensor_tensor(heads_of(scr[u][:, :], LH), k, swb[:, None, :].to_broadcast([P, LH, LD]),
                                    ALU.mult).then_inc(*I(u, "rdot"))
                    W(dve_done, u, "rdot")
                    v.tensor_reduce(zz[u][:, LH:2 * LH], heads_of(scr[u][:, :], LH), AX.X,
                                    ALU.add).then_inc(*I(u, "rsum"))
                    W(act_done, u, "K2tok")
                    k2 = K2tok[u][:, :, 0:LD]
                    v.tensor_scalar(k2, k2, 0.5, 0.5, ALU.mult, ALU.add).then_inc(*I(u, "K2tok"))
                    W(pool_done, u, "gdot")
                    v.tensor_reduce(zz[u][:, 0:LH], heads_of(scr2[u][:, :], LH), AX.X,
                                    ALU.add).then_inc(*I(u, "gsum"))
                    W(act_done, u, "egate")
                    v.tensor_scalar(ez[u][:, :], ez[u][:, :], 1.0, None, ALU.add).then_inc(*I(u, "e1"))
                    W(dve_done, u, "e1")
                    v.reciprocal(sig[u][:, :], ez[u][:, :]).then_inc(*I(u, "sig"))
                    W(dve_done, u, "sig")
                    v.tensor_scalar(gr[u][:, 0:LH], sig[u][:, 0:LH], 1e-6, None, ALU.max).then_inc(*I(u, "G"))
                    v.tensor_tensor(gr[u][:, LH:2 * LH], zz[u][:, LH:2 * LH], sig[u][:, LH:2 * LH],
                                    ALU.mult).then_inc(*I(u, "R"))
                elif s == "cum":
                    W(pe_done, u, "cum")
                    v.tensor_scalar(lc[u][:, :], A[:, 0:LH], 30.0, None, ALU.min).then_inc(*I(u, "Lmin"))
                    W(dve_done, u, "Lmin")
                    v.tensor_scalar(lc[u][:, :], lc[u][:, :], -30.0, None, ALU.max).then_inc(*I(u, "Lclip"))
                    W(act_done, u, "eL")
                    v.tensor_scalar(gc[u][:, :], gc[u][:, :], 1e-6, None, ALU.add).then_inc(*I(u, "Gc"))
                    W(dve_done, u, "Gc")
                    v.reciprocal(rgc[u][:, :], gc[u][:, :]).then_inc(*I(u, "rGc"))
                    W(dve_done, u, "rGc")
                    v.tensor_tensor(uu[u][:, :], gr[u][:, LH:2 * LH], rgc[u][:, :], ALU.mult).then_inc(*I(u, "u"))
                elif s == "s1a":
                    W(pe_done, u, "s1a")
                    masked(u, slA, 0, "A1a")
                elif s == "s1b":
                    W(pe_done, u, "s1b")
                    masked(u, slB, 1, "A1b")
                elif s == "o1":
                    W(pe_done, u, "o1")
                    v.tensor_tensor(heads_of(O1[u][:, :], LH), heads_of(A[:, 0:D], LH),
                                    gc[u][:, :, None].to_broadcast([P, LH, LD]), ALU.mult).then_inc(*I(u, "O1"))
                    grow_state(u, S1, 1)
                elif s == "shift":
                    W(pe_done, u, "shift")
                    v.tensor_tensor(En[u][:, :], B[:, 0:D], X[u][:, :], ALU.subtract).then_inc(*I(u, "En"))
                    W(dve_done, u, "En")
                    v.tensor_scalar(En[u][:, :], En[u][:, :], row0[:, 0:1] if prog.first else ones[:, 0:1], None,
                                    ALU.mult).then_inc(*I(u, "En0"))
                elif s == "s2a":
                    W(pe_done, u, "s2a")
                    masked(u, slA, 0, "A2a")
                elif s == "s2b":
                    W(pe_done, u, "s2b")
                    masked(u, slB, 1, "A2b")
                elif s == "o2":
                    W(pe_done, u, "o2")
                    v.tensor_tensor(En[u][:, :], A[:, 0:D], O1[u][:, :], ALU.add).then_inc(*I(u, "O"))
                    grow_state(u, S2, 2)
                elif s == "cproj":
                    W(pe_done, u, "cproj")
                    ln_stats(u, A[:, 0:D], "lnc")
                    ln_apply(u, scr[u][:, :], A[:, 0:D], "lnc", "lnc")
                    W(dve_done, u, "lnc")
                    v.tensor_tensor(x1[u][:, :], scr[u][:, :], xin[u][:, :], ALU.add).then_inc(*I(u, "mid_x"))
                    W(dve_done, u, "mid_x")
                    ln_stats(u, x1[u][:, :], "lnz")
                    ln_apply(u, X[u][:, :], x1[u][:, :], "lnz", "z")
                elif s == "rot":
                    W(act_done, u, f"sq{l}")
                    v.tensor_reduce(ssq[u][:, :], heads_of(big[u][:, 0:1024], 2 * AH), AX.X,
                                    ALU.add).then_inc(*I(u, f"ss{l}"))
                    W(dve_done, u, f"ss{l}")
                    v.tensor_scalar(ssq[u][:, :], ssq[u][:, :], 1e-24, None, ALU.max).then_inc(*I(u, f"ss_clip{l}"))
                    W(pool_done, u, f"tab{l}")
                    raw = qkraw[u].rearrange("p (s h a d) -> p s h a d", s=2, h=AH, a=2)
                    t2 = big[u][:, 1024:2048].rearrange("p (s h a d) -> p s h a d", s=2, h=AH, a=2)
                    half = AD // 2
                    for a in range(2):
                        ins = v.tensor_tensor(t2[:, :, :, a, :], raw[:, :, :, 1 - a, :],
                                              tabl[u][:, 1:4:2, None, a * half:(a + 1) * half].to_broadcast(
                                                  [P, 2, AH, half]), ALU.mult)
                    ins.then_inc(*I(u, f"t2{l}"))
                    W(dve_done, u, f"t2{l}")
                    W(pool_done, u, f"t1{l}")
                    v.tensor_tensor(qkrot[u], qkrot[u], big[u][:, 1024:2048], ALU.add).then_inc(*I(u, f"rot{l}"))
                    W(pool_done, u, f"rnorm{l}")
                    v.tensor_scalar(sc8[u][:, :], rnorm[u][:, 0:AH], QK_SCALE, None,
                                    ALU.mult).then_inc(*I(u, f"sc8{l}"))
                elif s in ("sa", "sb"):
                    W(pe_done, u, f"{s}{l}")
                    W(dve_done, u, f"sc8{l}")
                    settle(u)
                    slot, h0 = (A, 0) if s == "sa" else (B, 4)
                    lo = P if prog.first else 0
                    for i in range(4):
                        h = h0 + i
                        ins = v.tensor_tensor_reduce(big[u][:, 256 * h + lo:256 * h + 256],
                                                     slot[:, 256 * SLOT_OF[i] + lo:256 * SLOT_OF[i] + 256], band[:, lo:2 * P],
                                                     1.0, MASKED, ALU.add, ALU.max, mx[u][:, h:h + 1])
                    ins.then_inc(*I(u, f"m{s[1]}{l}"))
                    W(dve_done, u, f"m{s[1]}{l}")
                    v.scalar_tensor_tensor(nb[u][:, h0:h0 + 4], mx[u][:, h0:h0 + 4], -1.0, sc8[u][:, h0:h0 + 4],
                                           ALU.mult, ALU.mult).then_inc(*I(u, f"nb{s[1]}{l}"))
                elif s == "pb":
                    W(pe_done, u, f"pb{l}")
                    lo = P if prog.first else 0
                    v.tensor_copy(big[u][:, 1024:2048].rearrange("p (h n) -> p h n", h=4)[:, :, lo:256],
                                  B[:, :].rearrange("p (h n) -> p h n", h=4)[:, :, lo:256]).then_inc(*I(u, f"pb{l}"))
                elif s == "av":
                    v.reciprocal(rden[u][:, :], den[u][:, :]).then_inc(*I(u, f"rden{l}"))
                    W(dve_done, u, f"rden{l}")
                    W(pe_done, u, f"av{l}")
                    v.tensor_tensor(heads_of(on[u], AH), heads_of(A[:, 0:INNER], AH),
                                    rden[u][:, :, None].to_broadcast([P, AH, AD]), ALU.mult).then_inc(*I(u, f"on{l}"))
                elif s == "wo":
                    W(pe_done, u, f"wo{l}")
                    W(act_done, u, f"xph{l}")
                    v.tensor_tensor(X[u][:, :], X[u][:, :], A[:, 0:D], ALU.add).then_inc(*I(u, f"x{l}"))
                elif s == "xs":
                    W(pe_done, u, f"xs{l}")
                    W(dve_done, u, f"x{l}")
                    v.bn_stats(st6[u][:, 0, :], X[u][:, 0:P]).then_inc(*I(u, f"st_a{l}"))
                    v.bn_stats(st6[u][:, 1, :], B[:, 0:P]).then_inc(*I(u, f"st_b{l}"))
                    W(dve_done, u, f"st_b{l}")
                    settle(u)
                    v.bn_aggr(mv[u][:, :], st6[u][:, :, :].rearrange("p a b -> p (a b)")).then_inc(*I(u, f"ln_agg{l}"))
                    W(dve_done, u, f"ln_agg{l}")
                    v.tensor_scalar(ve[u][:, :], mv[u][:, 1:2], EPS, None, ALU.add).then_inc(*I(u, f"ln_eps{l}"))
                    W(pool_done, u, f"ln_rstd{l}")
                    v.tensor_scalar(hn[u][:, 0:P], X[u][:, 0:P], mv[u][:, 0:1], rstd[u][:, 0:1],
                                    ALU.subtract, ALU.mult)
                    v.tensor_scalar(hn[u][:, P:D], B[:, 0:P], mv[u][:, 0:1], rstd[u][:, 0:1],
                                    ALU.subtract, ALU.mult).then_inc(*I(u, f"hn{l}"))
                elif s == "w1a":
                    W(pe_done, u, f"w1a{l}")
                    W(act_done, u, f"gelu{l}")
                    for j in range(HT):
                        m = P if j < HT - 1 else HLAST
                        ins = v.scalar_tensor_tensor(big[u][0:m, 768 + j * P:768 + (j + 1) * P],
                                                     A[0:m, j * P:(j + 1) * P], b1a[l][0:m, j:j + 1],
                                                     big[u][0:m, j * P:(j + 1) * P], ALU.add, ALU.mult)
                    ins.then_inc(*I(u, f"hid{l}"))
                elif s == "w2":
                    W(pe_done, u, f"w2{l}")
                    W(pool_done, u, f"xb2{l}")
                    v.tensor_tensor(X[u][:, :], X[u][:, :], B[:, 0:D], ALU.add).then_inc(*I(u, f"x2{l}"))
                elif s == "out":
                    W(dve_done, u, f"x2{DEPTH - 1}")
                    ln_stats(u, X[u][:, :], "lnf")
                    ln_apply(u, scr[u][:, :], X[u][:, :], "lnf", "lnf")
                    W(dve_done, u, "lnf")
                    if not prog.first:
                        dve.wait_ge(stored[u], prog.chunk * 16)
                    v.tensor_tensor(xo[u][:, :], scr[u][:, :], x1[u][:, :], ALU.add).then_inc(*I(u, "out"))

            walk(dve, prog, stage)


def kernel(**inputs):
    import numpy as _np
    import concourse.bacc as _bacc
    from concourse import mybir as _mybir
    from concourse.bass_utils import run_bass_kernel_spmd as _run

    nc = _bacc.Bacc("TRN2", target_bir_lowering=False, num_devices=1)
    half_idx = _np.arange(0, AD, 2, dtype=_np.float64)
    t = _np.arange(SEQ, dtype=_np.float64)
    inv_freq = (1.0 / 10000.0 ** (half_idx / AD)).astype(_np.float32).astype(_np.float64)
    freqs = (t[:, None] * inv_freq[None, :]).astype(_np.float32).astype(_np.float64)
    freqs = _np.concatenate([freqs, freqs], axis=-1)
    base = (half_idx + 0.4 * AD) / (1.4 * AD)
    scale = base[None, :] ** ((t - SEQ // 2) / 64.0)[:, None]
    scale = _np.concatenate([scale, scale], axis=-1)
    sign = _np.concatenate([-_np.ones(AD // 2), _np.ones(AD // 2)])
    cos, sin = _np.cos(freqs), _np.sin(freqs) * sign
    xpos = _np.concatenate([cos * scale, sin * scale, cos / scale, sin / scale], axis=-1).astype(_np.float32)

    def arr(name):
        return _np.ascontiguousarray(inputs[name])

    data = {
        "x": arr("L0_attn_X").reshape(BATCH * SEQ, D), "xpos": xpos,
        "q1T": _np.ascontiguousarray(arr("L0_attn_q1_w").T), "k1T": _np.ascontiguousarray(arr("L0_attn_k1_w").T),
        "k2T": _np.ascontiguousarray(arr("L0_attn_k2_w").T),
        "gw": arr("L0_attn_gw_w"), "sw": arr("L0_attn_sw_w"),
        "cT": _np.ascontiguousarray(arr("L0_attn_c_proj_w").T),
        "wqkv": arr("L0_ffn_wqkv"), "qs": arr("L0_ffn_q_scale"), "ks": arr("L0_ffn_k_scale"),
        "wo": arr("L0_ffn_wo"), "lg": arr("L0_ffn_ln_g"), "lb": arr("L0_ffn_ln_b"),
        "w1": arr("L0_ffn_w1"), "b1": arr("L0_ffn_b1"), "w2": arr("L0_ffn_w2"), "b2": arr("L0_ffn_b2"),
    }
    args = [nc.dram_tensor(n, a.shape, _mybir.dt.from_np(a.dtype), kind="ExternalInput").ap()
            for n, a in data.items()]
    args.append(nc.dram_tensor("out", (BATCH * SEQ, D), F32, kind="ExternalOutput").ap())
    build(nc, *args)
    r = _run(nc, [data], core_ids=[0])
    return r.results[0]["out"].reshape(BATCH, SEQ, D)
```

```python
from contextlib import ExitStack

import concourse.bass as bass
from concourse import mybir

F32 = mybir.dt.float32
ALU = mybir.AluOpType
ACT = mybir.ActivationFunctionType
AX = mybir.AxisListType

P = 128
D = 256
KD = D // P
BATCH, SEQ = 4, 1024
CHUNKS = SEQ // P
UNITS = 2
STEPS = BATCH // UNITS * CHUNKS
LH, LD = 16, 16
LT = LH * LD // P
LPT = LH // LT
DEPTH = 2
AH, AD = 8, 64
INNER = AH * AD
AT = INNER // P
HID = 682
HT = (HID + P - 1) // P
HLAST = HID - (HT - 1) * P
QK_SCALE = 8.0
MASKED = -1e30
EPS = 1e-5
KEEP, KEEP_NEXT, ROW, PREV = range(4 * AD, 4 * AD + 4)
TABW = 4 * AD + 4

LAYER_PE = ["hT", "qk", "v", "qkT", "sa", "sb", "pa", "pb", "av", "oT", "wo", "xs", "h2T", "w1g", "w1a", "w2"]
LAYER_ACT = ["hT", "xph", "sq", "v", "qT", "kT", "ea", "eb", "pa", "oT", "xph2", "h2T", "gelu"]
LAYER_DVE = ["ss", "ss_clip", "t1", "t2", "rot", "kn", "sc8", "ma", "nba", "mb", "nbb", "pb", "rden", "on", "x",
             "st_a", "st_b", "ln_agg", "ln_eps", "hn", "hid", "x2"]
LAYER_POOL = ["tab", "rnorm", "ln_rstd", "xb2"]


def layered(names):
    return [f"{n}_{l}" for l in range(DEPTH) for n in names]


PE_STEPS = ["xT", "qT", "kT", "tok", "s1a", "s1b", "cum", "o1", "shift", "s2a", "s2b", "o2", "OT", "cproj"] \
    + layered(LAYER_PE)
ACT_STEPS = ["flags", "XT_halo", "XT", "QT", "QmT", "KT", "K2T", "K2tok", "egate", "lnG", "eL", "O1p", "OT"] \
    + layered(LAYER_ACT)
DVE_STEPS = ["ln0_stats", "ln0_agg", "ln0_eps", "X", "Qm", "bd1a", "bd1b", "K2T_1", "K2T",
             "Ktok", "rdot", "rsum", "gsum", "e1", "sig", "G", "R", "K2tok_1", "K2tok", "A1a", "A1b",
             "Lmin", "Lclip", "Gc", "rGc", "u", "O1", "dS1", "S1", "bd2b", "En", "En0",
             "A2a", "A2b", "O", "dS2", "S2", "lnc_stats", "lnc_agg", "lnc_eps", "lnc", "mid_x",
             "lnz_stats", "lnz_agg", "lnz_eps", "z"] + layered(LAYER_DVE) \
    + ["lnf_stats", "lnf_agg", "lnf_eps", "lnf", "out"]
POOL_STEPS = ["ln0_rstd", "band", "hmk", "gdot", "bd2a", "Vu", "acc", "acc_keep", "lnc_rstd", "lnz_rstd"] \
    + layered(LAYER_POOL) + ["lnf_rstd"]

LAYER_STAGES = ["h", "qk", "v", "rot", "qkT", "sa", "sb", "pa", "pb", "av", "oT", "wo", "xs", "h2T",
                "w1g", "w1a", "w2"]
STAGES = [(s, None) for s in ("ln0", "xT", "qT", "kT", "tok", "s1a", "s1b", "cum", "o1", "shift",
                              "s2a", "s2b", "o2", "OT", "cproj")] \
    + [(s, l) for l in range(DEPTH) for s in LAYER_STAGES] + [("out", None)]
LAG = 11


class Done:

    def __init__(self, sems, steps):
        assert len(set(steps)) == len(steps)
        self.sems, self.steps, self.at = sems, steps, {n: i + 1 for i, n in enumerate(steps)}

    def value(self, step, chunk):
        return chunk * len(self.steps) + self.at[step]


def build(nc, x, table, q1T, k1T, k2T, gw, sw, cT, wqkv, qs, ks, wo, lg, lb, w1, b1, w2, b2, out):
    with ExitStack() as ctx:
        def sb(name, *shape):
            return ctx.enter_context(nc.sbuf_tensor(name, [P, *shape], F32))

        def sem(name):
            return ctx.enter_context(nc.semaphore(name))

        ident, shift, last, tri, ones = (sb(n, P) for n in ("ident", "shift", "last", "tri", "ones"))
        band = sb("band", P)
        head1 = sb("head1", LPT)
        mhalf = sb("mhalf", LH)
        gwb, swb = sb("gwb", LD), sb("swb", LD)
        q1w, k1w, k2w = (sb(n, KD, D) for n in ("q1w", "k1w", "k2w"))
        cw = sb("cw", KD, D)
        wqkv_s = [sb(f"wqkv_{l}", KD, 3 * INNER) for l in range(DEPTH)]
        wo_s = [sb(f"wo_{l}", AT, D) for l in range(DEPTH)]
        w1_s = [sb(f"w1_{l}", KD, 2 * HID) for l in range(DEPTH)]
        w2_s = [sb(f"w2_{l}", HT, D) for l in range(DEPTH)]
        scales = [sb(f"scales_{l}", 4, AD) for l in range(DEPTH)]
        lgc, lbc = ([sb(f"{n}_{l}", KD) for l in range(DEPTH)] for n in ("lgc", "lbc"))
        b1a, b1g = ([sb(f"{n}_{l}", HT) for l in range(DEPTH)] for n in ("b1a", "b1g"))
        b2b = [sb(f"b2b_{l}", D) for l in range(DEPTH)]

        def per_unit(name, *shape):
            return [sb(f"{name}{u}", *shape) for u in range(UNITS)]

        xin, x1, X = per_unit("xin", D), per_unit("x1", D), per_unit("X", D)
        tab, tabl, fl = per_unit("tab", TABW), per_unit("tabl", 4, AD), per_unit("fl", 4)
        XT = per_unit("XT", KD, P + 1)
        big, mid = per_unit("big", 2048), per_unit("mid", 2 * LT * (2 * P + 1) + 1024)
        bandu = per_unit("bandu", 2 * P)
        hmk = per_unit("hmk", LPT)
        Ktok, K2tok = per_unit("Ktok", D), per_unit("K2tok", D)
        Vu, O1, O1p, En = (per_unit(n, D) for n in ("Vu", "O1", "O1p", "En"))
        S1, S2 = per_unit("S1", LT, P), per_unit("S2", LT, P)
        acc = per_unit("acc", LH)
        vcur, hT, hn, scr, scr2, xo = (per_unit(n, w) for n, w in (
            ("vcur", INNER), ("hT", D), ("hn", D), ("scr", D), ("scr2", D), ("xo", D)))
        kTd = [[sb(f"kTd{l}_{u}", AT, 2, 2 * P) for u in range(UNITS)] for l in range(DEPTH)]
        prevV = [[sb(f"prevV{l}_{u}", INNER) for u in range(UNITS)] for l in range(DEPTH)]
        xph = [[sb(f"xph{l}_{u}", P) for u in range(UNITS)] for l in range(DEPTH)]
        xph2 = [[sb(f"xph2{l}_{u}", P) for u in range(UNITS)] for l in range(DEPTH)]
        st6 = per_unit("st6", 2, 6)
        mv = per_unit("mv", 2)
        carry = per_unit("carry", 1)
        ve, rstd = per_unit("ve", 1), per_unit("rstd", 1)
        zz = per_unit("zz", 2 * LH)
        ez, sig = per_unit("ez", 2 * LH), per_unit("sig", 2 * LH)
        gr = per_unit("gr", 2 * LH)
        logG, lc, gc, rgc, uu = (per_unit(n, LH) for n in ("logG", "lc", "gc", "rgc", "uu"))
        ssq, rnorm = per_unit("ssq", 2 * AH), per_unit("rnorm", 2 * AH)
        sc8, mx, nb, den, rden = (per_unit(n, AH) for n in ("sc8", "mx", "nb", "den", "rden"))

        QT = [m[:, 0:258].rearrange("p (t n) -> p t n", t=LT) for m in mid]
        QmT = [m[:, 258:516].rearrange("p (t n) -> p t n", t=LT) for m in mid]
        KT = [m[:, 516:772].rearrange("p (t n) -> p t n", t=LT) for m in mid]
        K2T = [m[:, 772:1028].rearrange("p (t n) -> p t n", t=LT) for m in mid]
        bd2a = [m[:, 1028:2052] for m in mid]
        qT = [m[:, 0:512].rearrange("p (t n) -> p t n", t=AT) for m in mid]
        on = [m[:, 512:1024] for m in mid]
        qkrot = [m[:, 1024:2048] for m in mid]
        oT = [m[:, 1024:1536].rearrange("p (t n) -> p t n", t=AT) for m in mid]

        slA = [ctx.enter_context(nc.psum_tensor(f"slA{u}", [P, 1024], F32)) for u in range(UNITS)]
        slB = [ctx.enter_context(nc.psum_tensor(f"slB{u}", [P, 1024], F32)) for u in range(UNITS)]

        pe_done = Done([sem(f"pe_done{u}") for u in range(UNITS)], PE_STEPS)
        act_done = Done([sem(f"act_done{u}") for u in range(UNITS)], ACT_STEPS)
        dve_done = Done([sem(f"dve_done{u}") for u in range(UNITS)], DVE_STEPS)
        pool_done = Done([sem(f"pool_done{u}") for u in range(UNITS)], POOL_STEPS)
        x_in, tab_in = ([sem(f"{n}{u}") for u in range(UNITS)] for n in ("x_in", "tab_in"))
        kv_kept = [[sem(f"kv_kept{l}_{u}") for u in range(UNITS)] for l in range(DEPTH)]
        stored = [sem(f"stored{u}") for u in range(UNITS)]
        w_first, w_rest, made, made2 = (sem(n) for n in ("w_first", "w_rest", "made", "made2"))
        KV_DMAS = 3 * 16

        class Prog:

            def __init__(self, eng, done):
                self.eng, self.done = eng, done
                self.n, self.chunk, self.first, self.last = ([0] * UNITS for _ in range(4))

            def wait(self, done, u, step):
                self.eng.wait_ge(done.sems[u], done.value(step, self.chunk[u]))

            def wait_before(self, done, u, step):
                if not self.first[u]:
                    self.eng.wait_ge(done.sems[u], done.value(step, self.chunk[u]) - len(done.steps))

            def wait_dma_before(self, s, u, per_chunk):
                if not self.first[u]:
                    self.eng.wait_ge(s, self.chunk[u] * per_chunk)

            def inc(self, u, step):
                assert self.done.steps[self.n[u]] == step, (self.done.steps[self.n[u]], step)
                self.n[u] += 1
                return self.done.sems[u], 1

        def walk(eng, prog, stage):
            def do(i, u, chunk, first, last):
                if i == 0:
                    prog.n[u] = 0
                prog.chunk[u], prog.first[u], prog.last[u] = chunk, first, last
                stage(*STAGES[i], u)

            def body(c, first=False, last=False):
                n = len(STAGES)
                for j in range(n):
                    i0 = j + LAG
                    if i0 < n:
                        do(i0, 0, c, first, last)
                    elif not last:
                        do(i0 - n, 0, c + 1, False, False)
                    do(j, 1, c, first, last)

            for i in range(LAG):
                do(i, 0, 0, True, False)
            body(0, first=True)
            with eng.Fori(1, STEPS - 1) as c:
                body(c)
            body(STEPS - 1, last=True)

        block = ctx.enter_context(nc.Block())

        @block.sync
        def _(sp):
            def load(dst, src, s):
                sp.dma_start(dst, src).then_inc(s, 16)

            for dst, w in ((q1w, q1T), (k1w, k1T), (k2w, k2T), (cw, cT)):
                load(dst[:, :, :], w.rearrange("(k p) n -> p k n", p=P), w_first)
            load(gwb[:, :], gw.partition_broadcast(P), w_first)
            load(swb[:, :], sw.partition_broadcast(P), w_first)
            for l in range(DEPTH):
                load(wqkv_s[l][:, :, :], wqkv[l].rearrange("(k p) n -> p k n", p=P), w_rest)
                load(wo_s[l][:, :, :], wo[l].rearrange("(k p) n -> p k n", p=P), w_rest)
                load(w1_s[l][:, :, :], w1[l].rearrange("(k p) n -> p k n", p=P), w_rest)
                load(w2_s[l][:, 0:HT - 1, :], w2[l, 0:(HT - 1) * P].rearrange("(k p) n -> p k n", p=P), w_rest)
                load(w2_s[l][0:HLAST, HT - 1, :], w2[l, (HT - 1) * P:HID], w_rest)
                for i, s in ((0, qs), (2, ks)):
                    row = s[l].rearrange("(a n) -> a n", a=1)
                    half = AD // 2
                    load(scales[l][:, i, :], row.partition_broadcast(P), w_rest)
                    load(scales[l][:, i + 1, 0:half], row[:, half:AD].partition_broadcast(P), w_rest)
                    load(scales[l][:, i + 1, half:AD], row[:, 0:half].partition_broadcast(P), w_rest)
                load(b2b[l][:, :], b2[l].rearrange("(a n) -> a n", a=1).partition_broadcast(P), w_rest)
                with nc.allow_non_contiguous_dma("bias columns, once"):
                    load(lgc[l][:, :], lg[l].rearrange("(k p) -> p k", p=P), w_rest)
                    load(lbc[l][:, :], lb[l].rearrange("(k p) -> p k", p=P), w_rest)
                    for dst, o in ((b1a, 0), (b1g, HID)):
                        load(dst[l][:, 0:HT - 1], b1[l, o:o + (HT - 1) * P].rearrange("(k p) -> p k", p=P), w_rest)
                        load(dst[l][0:HLAST, HT - 1:HT],
                             b1[l, o + (HT - 1) * P:o + HID].rearrange("(p k) -> p k", k=1), w_rest)

            prog = Prog(sp, None)

            def load_next(u, c):
                sp.dma_start(xin[u][:, :], x[bass.ds(u * (STEPS * P) + c * P, P), :]).then_inc(x_in[u], 16)
                sp.dma_start(tab[u][:, :], table[bass.ds(c * P, P), :]).then_inc(tab_in[u], 16)

            def stage(s, l, u):
                if s == "oT":
                    prog.wait(pe_done, u, f"av_{l}")
                    for r in range(2):
                        half = slice(r * AD, (r + 1) * AD)
                        sp.dma_start(kTd[l][u][half, :, r, 0:P], kTd[l][u][half, :, r, P:2 * P]).then_inc(
                            kv_kept[l][u], 16)
                    sp.dma_start(prevV[l][u][:, :], vcur[u][:, :]).then_inc(kv_kept[l][u], 16)
                if s == "qkT" and l == DEPTH - 1 and not prog.last[u]:
                    prog.wait(dve_done, u, "mid_x")
                    prog.wait(act_done, u, "flags")
                    prog.wait(pool_done, u, f"tab_{l}")
                    load_next(u, prog.chunk[u] + 1)

            for u in range(UNITS):
                load_next(u, 0)
            walk(sp, prog, stage)
            for u in range(UNITS):
                sp.wait_ge(stored[u], STEPS * 16)
                for l in range(DEPTH):
                    sp.wait_ge(kv_kept[l][u], STEPS * KV_DMAS)

        @block.gpsimd
        def _(pool):
            g = nc.gpsimd
            fills = [(ident, 0.0), (shift, 0.0), (last, 0.0), (tri, 1.0), (ones, 1.0), (mhalf, -0.5), (head1, 1.0),
                     *((b, 0.0) for b in bandu)]
            fills += [(t, 0.0) for t in (*XT, *acc, *O1p, *S1, *S2, *kTd[0], *kTd[1], *prevV[0], *prevV[1],
                                         *xph[0], *xph[1], *xph2[0], *xph2[1])]
            for t, v in fills:
                g.memset(t[:], v).then_inc(made, 1)
            g.memset(band[:, :], 0.0).then_inc(made, 1)
            pool.wait_ge(made, len(fills) + 1)

            def sel(t, pattern, base, mult, op, fill):
                g.affine_select(out=t, in_=t, pattern=pattern, base=base, channel_multiplier=mult,
                                compare_op=op, fill=fill).then_inc(made2, 1)
            sel(ident[:, :], [[-1, P]], 0, 1, ALU.not_equal, 1.0)
            sel(shift[:, :], [[-1, P]], 1, 1, ALU.not_equal, 1.0)
            sel(last[:, :], [[-1, P]], -(P - 1), 1, ALU.not_equal, 1.0)
            sel(tri[:, :], [[1, P]], 0, -1, ALU.is_ge, 0.0)
            sel(band[:, :], [[1, P]], 0, -1, ALU.is_ge, MASKED)
            for u in range(UNITS):
                sel(bandu[u][:, P:2 * P], [[-1, P]], 0, 1, ALU.is_ge, MASKED)
            sel(head1[:, :], [[-LD, LPT]], 0, 1, ALU.is_ge, 0.0)
            pool.wait_ge(made2, 8)
            sel(head1[:, :], [[LD, LPT]], LD - 1, -1, ALU.is_ge, 0.0)
            pool.wait_ge(made2, 9)
            pool.wait_ge(w_first, 16 * 6)
            pool.wait_ge(w_rest, 16 * DEPTH * 18)
            prog = Prog(pool, pool_done)
            W, WB, I = prog.wait, prog.wait_before, prog.inc

            def rstd_of(u, name):
                W(dve_done, u, name + "_eps")
                g.tensor_tensor(rstd[u][:, :], ve[u][:, :], mhalf[:, 0:1], ALU.pow).then_inc(*I(u, name + "_rstd"))

            def stage(s, l, u):
                if s == "ln0":
                    rstd_of(u, "ln0")
                    W(act_done, u, "flags")
                    WB(dve_done, u, f"mb_{DEPTH - 1}")
                    g.tensor_tensor(bandu[u][:, 0:P], band[:, :], fl[u][:, 3:4].to_broadcast([P, P]),
                                    ALU.add).then_inc(*I(u, "band"))
                    g.tensor_tensor(hmk[u][:, :], head1[:, :], fl[u][:, 1:2].to_broadcast([P, LPT]),
                                    ALU.mult).then_inc(*I(u, "hmk"))
                elif s == "xT":
                    W(dve_done, u, "X")
                    g.tensor_tensor(scr2[u][:, :].rearrange("p (h d) -> p h d", h=LH),
                                    X[u][:, :].rearrange("p (h d) -> p h d", h=LH),
                                    gwb[:, None, :].to_broadcast([P, LH, LD]), ALU.mult).then_inc(*I(u, "gdot"))
                elif s == "qT":
                    W(dve_done, u, "Qm")
                    g.tensor_tensor(bd2a[u].rearrange("p (h n) -> p h n", h=LPT),
                                    QmT[u][:, 0:1, 0:P].to_broadcast([P, LPT, P]),
                                    head1[:, :, None].to_broadcast([P, LPT, P]), ALU.mult).then_inc(*I(u, "bd2a"))
                elif s == "cum":
                    W(dve_done, u, "u")
                    g.tensor_tensor(Vu[u][:, :].rearrange("p (h d) -> p h d", h=LH),
                                    X[u][:, :].rearrange("p (h d) -> p h d", h=LH),
                                    uu[u][:, :, None].to_broadcast([P, LH, LD]), ALU.mult).then_inc(*I(u, "Vu"))
                    g.tensor_tensor(acc[u][:, :], acc[u][:, :], logG[u][:, :], ALU.add).then_inc(*I(u, "acc"))
                    W(pool_done, u, "acc")
                    g.tensor_tensor(acc[u][:, :], acc[u][:, :], fl[u][:, 1:2].to_broadcast([P, LH]),
                                    ALU.mult).then_inc(*I(u, "acc_keep"))
                elif s == "cproj":
                    rstd_of(u, "lnc")
                    rstd_of(u, "lnz")
                elif s == "h":
                    W(act_done, u, "flags")
                    g.tensor_tensor(tabl[u][:, :, :], tab[u][:, 0:4 * AD].rearrange("p (a n) -> p a n", a=4), scales[l][:, :, :],
                                    ALU.mult).then_inc(*I(u, f"tab_{l}"))
                elif s == "rot":
                    W(dve_done, u, f"ss_clip_{l}")
                    g.tensor_tensor(rnorm[u][:, :], ssq[u][:, :], mhalf[:, :], ALU.pow).then_inc(*I(u, f"rnorm_{l}"))
                elif s == "xs":
                    W(dve_done, u, f"ln_eps_{l}")
                    g.tensor_tensor(rstd[u][:, :], ve[u][:, :], mhalf[:, 0:1], ALU.pow).then_inc(*I(u, f"ln_rstd_{l}"))
                elif s == "w1g":
                    W(act_done, u, f"xph2_{l}")
                    W(dve_done, u, f"hn_{l}")
                    g.tensor_tensor(X[u][:, :], X[u][:, :], b2b[l][:, :], ALU.add).then_inc(*I(u, f"xb2_{l}"))
                elif s == "out":
                    rstd_of(u, "lnf")

            walk(pool, prog, stage)

        @block.scalar
        def _(act):
            def A(out_, in_, func, **kw):
                return nc.scalar.activation(out_, in_, func, **kw)

            act.wait_ge(made2, 9)
            act.wait_ge(w_rest, 16 * DEPTH * 18)
            prog = Prog(act, act_done)
            W, WB, I = prog.wait, prog.wait_before, prog.inc

            def stage(s, l, u):
                if s == "ln0":
                    act.wait_ge(tab_in[u], prog.chunk[u] * 16 + 16)
                    A(fl[u][:, :], tab[u][:, 4 * AD:TABW], ACT.Copy).then_inc(*I(u, "flags"))
                    WB(pe_done, u, "tok")
                    W(act_done, u, "flags")
                    A(XT[u][:, :, 0:1], XT[u][:, :, P:P + 1], ACT.Copy,
                      scale=fl[u][:, 0:1]).then_inc(*I(u, "XT_halo"))
                elif s == "xT":
                    W(pe_done, u, "xT")
                    W(act_done, u, "XT_halo")
                    A(XT[u][:, :, 1:P + 1], slA[u][:, 0:D].rearrange("p (k n) -> p k n", k=KD),
                      ACT.Copy).then_inc(*I(u, "XT"))
                elif s == "qT":
                    W(pe_done, u, "qT")
                    A(QT[u], slB[u][:, 0:512].rearrange("p (t n) -> p t n", t=LT)[:, :, 0:P + 1],
                      ACT.Copy).then_inc(*I(u, "QT"))
                    W(act_done, u, "QT")
                    A(QmT[u], QT[u], ACT.Copy, scale=-1.0 / LD ** 0.5).then_inc(*I(u, "QmT"))
                elif s == "kT":
                    W(pe_done, u, "kT")
                    A(KT[u], slA[u][:, 0:D].rearrange("p (t n) -> p t n", t=LT), ACT.Copy).then_inc(*I(u, "KT"))
                    A(K2T[u], slA[u][:, D:2 * D].rearrange("p (t n) -> p t n", t=LT), ACT.Exp,
                      scale=-0.02 / D ** 0.5).then_inc(*I(u, "K2T"))
                elif s == "tok":
                    W(pe_done, u, "tok")
                    A(K2tok[u][:, :], slA[u][:, 512:512 + D], ACT.Exp,
                      scale=-0.02 / D ** 0.5).then_inc(*I(u, "K2tok"))
                    W(dve_done, u, "gsum")
                    A(ez[u][:, :], zz[u][:, :], ACT.Exp, scale=-1.0).then_inc(*I(u, "egate"))
                    W(dve_done, u, "G")
                    A(logG[u][:, :], gr[u][:, 0:LH], ACT.Ln).then_inc(*I(u, "lnG"))
                elif s == "cum":
                    W(dve_done, u, "Lclip")
                    A(gc[u][:, :], lc[u][:, :], ACT.Exp).then_inc(*I(u, "eL"))
                elif s == "shift":
                    W(pe_done, u, "shift")
                    A(O1p[u][:, :], O1[u][:, :], ACT.Copy, scale=fl[u][:, 1:2]).then_inc(*I(u, "O1p"))
                elif s == "OT":
                    W(pe_done, u, "OT")
                    A(hT[u][:, :], slB[u][:, 0:D], ACT.Copy).then_inc(*I(u, "OT"))
                elif s == "h":
                    W(pe_done, u, f"hT_{l}")
                    A(hT[u][:, :], slB[u][:, 0:D], ACT.Copy).then_inc(*I(u, f"hT_{l}"))
                    A(xph[l][u][:, :], X[u][:, P:D], ACT.Copy, scale=fl[u][:, 1:2]).then_inc(*I(u, f"xph_{l}"))
                elif s == "qk":
                    W(pe_done, u, f"qk_{l}")
                    A(big[u][:, 0:1024], slA[u][:, :], ACT.Square).then_inc(*I(u, f"sq_{l}"))
                elif s == "v":
                    W(pe_done, u, f"v_{l}")
                    if l:
                        act.wait_ge(kv_kept[l - 1][u], prog.chunk[u] * KV_DMAS + KV_DMAS)
                    else:
                        prog.wait_dma_before(kv_kept[DEPTH - 1][u], u, KV_DMAS)
                    A(vcur[u][:, :], slB[u][:, 0:INNER], ACT.Copy).then_inc(*I(u, f"v_{l}"))
                elif s == "qkT":
                    W(pe_done, u, f"qkT_{l}")
                    A(qT[u].rearrange("p t n -> p (t n)"), slA[u][:, 0:512], ACT.Copy).then_inc(*I(u, f"qT_{l}"))
                    prog.wait_dma_before(kv_kept[l][u], u, KV_DMAS)
                    for r in range(2):
                        half = slice(r * AD, (r + 1) * AD)
                        ins = A(kTd[l][u][half, :, r, P:2 * P],
                                slA[u][half, 512:1024].rearrange("p (t n) -> p t n", t=AT), ACT.Copy)
                    ins.then_inc(*I(u, f"kT_{l}"))
                elif s in ("pa", "pb") or s in ("sa", "sb"):
                    if s in ("sa", "sb"):
                        W(dve_done, u, f"nb{s[1]}_{l}")
                        for h in range(4 * (s == "sb"), 4 * (s == "sb") + 4):
                            p = big[u][:, 256 * h:256 * h + 256]
                            ins = A(p, p, ACT.Exp, bias=nb[u][:, h:h + 1], scale=sc8[u][:, h:h + 1],
                                    accum_out=den[u][:, h:h + 1])
                        ins.then_inc(*I(u, f"e{s[1]}_{l}"))
                    if s == "pa":
                        W(pe_done, u, f"pa_{l}")
                        A(big[u][:, 0:1024], slA[u][:, :], ACT.Copy).then_inc(*I(u, f"pa_{l}"))
                elif s == "oT":
                    W(pe_done, u, f"oT_{l}")
                    A(oT[u].rearrange("p t n -> p (t n)"), slB[u][:, 0:INNER], ACT.Copy).then_inc(*I(u, f"oT_{l}"))
                elif s == "xs":
                    W(pe_done, u, f"xs_{l}")
                    A(xph2[l][u][:, :], X[u][:, P:D], ACT.Copy, scale=fl[u][:, 1:2]).then_inc(*I(u, f"xph2_{l}"))
                elif s == "h2T":
                    W(pe_done, u, f"h2T_{l}")
                    for k in range(KD):
                        ins = A(hT[u][:, k * P:(k + 1) * P], slA[u][:, k * P:(k + 1) * P], ACT.Identity,
                                scale=lgc[l][:, k:k + 1], bias=lbc[l][:, k:k + 1])
                    ins.then_inc(*I(u, f"h2T_{l}"))
                elif s == "w1g":
                    W(pe_done, u, f"w1g_{l}")
                    for j in range(HT):
                        m = P if j < HT - 1 else HLAST
                        ins = A(big[u][0:m, j * P:(j + 1) * P], slB[u][0:m, j * P:(j + 1) * P], ACT.Gelu,
                                bias=b1g[l][0:m, j:j + 1])
                    ins.then_inc(*I(u, f"gelu_{l}"))
                elif s == "out":
                    W(dve_done, u, "out")
                    act.dma_start(out[bass.ds(u * (STEPS * P) + prog.chunk[u] * P, P), :],
                                  xo[u][:, :]).then_inc(stored[u], 16)

            walk(act, prog, stage)

        @block.tensor
        def _(pe):
            mm, tr = nc.tensor.matmul, nc.tensor.transpose
            pe.wait_ge(made2, 9)
            pe.wait_ge(w_first, 16 * 6)
            pe.wait_ge(w_rest, 16 * DEPTH * 18)
            prog = Prog(pe, pe_done)
            W, WB, I = prog.wait, prog.wait_before, prog.inc

            def scores(u, slot, k_rows, blocks, t):
                for n in range(2):
                    ins = mm(slot[u][:, n * 512:(n + 1) * 512], k_rows[u][:, t, :], blocks[:, n * 512:(n + 1) * 512],
                             start=True, stop=True)
                return ins

            def read_out(u, slot, q_rows, q0, state, v, k_tok):
                for t in range(LT):
                    mm(slot[u][:, t * P:(t + 1) * P], q_rows[u][:, t, q0:q0 + P], state[u][:, t, :],
                       start=t == 0, stop=False, skip_group_check=True)
                for h in range(LH):
                    mm(slot[u][:, h * LD:(h + 1) * LD], big[u][:, h * P:(h + 1) * P], v[u][:, h * LD:(h + 1) * LD],
                       start=False, stop=h == LH - 1, skip_group_check=True)
                for t in range(LT):
                    ins = mm(slot[u][:, 512 + t * P:512 + (t + 1) * P], k_tok[u][:, t * P:(t + 1) * P],
                             v[u][:, t * P:(t + 1) * P], start=True, stop=True)
                return ins

            def stage(s, l, u):
                A, B = slA[u], slB[u]
                if s == "xT":
                    W(dve_done, u, "X")
                    WB(dve_done, u, f"hid_{DEPTH - 1}")
                    for k in range(KD):
                        ins = tr(A[:, k * P:(k + 1) * P], X[u][:, k * P:(k + 1) * P], ident[:, :])
                    ins.then_inc(*I(u, "xT"))
                elif s == "qT":
                    W(act_done, u, "XT")
                    WB(dve_done, u, f"x2_{DEPTH - 1}")
                    prog.wait_dma_before(kv_kept[DEPTH - 1][u], u, KV_DMAS)
                    for t in range(LT):
                        for k in range(KD):
                            ins = mm(B[:, t * 256:t * 256 + P + 1], q1w[:, k, t * P:(t + 1) * P],
                                     XT[u][:, k, :], start=k == 0, stop=k == KD - 1)
                    ins.then_inc(*I(u, "qT"))
                elif s == "kT":
                    for i, (w, c0) in enumerate(((k1w, 1), (k2w, 0))):
                        for t in range(LT):
                            for k in range(KD):
                                ins = mm(A[:, D * i + t * P:D * i + (t + 1) * P], w[:, k, t * P:(t + 1) * P],
                                         XT[u][:, k, c0:c0 + P], start=k == 0, stop=k == KD - 1)
                    ins.then_inc(*I(u, "kT"))
                elif s == "tok":
                    for o, w, c0 in ((B[:, 512:512 + D], k1w, 1), (A[:, 512:512 + D], k2w, 0)):
                        for k in range(KD):
                            ins = mm(o, XT[u][:, k, c0:c0 + P], w[:, k, :], start=k == 0, stop=k == KD - 1)
                    ins.then_inc(*I(u, "tok"))
                elif s == "s1a":
                    W(dve_done, u, "bd1a")
                    W(act_done, u, "K2tok")
                    scores(u, slA, KT, big[u][:, 0:1024], 0).then_inc(*I(u, "s1a"))
                elif s == "s1b":
                    W(dve_done, u, "gsum")
                    scores(u, slB, KT, big[u][:, 1024:2048], 1).then_inc(*I(u, "s1b"))
                elif s == "cum":
                    W(act_done, u, "lnG")
                    W(dve_done, u, "A1a")
                    WB(pool_done, u, "acc_keep")
                    mm(A[:, 0:LH], tri[:, :], logG[u][:, :], start=True, stop=False)
                    mm(A[:, 0:LH], ones[:, :], acc[u][:, :], start=False, stop=True).then_inc(*I(u, "cum"))
                elif s == "o1":
                    W(dve_done, u, "A1b")
                    W(pool_done, u, "Vu")
                    read_out(u, slA, QT, 1, S1, Vu, Ktok).then_inc(*I(u, "o1"))
                elif s == "shift":
                    W(dve_done, u, "O1")
                    WB(act_done, u, "O1p")
                    mm(B[:, 0:D], shift[:, :], O1[u][:, :], start=True, stop=False)
                    mm(B[:, 0:D], last[:, :], O1p[u][:, :], start=False, stop=True).then_inc(*I(u, "shift"))
                elif s == "s2a":
                    W(dve_done, u, "dS1")
                    W(dve_done, u, "K2T")
                    W(pool_done, u, "bd2a")
                    scores(u, slA, K2T, bd2a[u], 0).then_inc(*I(u, "s2a"))
                elif s == "s2b":
                    W(dve_done, u, "En")
                    scores(u, slB, K2T, big[u][:, 1024:2048], 1).then_inc(*I(u, "s2b"))
                elif s == "o2":
                    W(dve_done, u, "A2b")
                    read_out(u, slA, QmT, 0, S2, En, K2tok).then_inc(*I(u, "o2"))
                elif s == "OT":
                    W(dve_done, u, "O")
                    for k in range(KD):
                        ins = tr(B[:, k * P:(k + 1) * P], En[u][:, k * P:(k + 1) * P], ident[:, :])
                    ins.then_inc(*I(u, "OT"))
                elif s == "cproj":
                    W(act_done, u, "OT")
                    W(dve_done, u, "dS2")
                    for k in range(KD):
                        ins = mm(A[:, 0:D], hT[u][:, k * P:(k + 1) * P], cw[:, k, :], start=k == 0, stop=k == KD - 1)
                    ins.then_inc(*I(u, "cproj"))
                elif s == "h":
                    W(dve_done, u, f"x2_{l - 1}" if l else "z")
                    tr(B[:, 0:P], X[u][:, 0:P], ident[:, :])
                    WB(act_done, u, f"xph_{l}")
                    mm(B[:, P:D], X[u][:, P:D], shift[:, :], start=True, stop=False)
                    mm(B[:, P:D], xph[l][u][:, :], last[:, :], start=False, stop=True).then_inc(*I(u, f"hT_{l}"))
                elif s == "qk":
                    W(act_done, u, f"hT_{l}")
                    W(dve_done, u, f"hid_{l - 1}" if l else "lnc")
                    for n in range(2):
                        for k in range(KD):
                            ins = mm(A[:, n * 512:(n + 1) * 512], hT[u][:, k * P:(k + 1) * P],
                                     wqkv_s[l][:, k, n * 512:(n + 1) * 512], start=k == 0, stop=k == KD - 1)
                    ins.then_inc(*I(u, f"qk_{l}"))
                elif s == "v":
                    for k in range(KD):
                        ins = mm(B[:, 0:512], hT[u][:, k * P:(k + 1) * P], wqkv_s[l][:, k, 1024:1536],
                                 start=k == 0, stop=k == KD - 1)
                    ins.then_inc(*I(u, f"v_{l}"))
                elif s == "qkT":
                    W(dve_done, u, f"kn_{l}")
                    for i in range(2 * AT):
                        ins = tr(A[:, i * P:(i + 1) * P], qkrot[u][:, i * P:(i + 1) * P], ident[:, :])
                    ins.then_inc(*I(u, f"qkT_{l}"))
                elif s in ("sa", "sb"):
                    if s == "sa":
                        W(act_done, u, f"kT_{l}")
                    else:
                        W(act_done, u, f"v_{l}")
                    slot, t0 = (A, 0) if s == "sa" else (B, 2)
                    for i in range(2):
                        ins = mm(slot[:, 512 * i:512 * i + 512], qT[u][:, t0 + i, :],
                                 kTd[l][u][:, t0 + i, :, :].rearrange("p h n -> p (h n)"), start=True, stop=True)
                    ins.then_inc(*I(u, f"{s}_{l}"))
                elif s in ("pa", "pb"):
                    W(act_done, u, f"e{s[1]}_{l}")
                    slot, o = (A, 0) if s == "pa" else (B, 1024)
                    for i in range(8):
                        ins = tr(slot[:, i * P:(i + 1) * P], big[u][:, o + i * P:o + (i + 1) * P], ident[:, :])
                    ins.then_inc(*I(u, f"{s}_{l}"))
                elif s == "av":
                    W(act_done, u, f"pa_{l}")
                    W(dve_done, u, f"pb_{l}")
                    for h in range(AH):
                        o = A[:, h * AD:(h + 1) * AD]
                        mm(o, big[u][:, 256 * h:256 * h + P], prevV[l][u][:, h * AD:(h + 1) * AD],
                           start=True, stop=False)
                        ins = mm(o, big[u][:, 256 * h + P:256 * h + 256], vcur[u][:, h * AD:(h + 1) * AD],
                                 start=False, stop=True)
                    ins.then_inc(*I(u, f"av_{l}"))
                elif s == "oT":
                    W(dve_done, u, f"on_{l}")
                    for t in range(AT):
                        ins = tr(B[:, t * P:(t + 1) * P], on[u][:, t * P:(t + 1) * P], ident[:, :])
                    ins.then_inc(*I(u, f"oT_{l}"))
                elif s == "wo":
                    W(act_done, u, f"oT_{l}")
                    for t in range(AT):
                        ins = mm(A[:, 0:D], oT[u][:, t, :], wo_s[l][:, t, :], start=t == 0, stop=t == AT - 1)
                    ins.then_inc(*I(u, f"wo_{l}"))
                elif s == "xs":
                    W(dve_done, u, f"x_{l}")
                    WB(act_done, u, f"xph2_{l}")
                    mm(B[:, 0:P], shift[:, :], X[u][:, P:D], start=True, stop=False)
                    mm(B[:, 0:P], last[:, :], xph2[l][u][:, :], start=False, stop=True).then_inc(*I(u, f"xs_{l}"))
                elif s == "h2T":
                    W(dve_done, u, f"hn_{l}")
                    for k in range(KD):
                        ins = tr(A[:, k * P:(k + 1) * P], hn[u][:, k * P:(k + 1) * P], ident[:, :])
                    ins.then_inc(*I(u, f"h2T_{l}"))
                elif s in ("w1g", "w1a"):
                    W(act_done, u, f"h2T_{l}")
                    slot, o = (B, HID) if s == "w1g" else (A, 0)
                    for j in range(HT):
                        m = P if j < HT - 1 else HLAST
                        for k in range(KD):
                            ins = mm(slot[0:m, j * P:(j + 1) * P], w1_s[l][:, k, o + j * P:o + j * P + m],
                                     hT[u][:, k * P:(k + 1) * P], start=k == 0, stop=k == KD - 1)
                    ins.then_inc(*I(u, f"{s}_{l}"))
                elif s == "w2":
                    W(dve_done, u, f"hid_{l}")
                    for j in range(HT):
                        m = P if j < HT - 1 else HLAST
                        ins = mm(B[:, 0:D], big[u][0:m, 768 + j * P:768 + (j + 1) * P], w2_s[l][0:m, j, :],
                                 start=j == 0, stop=j == HT - 1)
                    ins.then_inc(*I(u, f"w2_{l}"))

            walk(pe, prog, stage)

        @block.vector
        def _(dve):
            v = nc.vector
            dve.wait_ge(made2, 9)
            dve.wait_ge(w_first, 16 * 6)
            dve.wait_ge(w_rest, 16 * DEPTH * 18)
            prog = Prog(dve, dve_done)
            W, WB, I = prog.wait, prog.wait_before, prog.inc

            def heads_of(t, n):
                return t.rearrange("p (h d) -> p h d", h=n)

            def settle(u):
                v.memset(carry[u][:, :], 0.0)

            def ln_stats(u, src, name):
                v.bn_stats(st6[u][:, 0, :], src).then_inc(*I(u, name + "_stats"))
                W(dve_done, u, name + "_stats")
                settle(u)
                v.bn_aggr(mv[u][:, :], st6[u][:, 0, :]).then_inc(*I(u, name + "_agg"))
                W(dve_done, u, name + "_agg")
                v.tensor_scalar(ve[u][:, :], mv[u][:, 1:2], EPS, None, ALU.add).then_inc(*I(u, name + "_eps"))

            def ln_apply(u, dst, src, name, step):
                W(dve_done, u, name + "_eps")
                W(pool_done, u, name + "_rstd")
                v.tensor_scalar(dst, src, mv[u][:, 0:1], rstd[u][:, 0:1], ALU.subtract,
                                ALU.mult).then_inc(*I(u, step))

            def masked(u, slot, half, step):
                v.tensor_tensor(big[u][:, 1024 * half:1024 * half + 1024].rearrange("p (h n) -> p h n", h=8),
                                slot[u][:, :].rearrange("p (h n) -> p h n", h=8),
                                tri[:, None, :].to_broadcast([P, 8, P]), ALU.mult).then_inc(*I(u, step))

            def grow_state(u, state, n):
                ds = slA[u][:, 512:768].rearrange("p (t h e) -> p t h e", t=LT, h=LPT)
                W(pool_done, u, "hmk")
                tmp = scr[u][:, :].rearrange("p (t h e) -> p t h e", t=LT, h=LPT)
                v.tensor_tensor(tmp, ds, hmk[u][:, None, :, None].to_broadcast([P, LT, LPT, LD]),
                                ALU.mult).then_inc(*I(u, f"dS{n}"))
                W(dve_done, u, f"dS{n}")
                st = state[u][:, :, :].rearrange("p t n -> p (t n)")
                v.scalar_tensor_tensor(st, st, fl[u][:, 1:2], scr[u][:, :], ALU.mult,
                                       ALU.add).then_inc(*I(u, f"S{n}"))

            def head_blocks(u, dst, src, step):
                v.tensor_tensor(dst.rearrange("p (h n) -> p h n", h=LPT), src.to_broadcast([P, LPT, P]),
                                head1[:, :, None].to_broadcast([P, LPT, P]), ALU.mult).then_inc(*I(u, step))

            def sigmoid_of_exp(u, t, step):
                v.tensor_scalar(t, t, 1.0, None, ALU.add).then_inc(*I(u, step + "_1"))
                W(dve_done, u, step + "_1")
                v.reciprocal(t, t).then_inc(*I(u, step))

            def stage(s, l, u):
                A, B = slA[u], slB[u]
                if s == "ln0":
                    dve.wait_ge(x_in[u], prog.chunk[u] * 16 + 16)
                    WB(dve_done, u, "lnf")
                    WB(act_done, u, f"gelu_{DEPTH - 1}")
                    ln_stats(u, xin[u][:, :], "ln0")
                    ln_apply(u, X[u][:, :], xin[u][:, :], "ln0", "X")
                elif s == "qT":
                    W(act_done, u, "QmT")
                    v.scalar_tensor_tensor(QmT[u], QT[u], -0.02 / LD ** 0.5, QmT[u], ALU.mult,
                                           ALU.max).then_inc(*I(u, "Qm"))
                    head_blocks(u, big[u][:, 0:1024], QT[u][:, 0:1, 1:P + 1], "bd1a")
                    head_blocks(u, big[u][:, 1024:2048], QT[u][:, 1:2, 1:P + 1], "bd1b")
                elif s == "kT":
                    W(act_done, u, "K2T")
                    sigmoid_of_exp(u, K2T[u], "K2T")
                elif s == "tok":
                    W(pe_done, u, "tok")
                    k = B[:, 512:512 + D]
                    v.tensor_copy(Ktok[u][:, :], k).then_inc(*I(u, "Ktok"))
                    v.tensor_tensor(heads_of(scr[u][:, :], LH), heads_of(k, LH),
                                    swb[:, None, :].to_broadcast([P, LH, LD]), ALU.mult).then_inc(*I(u, "rdot"))
                    W(dve_done, u, "rdot")
                    v.tensor_reduce(zz[u][:, LH:2 * LH], heads_of(scr[u][:, :], LH), AX.X,
                                    ALU.add).then_inc(*I(u, "rsum"))
                    W(pool_done, u, "gdot")
                    v.tensor_reduce(zz[u][:, 0:LH], heads_of(scr2[u][:, :], LH), AX.X,
                                    ALU.add).then_inc(*I(u, "gsum"))
                    W(act_done, u, "egate")
                    v.tensor_scalar(ez[u][:, :], ez[u][:, :], 1.0, None, ALU.add).then_inc(*I(u, "e1"))
                    W(dve_done, u, "e1")
                    v.reciprocal(sig[u][:, :], ez[u][:, :]).then_inc(*I(u, "sig"))
                    W(dve_done, u, "sig")
                    v.tensor_scalar(gr[u][:, 0:LH], sig[u][:, 0:LH], 1e-6, None, ALU.max).then_inc(*I(u, "G"))
                    v.tensor_tensor(gr[u][:, LH:2 * LH], zz[u][:, LH:2 * LH], sig[u][:, LH:2 * LH],
                                    ALU.mult).then_inc(*I(u, "R"))
                    W(act_done, u, "K2tok")
                    sigmoid_of_exp(u, K2tok[u][:, :], "K2tok")
                elif s == "cum":
                    W(pe_done, u, "cum")
                    v.tensor_scalar(lc[u][:, :], A[:, 0:LH], 30.0, None, ALU.min).then_inc(*I(u, "Lmin"))
                    W(dve_done, u, "Lmin")
                    v.tensor_scalar(lc[u][:, :], lc[u][:, :], -30.0, None, ALU.max).then_inc(*I(u, "Lclip"))
                    W(act_done, u, "eL")
                    v.tensor_scalar(gc[u][:, :], gc[u][:, :], 1e-6, None, ALU.add).then_inc(*I(u, "Gc"))
                    W(dve_done, u, "Gc")
                    v.reciprocal(rgc[u][:, :], gc[u][:, :]).then_inc(*I(u, "rGc"))
                    W(dve_done, u, "rGc")
                    v.tensor_tensor(uu[u][:, :], gr[u][:, LH:2 * LH], rgc[u][:, :], ALU.mult).then_inc(*I(u, "u"))
                elif s == "s1a":
                    W(pe_done, u, "s1a")
                    masked(u, slA, 0, "A1a")
                elif s == "s1b":
                    W(pe_done, u, "s1b")
                    masked(u, slB, 1, "A1b")
                elif s == "o1":
                    W(pe_done, u, "o1")
                    v.tensor_tensor(heads_of(O1[u][:, :], LH), heads_of(A[:, 0:D], LH),
                                    gc[u][:, :, None].to_broadcast([P, LH, LD]), ALU.mult).then_inc(*I(u, "O1"))
                    grow_state(u, S1, 1)
                    head_blocks(u, big[u][:, 1024:2048], QmT[u][:, 1:2, 0:P], "bd2b")
                elif s == "shift":
                    W(pe_done, u, "shift")
                    v.tensor_tensor(En[u][:, :], B[:, 0:D], X[u][:, :], ALU.subtract).then_inc(*I(u, "En"))
                    W(dve_done, u, "En")
                    v.tensor_scalar(En[u][:, :], En[u][:, :], fl[u][:, 2:3], None,
                                    ALU.mult).then_inc(*I(u, "En0"))
                elif s == "s2a":
                    W(pe_done, u, "s2a")
                    masked(u, slA, 0, "A2a")
                elif s == "s2b":
                    W(pe_done, u, "s2b")
                    masked(u, slB, 1, "A2b")
                elif s == "o2":
                    W(pe_done, u, "o2")
                    v.tensor_tensor(En[u][:, :], A[:, 0:D], O1[u][:, :], ALU.add).then_inc(*I(u, "O"))
                    grow_state(u, S2, 2)
                elif s == "cproj":
                    W(pe_done, u, "cproj")
                    ln_stats(u, A[:, 0:D], "lnc")
                    ln_apply(u, scr[u][:, :], A[:, 0:D], "lnc", "lnc")
                    W(dve_done, u, "lnc")
                    v.tensor_tensor(x1[u][:, :], scr[u][:, :], xin[u][:, :], ALU.add).then_inc(*I(u, "mid_x"))
                    W(dve_done, u, "mid_x")
                    ln_stats(u, x1[u][:, :], "lnz")
                    ln_apply(u, X[u][:, :], x1[u][:, :], "lnz", "z")
                elif s == "rot":
                    W(act_done, u, f"sq_{l}")
                    v.tensor_reduce(ssq[u][:, :], heads_of(big[u][:, 0:1024], 2 * AH), AX.X,
                                    ALU.add).then_inc(*I(u, f"ss_{l}"))
                    W(dve_done, u, f"ss_{l}")
                    v.tensor_scalar(ssq[u][:, :], ssq[u][:, :], 1e-24, None, ALU.max).then_inc(*I(u, f"ss_clip_{l}"))
                    W(pool_done, u, f"tab_{l}")
                    pqk = A[:, :]
                    tb = tabl[u]
                    v.tensor_tensor(qkrot[u].rearrange("p (s h d) -> p s h d", s=2, h=AH),
                                    pqk.rearrange("p (s h d) -> p s h d", s=2, h=AH),
                                    tb[:, 0:4:2, None, :].to_broadcast([P, 2, AH, AD]),
                                    ALU.mult).then_inc(*I(u, f"t1_{l}"))
                    raw = pqk.rearrange("p (s h a d) -> p s h a d", s=2, h=AH, a=2)
                    t2 = big[u][:, 1024:2048].rearrange("p (s h a d) -> p s h a d", s=2, h=AH, a=2)
                    half = AD // 2
                    for a in range(2):
                        ins = v.tensor_tensor(t2[:, :, :, a, :], raw[:, :, :, 1 - a, :],
                                              tb[:, 1:4:2, None, a * half:(a + 1) * half].to_broadcast(
                                                  [P, 2, AH, half]), ALU.mult)
                    ins.then_inc(*I(u, f"t2_{l}"))
                    W(dve_done, u, f"t2_{l}")
                    v.tensor_tensor(qkrot[u], qkrot[u], big[u][:, 1024:2048], ALU.add).then_inc(*I(u, f"rot_{l}"))
                    W(dve_done, u, f"rot_{l}")
                    W(pool_done, u, f"rnorm_{l}")
                    k = heads_of(qkrot[u][:, INNER:2 * INNER], AH)
                    v.tensor_tensor(k, k, rnorm[u][:, AH:2 * AH, None].to_broadcast([P, AH, AD]),
                                    ALU.mult).then_inc(*I(u, f"kn_{l}"))
                    v.tensor_scalar(sc8[u][:, :], rnorm[u][:, 0:AH], QK_SCALE, None,
                                    ALU.mult).then_inc(*I(u, f"sc8_{l}"))
                elif s in ("sa", "sb"):
                    W(pe_done, u, f"{s}_{l}")
                    W(dve_done, u, f"sc8_{l}")
                    W(pool_done, u, "band")
                    settle(u)
                    slot, h0 = (A, 0) if s == "sa" else (B, 4)
                    for i in range(4):
                        h = h0 + i
                        ins = v.tensor_tensor_reduce(big[u][:, 256 * h:256 * h + 256],
                                                     slot[:, 256 * i:256 * i + 256], bandu[u][:, :],
                                                     1.0, MASKED, ALU.add, ALU.max, mx[u][:, h:h + 1])
                    ins.then_inc(*I(u, f"m{s[1]}_{l}"))
                    W(dve_done, u, f"m{s[1]}_{l}")
                    v.scalar_tensor_tensor(nb[u][:, h0:h0 + 4], mx[u][:, h0:h0 + 4], -1.0, sc8[u][:, h0:h0 + 4],
                                           ALU.mult, ALU.mult).then_inc(*I(u, f"nb{s[1]}_{l}"))
                elif s == "pb":
                    W(pe_done, u, f"pb_{l}")
                    v.tensor_copy(big[u][:, 1024:2048], B[:, :]).then_inc(*I(u, f"pb_{l}"))
                elif s == "av":
                    v.reciprocal(rden[u][:, :], den[u][:, :]).then_inc(*I(u, f"rden_{l}"))
                    W(dve_done, u, f"rden_{l}")
                    W(pe_done, u, f"av_{l}")
                    v.tensor_tensor(heads_of(on[u], AH), heads_of(A[:, 0:INNER], AH),
                                    rden[u][:, :, None].to_broadcast([P, AH, AD]), ALU.mult).then_inc(*I(u, f"on_{l}"))
                elif s == "wo":
                    W(pe_done, u, f"wo_{l}")
                    W(act_done, u, f"xph_{l}")
                    v.tensor_tensor(X[u][:, :], X[u][:, :], A[:, 0:D], ALU.add).then_inc(*I(u, f"x_{l}"))
                elif s == "xs":
                    W(pe_done, u, f"xs_{l}")
                    W(dve_done, u, f"x_{l}")
                    v.bn_stats(st6[u][:, 0, :], X[u][:, 0:P]).then_inc(*I(u, f"st_a_{l}"))
                    v.bn_stats(st6[u][:, 1, :], B[:, 0:P]).then_inc(*I(u, f"st_b_{l}"))
                    W(dve_done, u, f"st_b_{l}")
                    settle(u)
                    v.bn_aggr(mv[u][:, :], st6[u][:, :, :].rearrange("p a b -> p (a b)")).then_inc(*I(u, f"ln_agg_{l}"))
                    W(dve_done, u, f"ln_agg_{l}")
                    v.tensor_scalar(ve[u][:, :], mv[u][:, 1:2], EPS, None, ALU.add).then_inc(*I(u, f"ln_eps_{l}"))
                    W(pool_done, u, f"ln_rstd_{l}")
                    v.tensor_scalar(hn[u][:, 0:P], X[u][:, 0:P], mv[u][:, 0:1], rstd[u][:, 0:1],
                                    ALU.subtract, ALU.mult)
                    v.tensor_scalar(hn[u][:, P:D], B[:, 0:P], mv[u][:, 0:1], rstd[u][:, 0:1],
                                    ALU.subtract, ALU.mult).then_inc(*I(u, f"hn_{l}"))
                elif s == "w1a":
                    W(pe_done, u, f"w1a_{l}")
                    W(act_done, u, f"gelu_{l}")
                    for j in range(HT):
                        m = P if j < HT - 1 else HLAST
                        ins = v.scalar_tensor_tensor(big[u][0:m, 768 + j * P:768 + (j + 1) * P],
                                                     A[0:m, j * P:(j + 1) * P], b1a[l][0:m, j:j + 1],
                                                     big[u][0:m, j * P:(j + 1) * P], ALU.add, ALU.mult)
                    ins.then_inc(*I(u, f"hid_{l}"))
                elif s == "w2":
                    W(pe_done, u, f"w2_{l}")
                    W(pool_done, u, f"xb2_{l}")
                    v.tensor_tensor(X[u][:, :], X[u][:, :], B[:, 0:D], ALU.add).then_inc(*I(u, f"x2_{l}"))
                elif s == "out":
                    W(dve_done, u, f"x2_{DEPTH - 1}")
                    ln_stats(u, X[u][:, :], "lnf")
                    ln_apply(u, scr[u][:, :], X[u][:, :], "lnf", "lnf")
                    W(dve_done, u, "lnf")
                    prog.wait_dma_before(stored[u], u, 16)
                    v.tensor_tensor(xo[u][:, :], scr[u][:, :], x1[u][:, :], ALU.add).then_inc(*I(u, "out"))

            walk(dve, prog, stage)


def kernel(**inputs):
    import numpy as _np
    import concourse.bacc as _bacc
    from concourse import mybir as _mybir
    from concourse.bass_utils import run_bass_kernel_spmd as _run

    nc = _bacc.Bacc("TRN2", target_bir_lowering=False, num_devices=1)
    half_idx = _np.arange(0, AD, 2, dtype=_np.float64)
    t = _np.arange(SEQ, dtype=_np.float64)
    inv_freq = (1.0 / 10000.0 ** (half_idx / AD)).astype(_np.float32).astype(_np.float64)
    freqs = (t[:, None] * inv_freq[None, :]).astype(_np.float32).astype(_np.float64)
    freqs = _np.concatenate([freqs, freqs], axis=-1)
    base = (half_idx + 0.4 * AD) / (1.4 * AD)
    scale = base[None, :] ** ((t - SEQ // 2) / 64.0)[:, None]
    scale = _np.concatenate([scale, scale], axis=-1)
    sign = _np.concatenate([-_np.ones(AD // 2), _np.ones(AD // 2)])
    cos, sin = _np.cos(freqs), _np.sin(freqs) * sign
    xpos = _np.concatenate([cos * scale, sin * scale, cos / scale, sin / scale], axis=-1)
    flags = _np.ones((STEPS, P, 4))
    flags[:, :, 3] = 0.0
    flags[::CHUNKS, :, 0] = 0.0
    flags[CHUNKS - 1::CHUNKS, :, 1] = 0.0
    flags[::CHUNKS, 0, 2] = 0.0
    flags[::CHUNKS, :, 3] = MASKED
    table = _np.concatenate([_np.tile(xpos, (BATCH // UNITS, 1)), flags.reshape(STEPS * P, 4)],
                            axis=-1).astype(_np.float32)

    def arr(name):
        return _np.ascontiguousarray(inputs[name])

    data = {
        "x": arr("L0_attn_X").reshape(BATCH * SEQ, D), "table": table,
        "q1T": _np.ascontiguousarray(arr("L0_attn_q1_w").T), "k1T": _np.ascontiguousarray(arr("L0_attn_k1_w").T),
        "k2T": _np.ascontiguousarray(arr("L0_attn_k2_w").T),
        "gw": arr("L0_attn_gw_w"), "sw": arr("L0_attn_sw_w"),
        "cT": _np.ascontiguousarray(arr("L0_attn_c_proj_w").T),
        "wqkv": arr("L0_ffn_wqkv"), "qs": arr("L0_ffn_q_scale"), "ks": arr("L0_ffn_k_scale"),
        "wo": arr("L0_ffn_wo"), "lg": arr("L0_ffn_ln_g"), "lb": arr("L0_ffn_ln_b"),
        "w1": arr("L0_ffn_w1"), "b1": arr("L0_ffn_b1"), "w2": arr("L0_ffn_w2"), "b2": arr("L0_ffn_b2"),
    }
    args = [nc.dram_tensor(n, a.shape, _mybir.dt.from_np(a.dtype), kind="ExternalInput").ap()
            for n, a in data.items()]
    args.append(nc.dram_tensor("out", (BATCH * SEQ, D), F32, kind="ExternalOutput").ap())
    build(nc, *args)
    r = _run(nc, [data], core_ids=[0])
    return r.results[0]["out"].reshape(BATCH, SEQ, D)
```

```python
from contextlib import ExitStack

import concourse.bass as bass
from concourse import mybir

F32 = mybir.dt.float32
ALU = mybir.AluOpType
ACT = mybir.ActivationFunctionType
AX = mybir.AxisListType

P = 128
D = 256
KD = D // P
BATCH, SEQ = 4, 1024
CHUNKS = SEQ // P
UNITS = 2
STEPS = BATCH // UNITS * CHUNKS
LH, LD = 16, 16
LT = LH * LD // P
LPT = LH // LT
DEPTH = 2
AH, AD = 8, 64
INNER = AH * AD
AT = INNER // P
HID = 682
HT = (HID + P - 1) // P
HLAST = HID - (HT - 1) * P
QK_SCALE = 8.0
HID_TILES = {"": range(4), "2": range(4, HT)}
MASKED = -1e30
EPS = 1e-5
KEEP, KEEP_NEXT, ROW, PREV = range(4 * AD, 4 * AD + 4)
TABW = 4 * AD + 4


def layered(names):
    return [f"{n}_{l}" for l in range(DEPTH) for n in names]


PE_FIRST = ["xT", "qT", "kT", "tok", "s1a", "s1b", "cum", "o1", "shift", "tok2", "s2a", "s2b", "o2", "OT", "cproj"]
ACT_FIRST = ["XT_halo", "XT", "QT", "QmT", "KT", "K2T", "Ktok", "egate", "lnG", "eL", "O1p", "K2tok", "OT"]
DVE_FIRST = ["ln0_stats", "ln0_agg", "ln0_eps", "X", "Qm", "bd1a", "bd1b", "K2T_1", "K2T",
             "rdot", "rsum", "gsum", "e1", "sig", "G", "R", "A1a", "A1b",
             "Lmin", "Lclip", "Gc", "rGc", "u", "O1", "dS1", "S1", "bd2b", "En", "En0",
             "A2a", "A2b", "O", "dS2", "S2", "lnc_stats", "lnc_agg", "lnc_eps", "lnc", "mid_x",
             "lnz_stats", "lnz_agg", "lnz_eps", "z"]
POOL_FIRST = ["ln0_rstd", "hmk", "gdot", "Vu", "acc", "acc_keep", "bd2a", "lnc_rstd", "lnz_rstd"]
PE_LAYERS = layered(["hT", "v", "qk", "qkT", "s0", "s1", "s2", "s3", "p0", "p1", "p2", "p3", "av", "oT", "wo",
                     "xs", "h2T", "w1g", "w1a", "w1g2", "w1a2", "w2"])
ACT_LAYERS = ["flags", "x1", "z"] + layered(["halo", "hT", "v", "sq", "qT", "kT", "e0", "e1", "e2", "e3",
                                             "p0", "p2", "oT", "xph2", "h2T", "gelu", "gelu2"])
DVE_LAYERS = layered(["ss", "ss_clip", "t1", "t2", "rot", "kn", "sc8", "m0", "nb0", "m1", "nb1", "m2", "nb2",
                      "m3", "nb3", "p1", "p3", "rden", "on", "x", "st_a", "st_b", "ln_agg", "ln_eps", "hn",
                      "hid", "hid2", "x2"]) + ["lnf_stats", "lnf_agg", "lnf_eps", "lnf", "out"]
POOL_LAYERS = ["band"] + layered(["tab", "rnorm", "ln_rstd", "xb2"]) + ["lnf_rstd"]

FIRST, LAYERS = 0, 1
STAGES = ([(s, None) for s in ("ln0", "xT", "qT", "kT", "tok", "s1a", "s1b", "cum", "o1", "shift", "tok2",
                               "s2a", "s2b", "o2", "OT", "cproj")],
          [("in", None)] + [(s, l) for l in range(DEPTH) for s in (
              "h", "v", "qk", "rot", "qkT", "s0", "s1", "s2", "s3", "p0", "p1", "p2", "p3", "av", "oT", "wo",
              "xs", "h2T", "w1g", "w1a", "w1g2", "w1a2", "w2")] + [("out", None)])

THREADS = {"A": (FIRST, 0), "B": (FIRST, 1), "a": (LAYERS, 0), "b": (LAYERS, 1)}
PERIOD = {
    "sp": "baaAbbaB",
    "pool": "ABbaAbAbaaBabaABBbaAabbBBAAabBbbaa",
    "act": "abbAabbaaBAaaBbBbBBbabbabaaaaAbaBbaBabbbaBbaaAbbabBaabaaaBAaAbAAbbabbbAbAAaabaaaBabbbabAaa"
           "bbbB",
    "pe": "aabAaababBaAaaABbBbbAbabBbAaabaAababaBaababAababaBbbaBbbaabaaBbabBbbaBaaAAbBAbbbbABbbaBbba"
          "baabBaaAbaabBaAbabaAbbababaA",
    "dve": "AaaAAAabbbbbaAaaababbABBbBBAaaabaBbbaBaBABabaAAbAababBaBbABaAbaBbBBaaaaAbbbBbbaaaBabbbbaBA"
           "AbAABAbAbABabaaaAbabBbaBaABaBBAbaAbaabbbbB",
}
BEGIN = {
    "sp": {"A": (0, 2), "B": (0, 2), "a": (2, 0), "b": (1, 0)},
    "pool": {"A": (4, 1), "B": (1, 1), "a": (6, 0), "b": (2, 0)},
    "act": {"A": (9, 1), "B": (1, 1), "a": (16, 0), "b": (2, 0)},
    "pe": {"A": (8, 1), "B": (0, 1), "a": (17, 0), "b": (0, 0)},
    "dve": {"A": (13, 1), "B": (2, 1), "a": (16, 0), "b": (0, 0)},
}


class Done:

    def __init__(self, sems, steps):
        assert len(set(steps)) == len(steps)
        self.sems, self.steps, self.at = sems, steps, {n: i + 1 for i, n in enumerate(steps)}

    def __getitem__(self, u):
        return self.sems[u]

    def value(self, step, chunk):
        return chunk * len(self.steps) + self.at[step]


def build(nc, x, table, q1T, k1T, k2T, gw, sw, cT, wqkv, qs, ks, wo, lg, lb, w1, b1, w2, b2, out):
    with ExitStack() as ctx:
        def sb(name, *shape):
            return ctx.enter_context(nc.sbuf_tensor(name, [P, *shape], F32))

        def sem(name):
            return ctx.enter_context(nc.semaphore(name))

        ident, shift, last, tri, ones = (sb(n, P) for n in ("ident", "shift", "last", "tri", "ones"))
        band = sb("band", P)
        head1 = sb("head1", LPT)
        mhalf = sb("mhalf", LH)
        gwb, swb = sb("gwb", LD), sb("swb", LD)
        q1w, k1w, k2w = (sb(n, KD, D) for n in ("q1w", "k1w", "k2w"))
        cw = sb("cw", KD, D)
        wqkv_s = [sb(f"wqkv_{l}", KD, 3 * INNER) for l in range(DEPTH)]
        wo_s = [sb(f"wo_{l}", AT, D) for l in range(DEPTH)]
        w1_s = [sb(f"w1_{l}", KD, 2 * HID) for l in range(DEPTH)]
        w2_s = [sb(f"w2_{l}", HT, D) for l in range(DEPTH)]
        scales = [sb(f"scales_{l}", 4, AD) for l in range(DEPTH)]
        lgc, lbc = ([sb(f"{n}_{l}", KD) for l in range(DEPTH)] for n in ("lgc", "lbc"))
        b1a, b1g = ([sb(f"{n}_{l}", HT) for l in range(DEPTH)] for n in ("b1a", "b1g"))
        b2b = [sb(f"b2b_{l}", D) for l in range(DEPTH)]

        def per_unit(name, *shape):
            return [sb(f"{name}{u}", *shape) for u in range(UNITS)]

        xin, XA = per_unit("xin", D), per_unit("XA", D)
        fla = per_unit("fla", 4)
        XT = per_unit("XT", KD, P + 1)
        sc = per_unit("sc", 2048)
        QT, QmT = per_unit("QT", LT, P + 1), per_unit("QmT", LT, P + 1)
        KT, K2T = per_unit("KT", LT, P), per_unit("K2T", LT, P)
        hmk = per_unit("hmk", LPT)
        Ktok, K2tok = per_unit("Ktok", D), per_unit("K2tok", D)
        Vu, O1, O1p, En = (per_unit(n, D) for n in ("Vu", "O1", "O1p", "En"))
        S1, S2 = per_unit("S1", LT, P), per_unit("S2", LT, P)
        acc = per_unit("acc", LH)
        scr, scr2 = per_unit("scr", D), per_unit("scr2", D)
        zz = per_unit("zz", 2 * LH)
        ez, sig = per_unit("ez", 2 * LH), per_unit("sig", 2 * LH)
        gr = per_unit("gr", 2 * LH)
        logG, lc, gc, rgc, uu = (per_unit(n, LH) for n in ("logG", "lc", "gc", "rgc", "uu"))
        OT = scr2

        x1, X = per_unit("x1", D), per_unit("X", D)
        tab, tabl, fl = per_unit("tab", TABW), per_unit("tabl", 4, AD), per_unit("fl", 4)
        bandu = per_unit("bandu", 2 * P)
        big = per_unit("big", 2048)
        qTd = per_unit("qTd", AT, 2, P)
        vcur, hT, hn = (per_unit(n, w) for n, w in (("vcur", INNER), ("hT", D), ("hn", D)))
        kT = [[sb(f"kT{l}_{u}", AT, 2 * P) for u in range(UNITS)] for l in range(DEPTH)]
        prevV = [[sb(f"prevV{l}_{u}", INNER) for u in range(UNITS)] for l in range(DEPTH)]
        xTs = [[sb(f"xTs{l}_{u}", P + 1) for u in range(UNITS)] for l in range(DEPTH)]
        xph2 = [[sb(f"xph2{l}_{u}", P) for u in range(UNITS)] for l in range(DEPTH)]
        ssq, rnorm = per_unit("ssq", 2 * AH), per_unit("rnorm", 2 * AH)
        sc8, mx, nb, den, rden = (per_unit(n, AH) for n in ("sc8", "mx", "nb", "den", "rden"))
        xo = hn

        def per_block(name, *shape):
            return [per_unit(name + b, *shape) for b in "ab"]
        st6, mv, ve, rstd = (per_block(n, *w) for n, w in (("st6", (2, 6)), ("mv", (2,)), ("ve", (1,)), ("rstd", (1,))))
        carry = per_block("carry", 1)

        qkrot = [b[:, 0:1024] for b in big]
        on = [b[:, 0:INNER] for b in big]
        oT = [b[:, 512:1024].rearrange("p (t n) -> p t n", t=AT) for b in big]

        psum = [[ctx.enter_context(nc.psum_tensor(f"psum{b}{u}", [P, 1024], F32)) for u in range(UNITS)]
                for b in "ab"]
        BANK = 512

        def done(name, steps):
            return Done([sem(f"{name}{u}") for u in range(UNITS)], steps)

        pe_first, act_first = done("pe_first", PE_FIRST), done("act_first", ACT_FIRST)
        dve_first, pool_first = done("dve_first", DVE_FIRST), done("pool_first", POOL_FIRST)
        pe_done, act_done = done("pe_done", PE_LAYERS), done("act_done", ACT_LAYERS)
        dve_done, pool_done = done("dve_done", DVE_LAYERS), done("pool_done", POOL_LAYERS)
        x_in, fla_in, tab_in = ([sem(f"{n}{u}") for u in range(UNITS)] for n in ("x_in", "fla_in", "tab_in"))
        kv_kept = [[sem(f"kv_kept{l}_{u}") for u in range(UNITS)] for l in range(DEPTH)]
        stored = [sem(f"stored{u}") for u in range(UNITS)]
        w_first, w_rest, made, made2 = (sem(n) for n in ("w_first", "w_rest", "made", "made2"))
        KV_DMAS = 2 * 16

        class Prog:

            def __init__(self, done):
                self.done, self.chunk, self.first, self.n = done, [0] * UNITS, [True] * UNITS, [0] * UNITS

            def at(self, done, u, step):
                return done.value(step, self.chunk[u])

            def again(self, u):
                return not self.first[u]

            def before(self, done, u, step):
                return done.value(step, self.chunk[u]) - len(done.steps)

            def inc(self, u, step):
                assert self.done.steps[self.n[u]] == step, (self.done.steps[self.n[u]], step)
                self.n[u] += 1
                return self.done[u], 1

        def walk(eng, name, progs, stages):
            def turns_of(block_, u):
                while True:
                    progs[block_].n[u] = 0
                    for s, l in STAGES[block_]:
                        yield from stages[block_](s, l, u)

            threads = {t: turns_of(*of) for t, of in THREADS.items()}
            order, begin = PERIOD[name], BEGIN[name]
            ahead = [max(a + (at > 0) for at, a in begin.values()), min(a for at, a in begin.values())]

            def period(c, number=True):
                at = {t: b[0] for t, b in begin.items()}
                lead = {t: b[1] for t, b in begin.items()}
                own = {}
                for t in order:
                    block_, u = THREADS[t]
                    if at[t] == order.count(t):
                        at[t], lead[t] = 0, lead[t] + 1
                    at[t] += 1
                    chunk = c + lead[t]
                    if number:
                        if not 0 <= chunk < STEPS:
                            continue
                    else:
                        if (t, lead[t]) not in own:
                            reg = eng.alloc_register(f"chunk_{t}{lead[t]}")
                            eng.reg_mov(reg, chunk)
                            own[t, lead[t]] = eng.snap(reg, donate=True, min_val=0, max_val=STEPS - 1)
                        chunk = own[t, lead[t]]
                    progs[block_].chunk[u], progs[block_].first[u] = chunk, number and chunk == 0
                    next(threads[t])

            first_full, last_full = 1 - ahead[1], STEPS - 1 - ahead[0]
            for c in range(-ahead[0], first_full):
                period(c)
            with eng.Fori(first_full, last_full + 1) as c:
                period(c, number=False)
            for c in range(last_full + 1, STEPS - ahead[1]):
                period(c)

        block = ctx.enter_context(nc.Block())

        @block.sync
        def _(sp):
            def load(dst, src, s):
                sp.dma_start(dst, src).then_inc(s, 16)

            for dst, w in ((q1w, q1T), (k1w, k1T), (k2w, k2T), (cw, cT)):
                load(dst[:, :, :], w.rearrange("(k p) n -> p k n", p=P), w_first)
            load(gwb[:, :], gw.partition_broadcast(P), w_first)
            load(swb[:, :], sw.partition_broadcast(P), w_first)
            def load_layers():
                for l in range(DEPTH):
                    load(wqkv_s[l][:, :, :], wqkv[l].rearrange("(k p) n -> p k n", p=P), w_rest)
                    load(wo_s[l][:, :, :], wo[l].rearrange("(k p) n -> p k n", p=P), w_rest)
                    load(w1_s[l][:, :, :], w1[l].rearrange("(k p) n -> p k n", p=P), w_rest)
                    load(w2_s[l][:, 0:HT - 1, :], w2[l, 0:(HT - 1) * P].rearrange("(k p) n -> p k n", p=P), w_rest)
                    load(w2_s[l][0:HLAST, HT - 1, :], w2[l, (HT - 1) * P:HID], w_rest)
                    for i, s in ((0, qs), (2, ks)):
                        row = s[l].rearrange("(a n) -> a n", a=1)
                        half = AD // 2
                        load(scales[l][:, i, :], row.partition_broadcast(P), w_rest)
                        load(scales[l][:, i + 1, 0:half], row[:, half:AD].partition_broadcast(P), w_rest)
                        load(scales[l][:, i + 1, half:AD], row[:, 0:half].partition_broadcast(P), w_rest)
                    load(b2b[l][:, :], b2[l].rearrange("(a n) -> a n", a=1).partition_broadcast(P), w_rest)
                    with nc.allow_non_contiguous_dma("bias columns, once"):
                        load(lgc[l][:, :], lg[l].rearrange("(k p) -> p k", p=P), w_rest)
                        load(lbc[l][:, :], lb[l].rearrange("(k p) -> p k", p=P), w_rest)
                        for dst, o in ((b1a, 0), (b1g, HID)):
                            load(dst[l][:, 0:HT - 1], b1[l, o:o + (HT - 1) * P].rearrange("(k p) -> p k", p=P), w_rest)
                            load(dst[l][0:HLAST, HT - 1:HT],
                                 b1[l, o + (HT - 1) * P:o + HID].rearrange("(p k) -> p k", k=1), w_rest)

            first, layers = Prog(None), Prog(None)

            def stage_first(s, l, u):
                if s == "ln0":
                    c = first.chunk[u]
                    if first.again(u):
                        sp.wait_ge(dve_first[u], first.before(dve_first, u, "z"))
                    sp.dma_start(xin[u][:, :], x[bass.ds(u * (STEPS * P) + c * P, P), :]).then_inc(x_in[u], 16)
                    sp.dma_start(fla[u][:, :], table[bass.ds(c * P, P), 4 * AD:TABW]).then_inc(fla_in[u], 16)
                    if u == UNITS - 1 and first.first[u]:
                        load_layers()
                    yield

            def stage_layers(s, l, u):
                c = layers.chunk[u]
                if s == "in":
                    if layers.again(u):
                        sp.wait_ge(pool_done[u], layers.before(pool_done, u, f"tab_{DEPTH - 1}"))
                    sp.dma_start(tab[u][:, :], table[bass.ds(c * P, P), :]).then_inc(tab_in[u], 16)
                    yield
                elif s == "oT":
                    sp.wait_ge(pe_done[u], layers.at(pe_done, u, f"av_{l}"))
                    sp.dma_start(kT[l][u][:, :, 0:P], kT[l][u][:, :, P:2 * P]).then_inc(kv_kept[l][u], 16)
                    sp.dma_start(prevV[l][u][:, :], vcur[u][:, :]).then_inc(kv_kept[l][u], 16)
                    yield

            walk(sp, "sp", (first, layers), (stage_first, stage_layers))
            for u in range(UNITS):
                sp.wait_ge(stored[u], STEPS * 16)
                for l in range(DEPTH):
                    sp.wait_ge(kv_kept[l][u], STEPS * KV_DMAS)

        @block.gpsimd
        def _(pool):
            g = nc.gpsimd
            fills = [(ident, 0.0), (shift, 0.0), (last, 0.0), (tri, 1.0), (ones, 1.0), (mhalf, -0.5), (head1, 1.0),
                     *((b, 0.0) for b in bandu)]
            fills += [(t, 0.0) for t in (*XT, *acc, *O1p, *S1, *S2, *kT[0], *kT[1], *qTd, *prevV[0], *prevV[1],
                                         *xTs[0], *xTs[1], *xph2[0], *xph2[1])]
            for t, v in fills:
                g.memset(t[:], v).then_inc(made, 1)
            g.memset(band[:, :], 0.0).then_inc(made, 1)
            pool.wait_ge(made, len(fills) + 1)

            def sel(t, pattern, base, mult, op, fill):
                g.affine_select(out=t, in_=t, pattern=pattern, base=base, channel_multiplier=mult,
                                compare_op=op, fill=fill).then_inc(made2, 1)
            sel(ident[:, :], [[-1, P]], 0, 1, ALU.not_equal, 1.0)
            sel(shift[:, :], [[-1, P]], 1, 1, ALU.not_equal, 1.0)
            sel(last[:, :], [[-1, P]], -(P - 1), 1, ALU.not_equal, 1.0)
            sel(tri[:, :], [[1, P]], 0, -1, ALU.is_ge, 0.0)
            sel(band[:, :], [[1, P]], 0, -1, ALU.is_ge, MASKED)
            for u in range(UNITS):
                sel(bandu[u][:, P:2 * P], [[-1, P]], 0, 1, ALU.is_ge, MASKED)
            sel(head1[:, :], [[-LD, LPT]], 0, 1, ALU.is_ge, 0.0)
            pool.wait_ge(made2, 8)
            sel(head1[:, :], [[LD, LPT]], LD - 1, -1, ALU.is_ge, 0.0)
            pool.wait_ge(made2, 9)
            pool.wait_ge(w_first, 16 * 6)
            first, layers = Prog(pool_first), Prog(pool_done)

            def rstd_of(u, block_, name):
                prog, dve_steps = ((first, dve_first), (layers, dve_done))[block_]
                pool.wait_ge(dve_steps[u], prog.at(dve_steps, u, name.replace("ln_rstd", "ln_eps").replace("_rstd", "_eps")))
                g.tensor_tensor(rstd[block_][u][:, :], ve[block_][u][:, :], mhalf[:, 0:1],
                                ALU.pow).then_inc(*prog.inc(u, name))

            def stage_first(s, l, u):
                at, again, before, I = first.at, first.again, first.before, first.inc
                if s == "ln0":
                    rstd_of(u, FIRST, "ln0_rstd")
                    pool.wait_ge(fla_in[u], first.chunk[u] * 16 + 16)
                    g.tensor_tensor(hmk[u][:, :], head1[:, :], fla[u][:, 1:2].to_broadcast([P, LPT]),
                                    ALU.mult).then_inc(*I(u, "hmk"))
                    yield
                elif s == "xT":
                    pool.wait_ge(dve_first[u], at(dve_first, u, "X"))
                    g.tensor_tensor(scr2[u][:, :].rearrange("p (h d) -> p h d", h=LH),
                                    XA[u][:, :].rearrange("p (h d) -> p h d", h=LH),
                                    gwb[:, None, :].to_broadcast([P, LH, LD]), ALU.mult).then_inc(*I(u, "gdot"))
                    yield
                elif s == "cum":
                    pool.wait_ge(dve_first[u], at(dve_first, u, "u"))
                    g.tensor_tensor(Vu[u][:, :].rearrange("p (h d) -> p h d", h=LH),
                                    XA[u][:, :].rearrange("p (h d) -> p h d", h=LH),
                                    uu[u][:, :, None].to_broadcast([P, LH, LD]), ALU.mult).then_inc(*I(u, "Vu"))
                    g.tensor_tensor(acc[u][:, :], acc[u][:, :], logG[u][:, :], ALU.add).then_inc(*I(u, "acc"))
                    yield
                    pool.wait_ge(pool_first[u], at(pool_first, u, "acc"))
                    g.tensor_tensor(acc[u][:, :], acc[u][:, :], fla[u][:, 1:2].to_broadcast([P, LH]),
                                    ALU.mult).then_inc(*I(u, "acc_keep"))
                    yield
                elif s == "o1":
                    pool.wait_ge(pe_first[u], at(pe_first, u, "o1"))
                    g.tensor_tensor(sc[u][:, 0:1024].rearrange("p (h n) -> p h n", h=LPT),
                                    QmT[u][:, 0:1, 0:P].to_broadcast([P, LPT, P]),
                                    head1[:, :, None].to_broadcast([P, LPT, P]), ALU.mult).then_inc(*I(u, "bd2a"))
                    yield
                elif s == "cproj":
                    rstd_of(u, FIRST, "lnc_rstd")
                    yield
                    rstd_of(u, FIRST, "lnz_rstd")
                    yield

            def stage_layers(s, l, u):
                at, again, before, I = layers.at, layers.again, layers.before, layers.inc
                if s == "in":
                    pool.wait_ge(act_done[u], at(act_done, u, "flags"))
                    if again(u):
                        pool.wait_ge(dve_done[u], before(dve_done, u, f"m3_{DEPTH - 1}"))
                    g.tensor_tensor(bandu[u][:, 0:P], band[:, :], fl[u][:, 3:4].to_broadcast([P, P]),
                                    ALU.add).then_inc(*I(u, "band"))
                    yield
                elif s == "h":
                    if layers.first[u]:
                        pool.wait_ge(w_rest, 16 * DEPTH * 18)
                    pool.wait_ge(act_done[u], at(act_done, u, "flags"))
                    g.tensor_tensor(tabl[u][:, :, :], tab[u][:, 0:4 * AD].rearrange("p (a n) -> p a n", a=4),
                                    scales[l][:, :, :], ALU.mult).then_inc(*I(u, f"tab_{l}"))
                    yield
                elif s == "rot":
                    pool.wait_ge(dve_done[u], at(dve_done, u, f"ss_clip_{l}"))
                    g.tensor_tensor(rnorm[u][:, :], ssq[u][:, :], mhalf[:, :], ALU.pow).then_inc(*I(u, f"rnorm_{l}"))
                    yield
                elif s == "xs":
                    rstd_of(u, LAYERS, f"ln_rstd_{l}")
                    yield
                elif s == "w1g":
                    pool.wait_ge(act_done[u], at(act_done, u, f"xph2_{l}"))
                    pool.wait_ge(dve_done[u], at(dve_done, u, f"hn_{l}"))
                    g.tensor_tensor(X[u][:, :], X[u][:, :], b2b[l][:, :], ALU.add).then_inc(*I(u, f"xb2_{l}"))
                    yield
                elif s == "out":
                    rstd_of(u, LAYERS, "lnf_rstd")
                    yield

            walk(pool, "pool", (first, layers), (stage_first, stage_layers))

        @block.scalar
        def _(act):
            def A(out_, in_, func, **kw):
                return nc.scalar.activation(out_, in_, func, **kw)

            act.wait_ge(made2, 9)
            first, layers = Prog(act_first), Prog(act_done)

            def stage_first(s, l, u):
                at, again, before, I = first.at, first.again, first.before, first.inc
                S = psum[FIRST][u]
                if s == "ln0":
                    act.wait_ge(fla_in[u], first.chunk[u] * 16 + 16)
                    if again(u):
                        act.wait_ge(pe_first[u], before(pe_first, u, "kT"))
                    A(XT[u][:, :, 0:1], XT[u][:, :, P:P + 1], ACT.Copy,
                      scale=fla[u][:, 0:1]).then_inc(*I(u, "XT_halo"))
                    yield
                elif s == "xT":
                    act.wait_ge(pe_first[u], at(pe_first, u, "xT"))
                    act.wait_ge(act_first[u], at(act_first, u, "XT_halo"))
                    A(XT[u][:, :, 1:P + 1], S[:, 0:D].rearrange("p (k n) -> p k n", k=KD),
                      ACT.Copy).then_inc(*I(u, "XT"))
                    yield
                elif s == "qT":
                    act.wait_ge(pe_first[u], at(pe_first, u, "qT"))
                    if again(u):
                        act.wait_ge(pe_first[u], before(pe_first, u, "o2"))
                    A(QT[u][:, :, :], S[:, BANK:1024].rearrange("p (t n) -> p t n", t=LT)[:, :, 0:P + 1],
                      ACT.Copy).then_inc(*I(u, "QT"))
                    yield
                    act.wait_ge(act_first[u], at(act_first, u, "QT"))
                    A(QmT[u][:, :, :], QT[u][:, :, :], ACT.Copy, scale=-1.0 / LD ** 0.5).then_inc(*I(u, "QmT"))
                    yield
                elif s == "kT":
                    act.wait_ge(pe_first[u], at(pe_first, u, "kT"))
                    A(KT[u][:, :, :], S[:, 0:D].rearrange("p (t n) -> p t n", t=LT), ACT.Copy).then_inc(*I(u, "KT"))
                    A(K2T[u][:, :, :], S[:, D:2 * D].rearrange("p (t n) -> p t n", t=LT), ACT.Exp,
                      scale=-0.02 / D ** 0.5).then_inc(*I(u, "K2T"))
                    yield
                elif s == "tok":
                    act.wait_ge(pe_first[u], at(pe_first, u, "tok"))
                    A(Ktok[u][:, :], S[:, BANK:BANK + D], ACT.Copy).then_inc(*I(u, "Ktok"))
                    yield
                    act.wait_ge(dve_first[u], at(dve_first, u, "gsum"))
                    A(ez[u][:, :], zz[u][:, :], ACT.Exp, scale=-1.0).then_inc(*I(u, "egate"))
                    yield
                    act.wait_ge(dve_first[u], at(dve_first, u, "G"))
                    A(logG[u][:, :], gr[u][:, 0:LH], ACT.Ln).then_inc(*I(u, "lnG"))
                    yield
                elif s == "cum":
                    act.wait_ge(dve_first[u], at(dve_first, u, "Lclip"))
                    A(gc[u][:, :], lc[u][:, :], ACT.Exp).then_inc(*I(u, "eL"))
                    yield
                elif s == "shift":
                    act.wait_ge(pe_first[u], at(pe_first, u, "shift"))
                    A(O1p[u][:, :], O1[u][:, :], ACT.Copy, scale=fla[u][:, 1:2]).then_inc(*I(u, "O1p"))
                    yield
                elif s == "tok2":
                    act.wait_ge(pe_first[u], at(pe_first, u, "tok2"))
                    A(K2tok[u][:, :], S[:, BANK:BANK + D], ACT.Copy).then_inc(*I(u, "K2tok"))
                    yield
                elif s == "OT":
                    act.wait_ge(pe_first[u], at(pe_first, u, "OT"))
                    A(OT[u][:, :], S[:, 0:D], ACT.Copy).then_inc(*I(u, "OT"))
                    yield

            def stage_layers(s, l, u):
                at, again, before, I = layers.at, layers.again, layers.before, layers.inc
                S = psum[LAYERS][u]
                if s == "in":
                    act.wait_ge(tab_in[u], layers.chunk[u] * 16 + 16)
                    A(fl[u][:, :], tab[u][:, 4 * AD:TABW], ACT.Copy).then_inc(*I(u, "flags"))
                    yield
                    act.wait_ge(dve_first[u], at(dve_first, u, "z"))
                    if again(u):
                        act.wait_ge(dve_done[u], before(dve_done, u, "out"))
                    A(x1[u][:, :], scr[u][:, :], ACT.Copy).then_inc(*I(u, "x1"))
                    A(X[u][:, :], XA[u][:, :], ACT.Copy).then_inc(*I(u, "z"))
                    yield
                elif s == "h":
                    act.wait_ge(act_done[u], at(act_done, u, "flags"))
                    if again(u):
                        act.wait_ge(pe_done[u], before(pe_done, u, f"qk_{l}"))
                    A(xTs[l][u][:, 0:1], xTs[l][u][:, P:P + 1], ACT.Copy, scale=fl[u][:, 0:1]).then_inc(*I(u, f"halo_{l}"))
                    yield
                    act.wait_ge(pe_done[u], at(pe_done, u, f"hT_{l}"))
                    act.wait_ge(act_done[u], at(act_done, u, f"halo_{l}"))
                    A(hT[u][:, 0:P], S[:, BANK:BANK + P], ACT.Copy)
                    A(xTs[l][u][:, 1:P + 1], S[:, BANK + P:BANK + D], ACT.Copy).then_inc(*I(u, f"hT_{l}"))
                    yield
                elif s == "v":
                    act.wait_ge(pe_done[u], at(pe_done, u, f"v_{l}"))
                    if l:
                        act.wait_ge(kv_kept[l - 1][u], layers.chunk[u] * KV_DMAS + KV_DMAS)
                    else:
                        if layers.again(u):
                            act.wait_ge(kv_kept[DEPTH - 1][u], layers.chunk[u] * KV_DMAS)
                    A(vcur[u][:, :], S[:, 0:INNER], ACT.Copy).then_inc(*I(u, f"v_{l}"))
                    yield
                elif s == "qk":
                    act.wait_ge(pe_done[u], at(pe_done, u, f"qk_{l}"))
                    A(big[u][:, 0:1024], S[:, :], ACT.Square).then_inc(*I(u, f"sq_{l}"))
                    yield
                elif s == "qkT":
                    act.wait_ge(pe_done[u], at(pe_done, u, f"qkT_{l}"))
                    for r in range(2):
                        half = slice(r * AD, (r + 1) * AD)
                        ins = A(qTd[u][half, :, r, :], S[half, 0:BANK].rearrange("p (t n) -> p t n", t=AT), ACT.Copy)
                    ins.then_inc(*I(u, f"qT_{l}"))
                    if layers.again(u):
                        act.wait_ge(kv_kept[l][u], layers.chunk[u] * KV_DMAS)
                    A(kT[l][u][:, :, P:2 * P], S[:, BANK:1024].rearrange("p (t n) -> p t n", t=AT),
                      ACT.Copy).then_inc(*I(u, f"kT_{l}"))
                    yield
                elif s in ("s0", "s1", "s2", "s3"):
                    i = int(s[1])
                    act.wait_ge(dve_done[u], at(dve_done, u, f"nb{i}_{l}"))
                    for h in (2 * i, 2 * i + 1):
                        p = big[u][:, 256 * h:256 * h + 256]
                        ins = A(p, p, ACT.Exp, bias=nb[u][:, h:h + 1], scale=sc8[u][:, h:h + 1],
                                accum_out=den[u][:, h:h + 1])
                    ins.then_inc(*I(u, f"e{i}_{l}"))
                    yield
                elif s in ("p0", "p2"):
                    i = int(s[1])
                    act.wait_ge(pe_done[u], at(pe_done, u, f"p{i}_{l}"))
                    A(big[u][:, 512 * i:512 * i + 512], S[:, 0:BANK], ACT.Copy).then_inc(*I(u, f"p{i}_{l}"))
                    yield
                elif s == "oT":
                    act.wait_ge(pe_done[u], at(pe_done, u, f"oT_{l}"))
                    A(oT[u].rearrange("p t n -> p (t n)"), S[:, BANK:1024], ACT.Copy).then_inc(*I(u, f"oT_{l}"))
                    yield
                elif s == "xs":
                    act.wait_ge(pe_done[u], at(pe_done, u, f"xs_{l}"))
                    A(xph2[l][u][:, :], X[u][:, P:D], ACT.Copy, scale=fl[u][:, 1:2]).then_inc(*I(u, f"xph2_{l}"))
                    yield
                elif s == "h2T":
                    act.wait_ge(pe_done[u], at(pe_done, u, f"h2T_{l}"))
                    if layers.first[u]:
                        act.wait_ge(w_rest, 16 * DEPTH * 18)
                    for k in range(KD):
                        ins = A(hT[u][:, k * P:(k + 1) * P], S[:, k * P:(k + 1) * P], ACT.Identity,
                                scale=lgc[l][:, k:k + 1], bias=lbc[l][:, k:k + 1])
                    ins.then_inc(*I(u, f"h2T_{l}"))
                    yield
                elif s in ("w1g", "w1g2"):
                    act.wait_ge(pe_done[u], at(pe_done, u, f"{s}_{l}"))
                    tiles = HID_TILES[s[3:]]
                    for n, j in enumerate(tiles):
                        m = P if j < HT - 1 else HLAST
                        ins = A(big[u][0:m, j * P:(j + 1) * P], S[0:m, n * P:(n + 1) * P], ACT.Gelu,
                                bias=b1g[l][0:m, j:j + 1])
                    ins.then_inc(*I(u, f"gelu{s[3:]}_{l}"))
                    yield
                elif s == "out":
                    act.wait_ge(dve_done[u], at(dve_done, u, "out"))
                    act.dma_start(out[bass.ds(u * (STEPS * P) + layers.chunk[u] * P, P), :],
                                  xo[u][:, :]).then_inc(stored[u], 16)
                    yield

            walk(act, "act", (first, layers), (stage_first, stage_layers))

        @block.tensor
        def _(pe):
            mm, tr = nc.tensor.matmul, nc.tensor.transpose
            pe.wait_ge(made2, 9)
            pe.wait_ge(w_first, 16 * 6)
            first, layers = Prog(pe_first), Prog(pe_done)

            def scores(u, k_rows, half):
                for n in range(2):
                    ins = mm(psum[FIRST][u][:, n * BANK:(n + 1) * BANK], k_rows[u][:, half, :],
                             sc[u][:, 1024 * half + n * BANK:1024 * half + (n + 1) * BANK], start=True, stop=True)
                return ins

            def read_out(u, q_rows, q0, state, v, k_tok):
                S = psum[FIRST][u]
                for t in range(LT):
                    mm(S[:, t * P:(t + 1) * P], q_rows[u][:, t, q0:q0 + P], state[u][:, t, :],
                       start=t == 0, stop=False, skip_group_check=True)
                for h in range(LH):
                    mm(S[:, h * LD:(h + 1) * LD], sc[u][:, h * P:(h + 1) * P], v[u][:, h * LD:(h + 1) * LD],
                       start=False, stop=h == LH - 1, skip_group_check=True)
                for t in range(LT):
                    ins = mm(S[:, BANK + t * P:BANK + (t + 1) * P], k_tok[u][:, t * P:(t + 1) * P],
                             v[u][:, t * P:(t + 1) * P], start=True, stop=True)
                return ins

            def stage_first(s, l, u):
                at, again, before, I = first.at, first.again, first.before, first.inc
                S = psum[FIRST][u]
                if s == "xT":
                    pe.wait_ge(dve_first[u], at(dve_first, u, "X"))
                    for k in range(KD):
                        ins = tr(S[:, k * P:(k + 1) * P], XA[u][:, k * P:(k + 1) * P], ident[:, :])
                    ins.then_inc(*I(u, "xT"))
                    yield
                elif s == "qT":
                    pe.wait_ge(act_first[u], at(act_first, u, "XT"))
                    for t in range(LT):
                        for k in range(KD):
                            ins = mm(S[:, BANK + t * 256:BANK + t * 256 + P + 1], q1w[:, k, t * P:(t + 1) * P],
                                     XT[u][:, k, :], start=k == 0, stop=k == KD - 1)
                    ins.then_inc(*I(u, "qT"))
                    yield
                elif s == "kT":
                    for i, (w, c0) in enumerate(((k1w, 1), (k2w, 0))):
                        for t in range(LT):
                            for k in range(KD):
                                ins = mm(S[:, D * i + t * P:D * i + (t + 1) * P], w[:, k, t * P:(t + 1) * P],
                                         XT[u][:, k, c0:c0 + P], start=k == 0, stop=k == KD - 1)
                    ins.then_inc(*I(u, "kT"))
                    yield
                elif s in ("tok", "tok2"):
                    if s == "tok":
                        pe.wait_ge(act_first[u], at(act_first, u, "KT"))
                    else:
                        pe.wait_ge(dve_first[u], at(dve_first, u, "dS1"))
                    for t in range(LT):
                        ins = tr(S[:, BANK + t * P:BANK + (t + 1) * P], (KT if s == "tok" else K2T)[u][:, t, :],
                                 ident[:, :])
                    ins.then_inc(*I(u, s))
                    yield
                elif s == "s1a":
                    pe.wait_ge(dve_first[u], at(dve_first, u, "bd1a"))
                    pe.wait_ge(act_first[u], at(act_first, u, "Ktok"))
                    scores(u, KT, 0).then_inc(*I(u, "s1a"))
                    yield
                elif s == "s1b":
                    pe.wait_ge(dve_first[u], at(dve_first, u, "A1a"))
                    scores(u, KT, 1).then_inc(*I(u, "s1b"))
                    yield
                elif s == "cum":
                    pe.wait_ge(act_first[u], at(act_first, u, "lnG"))
                    pe.wait_ge(dve_first[u], at(dve_first, u, "A1b"))
                    if again(u):
                        pe.wait_ge(pool_first[u], before(pool_first, u, "acc_keep"))
                    mm(S[:, 0:LH], tri[:, :], logG[u][:, :], start=True, stop=False)
                    mm(S[:, 0:LH], ones[:, :], acc[u][:, :], start=False, stop=True).then_inc(*I(u, "cum"))
                    yield
                elif s == "o1":
                    pe.wait_ge(pool_first[u], at(pool_first, u, "Vu"))
                    read_out(u, QT, 1, S1, Vu, Ktok).then_inc(*I(u, "o1"))
                    yield
                elif s == "shift":
                    pe.wait_ge(dve_first[u], at(dve_first, u, "O1"))
                    if again(u):
                        pe.wait_ge(act_first[u], before(act_first, u, "O1p"))
                    mm(S[:, 0:D], shift[:, :], O1[u][:, :], start=True, stop=False)
                    mm(S[:, 0:D], last[:, :], O1p[u][:, :], start=False, stop=True).then_inc(*I(u, "shift"))
                    yield
                elif s == "s2a":
                    pe.wait_ge(dve_first[u], at(dve_first, u, "En"))
                    pe.wait_ge(pool_first[u], at(pool_first, u, "bd2a"))
                    pe.wait_ge(act_first[u], at(act_first, u, "K2tok"))
                    scores(u, K2T, 0).then_inc(*I(u, "s2a"))
                    yield
                elif s == "s2b":
                    pe.wait_ge(dve_first[u], at(dve_first, u, "A2a"))
                    scores(u, K2T, 1).then_inc(*I(u, "s2b"))
                    yield
                elif s == "o2":
                    pe.wait_ge(dve_first[u], at(dve_first, u, "A2b"))
                    read_out(u, QmT, 0, S2, En, K2tok).then_inc(*I(u, "o2"))
                    yield
                elif s == "OT":
                    pe.wait_ge(dve_first[u], at(dve_first, u, "O"))
                    for k in range(KD):
                        ins = tr(S[:, k * P:(k + 1) * P], En[u][:, k * P:(k + 1) * P], ident[:, :])
                    ins.then_inc(*I(u, "OT"))
                    yield
                elif s == "cproj":
                    pe.wait_ge(act_first[u], at(act_first, u, "OT"))
                    pe.wait_ge(dve_first[u], at(dve_first, u, "dS2"))
                    for k in range(KD):
                        ins = mm(S[:, BANK:BANK + D], OT[u][:, k * P:(k + 1) * P], cw[:, k, :],
                                 start=k == 0, stop=k == KD - 1)
                    ins.then_inc(*I(u, "cproj"))
                    yield

            def stage_layers(s, l, u):
                at, again, before, I = layers.at, layers.again, layers.before, layers.inc
                S = psum[LAYERS][u]
                if s == "h":
                    if l:
                        pe.wait_ge(dve_done[u], at(dve_done, u, f"x2_{l - 1}"))
                    else:
                        pe.wait_ge(act_done[u], at(act_done, u, "z"))
                    for k in range(KD):
                        ins = tr(S[:, BANK + k * P:BANK + (k + 1) * P], X[u][:, k * P:(k + 1) * P], ident[:, :])
                    ins.then_inc(*I(u, f"hT_{l}"))
                    yield
                elif s == "v":
                    if layers.first[u]:
                        pe.wait_ge(w_rest, 16 * DEPTH * 18)
                    pe.wait_ge(act_done[u], at(act_done, u, f"hT_{l}"))
                    for k in range(KD):
                        ins = mm(S[:, 0:INNER], (hT[u], xTs[l][u])[k][:, 0:P], wqkv_s[l][:, k, 2 * INNER:3 * INNER],
                                 start=k == 0, stop=k == KD - 1)
                    ins.then_inc(*I(u, f"v_{l}"))
                    yield
                elif s == "qk":
                    for n in (1, 0):
                        if n == 0:
                            pe.wait_ge(act_done[u], at(act_done, u, f"v_{l}"))
                        for k in range(KD):
                            ins = mm(S[:, n * BANK:(n + 1) * BANK], (hT[u], xTs[l][u])[k][:, 0:P],
                                     wqkv_s[l][:, k, n * INNER:(n + 1) * INNER], start=k == 0, stop=k == KD - 1)
                    ins.then_inc(*I(u, f"qk_{l}"))
                    yield
                elif s == "qkT":
                    pe.wait_ge(dve_done[u], at(dve_done, u, f"kn_{l}"))
                    for i in range(2 * AT):
                        ins = tr(S[:, i * P:(i + 1) * P], qkrot[u][:, i * P:(i + 1) * P], ident[:, :])
                    ins.then_inc(*I(u, f"qkT_{l}"))
                    yield
                elif s in ("s0", "s1", "s2", "s3"):
                    i = int(s[1])
                    if i == 0:
                        pe.wait_ge(act_done[u], at(act_done, u, f"kT_{l}"))
                    elif i > 1:
                        pe.wait_ge(dve_done[u], at(dve_done, u, f"m{i - 2}_{l}"))
                    for r in range(2):
                        c0 = (i % 2) * BANK + r * 2 * P
                        ins = mm(S[:, c0:c0 + 2 * P], qTd[u][:, i, r, :], kT[l][u][:, i, :], start=True, stop=True)
                    ins.then_inc(*I(u, f"{s}_{l}"))
                    yield
                elif s in ("p0", "p1", "p2", "p3"):
                    i = int(s[1])
                    pe.wait_ge(act_done[u], at(act_done, u, f"e{i}_{l}"))
                    if i < 2:
                        pe.wait_ge(dve_done[u], at(dve_done, u, f"m{i + 2}_{l}"))
                    else:
                        out_of_bank = act_done if i == 2 else dve_done
                        pe.wait_ge(out_of_bank[u], at(out_of_bank, u, f"p{i - 2}_{l}"))
                    for j in range(4):
                        c0 = (i % 2) * BANK + j * P
                        ins = tr(S[:, c0:c0 + P], big[u][:, 512 * i + j * P:512 * i + (j + 1) * P], ident[:, :])
                    ins.then_inc(*I(u, f"{s}_{l}"))
                    yield
                elif s == "av":
                    pe.wait_ge(act_done[u], at(act_done, u, f"p2_{l}"))
                    pe.wait_ge(dve_done[u], at(dve_done, u, f"p3_{l}"))
                    for h in range(AH):
                        o = S[:, h * AD:(h + 1) * AD]
                        mm(o, big[u][:, 256 * h:256 * h + P], prevV[l][u][:, h * AD:(h + 1) * AD],
                           start=True, stop=False)
                        ins = mm(o, big[u][:, 256 * h + P:256 * h + 256], vcur[u][:, h * AD:(h + 1) * AD],
                                 start=False, stop=True)
                    ins.then_inc(*I(u, f"av_{l}"))
                    yield
                elif s == "oT":
                    pe.wait_ge(dve_done[u], at(dve_done, u, f"on_{l}"))
                    for t in range(AT):
                        ins = tr(S[:, BANK + t * P:BANK + (t + 1) * P], on[u][:, t * P:(t + 1) * P], ident[:, :])
                    ins.then_inc(*I(u, f"oT_{l}"))
                    yield
                elif s == "wo":
                    pe.wait_ge(act_done[u], at(act_done, u, f"oT_{l}"))
                    for t in range(AT):
                        ins = mm(S[:, 0:D], oT[u][:, t, :], wo_s[l][:, t, :], start=t == 0, stop=t == AT - 1)
                    ins.then_inc(*I(u, f"wo_{l}"))
                    yield
                elif s == "xs":
                    pe.wait_ge(dve_done[u], at(dve_done, u, f"x_{l}"))
                    if again(u):
                        pe.wait_ge(act_done[u], before(act_done, u, f"xph2_{l}"))
                    mm(S[:, BANK:BANK + P], shift[:, :], X[u][:, P:D], start=True, stop=False)
                    mm(S[:, BANK:BANK + P], last[:, :], xph2[l][u][:, :],
                       start=False, stop=True).then_inc(*I(u, f"xs_{l}"))
                    yield
                elif s == "h2T":
                    pe.wait_ge(dve_done[u], at(dve_done, u, f"hn_{l}"))
                    for k in range(KD):
                        ins = tr(S[:, k * P:(k + 1) * P], hn[u][:, k * P:(k + 1) * P], ident[:, :])
                    ins.then_inc(*I(u, f"h2T_{l}"))
                    yield
                elif s in ("w1g", "w1a", "w1g2", "w1a2"):
                    if s == "w1g":
                        pe.wait_ge(act_done[u], at(act_done, u, f"h2T_{l}"))
                    elif s == "w1g2":
                        pe.wait_ge(act_done[u], at(act_done, u, f"gelu_{l}"))
                    elif s == "w1a2":
                        pe.wait_ge(dve_done[u], at(dve_done, u, f"hid_{l}"))
                    c, o = (0, HID) if s[2] == "g" else (BANK, 0)
                    for n, j in enumerate(HID_TILES[s[3:]]):
                        m = P if j < HT - 1 else HLAST
                        for k in range(KD):
                            ins = mm(S[0:m, c + n * P:c + (n + 1) * P], w1_s[l][:, k, o + j * P:o + j * P + m],
                                     hT[u][:, k * P:(k + 1) * P], start=k == 0, stop=k == KD - 1)
                    ins.then_inc(*I(u, f"{s}_{l}"))
                    yield
                elif s == "w2":
                    pe.wait_ge(dve_done[u], at(dve_done, u, f"hid2_{l}"))
                    for j in range(HT):
                        m = P if j < HT - 1 else HLAST
                        ins = mm(S[:, 0:D], big[u][0:m, 768 + j * P:768 + (j + 1) * P], w2_s[l][0:m, j, :],
                                 start=j == 0, stop=j == HT - 1)
                    ins.then_inc(*I(u, f"w2_{l}"))
                    yield

            walk(pe, "pe", (first, layers), (stage_first, stage_layers))

        @block.vector
        def _(dve):
            v = nc.vector
            dve.wait_ge(made2, 9)
            dve.wait_ge(w_first, 16 * 6)
            first, layers = Prog(dve_first), Prog(dve_done)

            def heads_of(t, n):
                return t.rearrange("p (h d) -> p h d", h=n)

            def settle(block_, u):
                v.memset(carry[block_][u][:, :], 0.0)

            def ln_stats(prog, block_, u, src, name):
                own, m = prog.done, mv[block_][u]
                v.bn_stats(st6[block_][u][:, 0, :], src).then_inc(*prog.inc(u, name + "_stats"))
                dve.wait_ge(own[u], prog.at(own, u, name + "_stats"))
                settle(block_, u)
                v.bn_aggr(m[:, :], st6[block_][u][:, 0, :]).then_inc(*prog.inc(u, name + "_agg"))
                dve.wait_ge(own[u], prog.at(own, u, name + "_agg"))
                v.tensor_scalar(ve[block_][u][:, :], m[:, 1:2], EPS, None, ALU.add).then_inc(*prog.inc(u, name + "_eps"))

            def ln_apply(prog, block_, u, dst, src, name, step):
                dve.wait_ge(prog.done[u], prog.at(prog.done, u, name + "_eps"))
                pool_steps = (pool_first, pool_done)[block_]
                dve.wait_ge(pool_steps[u], prog.at(pool_steps, u, name + "_rstd"))
                v.tensor_scalar(dst, src, mv[block_][u][:, 0:1], rstd[block_][u][:, 0:1], ALU.subtract,
                                ALU.mult).then_inc(*prog.inc(u, step))

            def masked(u, half, step):
                v.tensor_tensor(sc[u][:, 1024 * half:1024 * half + 1024].rearrange("p (h n) -> p h n", h=LPT),
                                psum[FIRST][u][:, :].rearrange("p (h n) -> p h n", h=LPT),
                                tri[:, None, :].to_broadcast([P, LPT, P]), ALU.mult).then_inc(*first.inc(u, step))

            def grow_state(u, state, n):
                ds = psum[FIRST][u][:, BANK:BANK + D].rearrange("p (t h e) -> p t h e", t=LT, h=LPT)
                dve.wait_ge(pool_first[u], first.at(pool_first, u, "hmk"))
                tmp = scr[u][:, :].rearrange("p (t h e) -> p t h e", t=LT, h=LPT)
                v.tensor_tensor(tmp, ds, hmk[u][:, None, :, None].to_broadcast([P, LT, LPT, LD]),
                                ALU.mult).then_inc(*first.inc(u, f"dS{n}"))
                dve.wait_ge(dve_first[u], first.at(dve_first, u, f"dS{n}"))
                st = state[u][:, :, :].rearrange("p t n -> p (t n)")
                v.scalar_tensor_tensor(st, st, fla[u][:, 1:2], scr[u][:, :], ALU.mult,
                                       ALU.add).then_inc(*first.inc(u, f"S{n}"))

            def head_blocks(u, dst, src, step):
                v.tensor_tensor(dst.rearrange("p (h n) -> p h n", h=LPT), src.to_broadcast([P, LPT, P]),
                                head1[:, :, None].to_broadcast([P, LPT, P]), ALU.mult).then_inc(*first.inc(u, step))

            def sigmoid_of_exp(u, t, step):
                v.tensor_scalar(t, t, 1.0, None, ALU.add).then_inc(*first.inc(u, step + "_1"))
                dve.wait_ge(dve_first[u], first.at(dve_first, u, step + "_1"))
                v.reciprocal(t, t).then_inc(*first.inc(u, step))

            def stage_first(s, l, u):
                at, again, before, I = first.at, first.again, first.before, first.inc
                S = psum[FIRST][u]
                if s == "ln0":
                    dve.wait_ge(x_in[u], first.chunk[u] * 16 + 16)
                    if again(u):
                        dve.wait_ge(dve_first[u], before(dve_first, u, "z"))
                    ln_stats(first, FIRST, u, xin[u][:, :], "ln0")
                    yield
                    if again(u):
                        dve.wait_ge(act_done[u], before(act_done, u, "z"))
                    ln_apply(first, FIRST, u, XA[u][:, :], xin[u][:, :], "ln0", "X")
                    yield
                elif s == "qT":
                    dve.wait_ge(act_first[u], at(act_first, u, "QmT"))
                    v.scalar_tensor_tensor(QmT[u][:, :, :], QT[u][:, :, :], -0.02 / LD ** 0.5, QmT[u][:, :, :], ALU.mult,
                                           ALU.max).then_inc(*I(u, "Qm"))
                    yield
                    if again(u):
                        dve.wait_ge(pe_first[u], before(pe_first, u, "o2"))
                    head_blocks(u, sc[u][:, 0:1024], QT[u][:, 0:1, 1:P + 1], "bd1a")
                    yield
                    head_blocks(u, sc[u][:, 1024:2048], QT[u][:, 1:2, 1:P + 1], "bd1b")
                    yield
                elif s == "kT":
                    dve.wait_ge(act_first[u], at(act_first, u, "K2T"))
                    sigmoid_of_exp(u, K2T[u][:, :, :], "K2T")
                    yield
                elif s == "tok":
                    dve.wait_ge(act_first[u], at(act_first, u, "Ktok"))
                    v.tensor_tensor(heads_of(scr[u][:, :], LH), heads_of(Ktok[u][:, :], LH),
                                    swb[:, None, :].to_broadcast([P, LH, LD]), ALU.mult).then_inc(*I(u, "rdot"))
                    dve.wait_ge(dve_first[u], at(dve_first, u, "rdot"))
                    v.tensor_reduce(zz[u][:, LH:2 * LH], heads_of(scr[u][:, :], LH), AX.X,
                                    ALU.add).then_inc(*I(u, "rsum"))
                    yield
                    dve.wait_ge(pool_first[u], at(pool_first, u, "gdot"))
                    v.tensor_reduce(zz[u][:, 0:LH], heads_of(scr2[u][:, :], LH), AX.X,
                                    ALU.add).then_inc(*I(u, "gsum"))
                    yield
                    dve.wait_ge(act_first[u], at(act_first, u, "egate"))
                    v.tensor_scalar(ez[u][:, :], ez[u][:, :], 1.0, None, ALU.add).then_inc(*I(u, "e1"))
                    dve.wait_ge(dve_first[u], at(dve_first, u, "e1"))
                    v.reciprocal(sig[u][:, :], ez[u][:, :]).then_inc(*I(u, "sig"))
                    dve.wait_ge(dve_first[u], at(dve_first, u, "sig"))
                    v.tensor_scalar(gr[u][:, 0:LH], sig[u][:, 0:LH], 1e-6, None, ALU.max).then_inc(*I(u, "G"))
                    v.tensor_tensor(gr[u][:, LH:2 * LH], zz[u][:, LH:2 * LH], sig[u][:, LH:2 * LH],
                                    ALU.mult).then_inc(*I(u, "R"))
                    yield
                elif s == "cum":
                    dve.wait_ge(pe_first[u], at(pe_first, u, "cum"))
                    v.tensor_scalar(lc[u][:, :], S[:, 0:LH], 30.0, None, ALU.min).then_inc(*I(u, "Lmin"))
                    dve.wait_ge(dve_first[u], at(dve_first, u, "Lmin"))
                    v.tensor_scalar(lc[u][:, :], lc[u][:, :], -30.0, None, ALU.max).then_inc(*I(u, "Lclip"))
                    yield
                    dve.wait_ge(act_first[u], at(act_first, u, "eL"))
                    v.tensor_scalar(gc[u][:, :], gc[u][:, :], 1e-6, None, ALU.add).then_inc(*I(u, "Gc"))
                    dve.wait_ge(dve_first[u], at(dve_first, u, "Gc"))
                    v.reciprocal(rgc[u][:, :], gc[u][:, :]).then_inc(*I(u, "rGc"))
                    dve.wait_ge(dve_first[u], at(dve_first, u, "rGc"))
                    v.tensor_tensor(uu[u][:, :], gr[u][:, LH:2 * LH], rgc[u][:, :], ALU.mult).then_inc(*I(u, "u"))
                    yield
                elif s == "s1a":
                    dve.wait_ge(pe_first[u], at(pe_first, u, "s1a"))
                    masked(u, 0, "A1a")
                    yield
                elif s == "s1b":
                    dve.wait_ge(pe_first[u], at(pe_first, u, "s1b"))
                    masked(u, 1, "A1b")
                    yield
                elif s == "o1":
                    dve.wait_ge(pe_first[u], at(pe_first, u, "o1"))
                    v.tensor_tensor(heads_of(O1[u][:, :], LH), heads_of(S[:, 0:D], LH),
                                    gc[u][:, :, None].to_broadcast([P, LH, LD]), ALU.mult).then_inc(*I(u, "O1"))
                    yield
                    grow_state(u, S1, 1)
                    yield
                    head_blocks(u, sc[u][:, 1024:2048], QmT[u][:, 1:2, 0:P], "bd2b")
                    yield
                elif s == "shift":
                    dve.wait_ge(pe_first[u], at(pe_first, u, "shift"))
                    v.tensor_tensor(En[u][:, :], S[:, 0:D], XA[u][:, :], ALU.subtract).then_inc(*I(u, "En"))
                    dve.wait_ge(dve_first[u], at(dve_first, u, "En"))
                    v.tensor_scalar(En[u][:, :], En[u][:, :], fla[u][:, 2:3], None,
                                    ALU.mult).then_inc(*I(u, "En0"))
                    yield
                elif s == "s2a":
                    dve.wait_ge(pe_first[u], at(pe_first, u, "s2a"))
                    masked(u, 0, "A2a")
                    yield
                elif s == "s2b":
                    dve.wait_ge(pe_first[u], at(pe_first, u, "s2b"))
                    masked(u, 1, "A2b")
                    yield
                elif s == "o2":
                    dve.wait_ge(pe_first[u], at(pe_first, u, "o2"))
                    v.tensor_tensor(En[u][:, :], S[:, 0:D], O1[u][:, :], ALU.add).then_inc(*I(u, "O"))
                    yield
                    grow_state(u, S2, 2)
                    yield
                elif s == "cproj":
                    dve.wait_ge(pe_first[u], at(pe_first, u, "cproj"))
                    ln_stats(first, FIRST, u, S[:, BANK:BANK + D], "lnc")
                    yield
                    ln_apply(first, FIRST, u, scr[u][:, :], S[:, BANK:BANK + D], "lnc", "lnc")
                    dve.wait_ge(dve_first[u], at(dve_first, u, "lnc"))
                    v.tensor_tensor(scr[u][:, :], scr[u][:, :], xin[u][:, :], ALU.add).then_inc(*I(u, "mid_x"))
                    yield
                    dve.wait_ge(dve_first[u], at(dve_first, u, "mid_x"))
                    ln_stats(first, FIRST, u, scr[u][:, :], "lnz")
                    yield
                    ln_apply(first, FIRST, u, XA[u][:, :], scr[u][:, :], "lnz", "z")
                    yield

            def stage_layers(s, l, u):
                at, again, before, I = layers.at, layers.again, layers.before, layers.inc
                S = psum[LAYERS][u]
                if s == "rot":
                    dve.wait_ge(act_done[u], at(act_done, u, f"sq_{l}"))
                    v.tensor_reduce(ssq[u][:, :], heads_of(big[u][:, 0:1024], 2 * AH), AX.X,
                                    ALU.add).then_inc(*I(u, f"ss_{l}"))
                    dve.wait_ge(dve_done[u], at(dve_done, u, f"ss_{l}"))
                    v.tensor_scalar(ssq[u][:, :], ssq[u][:, :], 1e-24, None, ALU.max).then_inc(*I(u, f"ss_clip_{l}"))
                    yield
                    dve.wait_ge(pool_done[u], at(pool_done, u, f"tab_{l}"))
                    tb = tabl[u]
                    v.tensor_tensor(qkrot[u].rearrange("p (s h d) -> p s h d", s=2, h=AH),
                                    S[:, :].rearrange("p (s h d) -> p s h d", s=2, h=AH),
                                    tb[:, 0:4:2, None, :].to_broadcast([P, 2, AH, AD]),
                                    ALU.mult).then_inc(*I(u, f"t1_{l}"))
                    yield
                    raw = S[:, :].rearrange("p (s h a d) -> p s h a d", s=2, h=AH, a=2)
                    t2 = big[u][:, 1024:2048].rearrange("p (s h a d) -> p s h a d", s=2, h=AH, a=2)
                    half = AD // 2
                    for a in range(2):
                        ins = v.tensor_tensor(t2[:, :, :, a, :], raw[:, :, :, 1 - a, :],
                                              tb[:, 1:4:2, None, a * half:(a + 1) * half].to_broadcast(
                                                  [P, 2, AH, half]), ALU.mult)
                    ins.then_inc(*I(u, f"t2_{l}"))
                    yield
                    dve.wait_ge(dve_done[u], at(dve_done, u, f"t2_{l}"))
                    v.tensor_tensor(qkrot[u], qkrot[u], big[u][:, 1024:2048], ALU.add).then_inc(*I(u, f"rot_{l}"))
                    yield
                    dve.wait_ge(dve_done[u], at(dve_done, u, f"rot_{l}"))
                    dve.wait_ge(pool_done[u], at(pool_done, u, f"rnorm_{l}"))
                    k = heads_of(qkrot[u][:, INNER:2 * INNER], AH)
                    v.tensor_tensor(k, k, rnorm[u][:, AH:2 * AH, None].to_broadcast([P, AH, AD]),
                                    ALU.mult).then_inc(*I(u, f"kn_{l}"))
                    v.tensor_scalar(sc8[u][:, :], rnorm[u][:, 0:AH], QK_SCALE, None,
                                    ALU.mult).then_inc(*I(u, f"sc8_{l}"))
                    yield
                elif s in ("s0", "s1", "s2", "s3"):
                    i = int(s[1])
                    dve.wait_ge(pe_done[u], at(pe_done, u, f"{s}_{l}"))
                    if i == 0:
                        dve.wait_ge(dve_done[u], at(dve_done, u, f"sc8_{l}"))
                        dve.wait_ge(pool_done[u], at(pool_done, u, "band"))
                    settle(LAYERS, u)
                    for r in range(2):
                        h = 2 * i + r
                        c0 = (i % 2) * BANK + r * 2 * P
                        ins = v.tensor_tensor_reduce(big[u][:, 256 * h:256 * h + 256], S[:, c0:c0 + 2 * P],
                                                     bandu[u][:, :], 1.0, MASKED, ALU.add, ALU.max, mx[u][:, h:h + 1])
                    ins.then_inc(*I(u, f"m{i}_{l}"))
                    dve.wait_ge(dve_done[u], at(dve_done, u, f"m{i}_{l}"))
                    v.scalar_tensor_tensor(nb[u][:, 2 * i:2 * i + 2], mx[u][:, 2 * i:2 * i + 2], -1.0,
                                           sc8[u][:, 2 * i:2 * i + 2], ALU.mult, ALU.mult).then_inc(*I(u, f"nb{i}_{l}"))
                    yield
                elif s in ("p1", "p3"):
                    i = int(s[1])
                    dve.wait_ge(pe_done[u], at(pe_done, u, f"p{i}_{l}"))
                    v.tensor_copy(big[u][:, 512 * i:512 * i + 512], S[:, BANK:1024]).then_inc(*I(u, f"p{i}_{l}"))
                    yield
                elif s == "av":
                    v.reciprocal(rden[u][:, :], den[u][:, :]).then_inc(*I(u, f"rden_{l}"))
                    dve.wait_ge(dve_done[u], at(dve_done, u, f"rden_{l}"))
                    yield
                    dve.wait_ge(pe_done[u], at(pe_done, u, f"av_{l}"))
                    v.tensor_tensor(heads_of(on[u], AH), heads_of(S[:, 0:INNER], AH),
                                    rden[u][:, :, None].to_broadcast([P, AH, AD]), ALU.mult).then_inc(*I(u, f"on_{l}"))
                    yield
                elif s == "wo":
                    dve.wait_ge(pe_done[u], at(pe_done, u, f"wo_{l}"))
                    v.tensor_tensor(X[u][:, :], X[u][:, :], S[:, 0:D], ALU.add).then_inc(*I(u, f"x_{l}"))
                    yield
                elif s == "xs":
                    dve.wait_ge(pe_done[u], at(pe_done, u, f"xs_{l}"))
                    dve.wait_ge(dve_done[u], at(dve_done, u, f"x_{l}"))
                    st, m, sh = st6[LAYERS][u], mv[LAYERS][u], S[:, BANK:BANK + P]
                    v.bn_stats(st[:, 0, :], X[u][:, 0:P]).then_inc(*I(u, f"st_a_{l}"))
                    v.bn_stats(st[:, 1, :], sh).then_inc(*I(u, f"st_b_{l}"))
                    dve.wait_ge(dve_done[u], at(dve_done, u, f"st_b_{l}"))
                    settle(LAYERS, u)
                    v.bn_aggr(m[:, :], st[:, :, :].rearrange("p a b -> p (a b)")).then_inc(*I(u, f"ln_agg_{l}"))
                    dve.wait_ge(dve_done[u], at(dve_done, u, f"ln_agg_{l}"))
                    v.tensor_scalar(ve[LAYERS][u][:, :], m[:, 1:2], EPS, None, ALU.add).then_inc(*I(u, f"ln_eps_{l}"))
                    if l == 0:
                        if layers.again(u):
                            dve.wait_ge(stored[u], layers.chunk[u] * 16)
                    yield
                    dve.wait_ge(pool_done[u], at(pool_done, u, f"ln_rstd_{l}"))
                    r = rstd[LAYERS][u][:, 0:1]
                    v.tensor_scalar(hn[u][:, 0:P], X[u][:, 0:P], m[:, 0:1], r, ALU.subtract, ALU.mult)
                    v.tensor_scalar(hn[u][:, P:D], sh, m[:, 0:1], r,
                                    ALU.subtract, ALU.mult).then_inc(*I(u, f"hn_{l}"))
                    yield
                elif s in ("w1a", "w1a2"):
                    n = s[3:]
                    if layers.first[u]:
                        dve.wait_ge(w_rest, 16 * DEPTH * 18)
                    dve.wait_ge(pe_done[u], at(pe_done, u, f"{s}_{l}"))
                    dve.wait_ge(act_done[u], at(act_done, u, f"gelu{n}_{l}"))
                    for i, j in enumerate(HID_TILES[n]):
                        m = P if j < HT - 1 else HLAST
                        ins = v.scalar_tensor_tensor(big[u][0:m, 768 + j * P:768 + (j + 1) * P],
                                                     S[0:m, BANK + i * P:BANK + (i + 1) * P], b1a[l][0:m, j:j + 1],
                                                     big[u][0:m, j * P:(j + 1) * P], ALU.add, ALU.mult)
                    ins.then_inc(*I(u, f"hid{n}_{l}"))
                    yield
                elif s == "w2":
                    dve.wait_ge(pe_done[u], at(pe_done, u, f"w2_{l}"))
                    dve.wait_ge(pool_done[u], at(pool_done, u, f"xb2_{l}"))
                    v.tensor_tensor(X[u][:, :], X[u][:, :], S[:, 0:D], ALU.add).then_inc(*I(u, f"x2_{l}"))
                    yield
                elif s == "out":
                    dve.wait_ge(dve_done[u], at(dve_done, u, f"x2_{DEPTH - 1}"))
                    ln_stats(layers, LAYERS, u, X[u][:, :], "lnf")
                    yield
                    ln_apply(layers, LAYERS, u, X[u][:, :], X[u][:, :], "lnf", "lnf")
                    dve.wait_ge(dve_done[u], at(dve_done, u, "lnf"))
                    yield
                    dve.wait_ge(pe_done[u], at(pe_done, u, f"w2_{DEPTH - 1}"))
                    v.tensor_tensor(xo[u][:, :], X[u][:, :], x1[u][:, :], ALU.add).then_inc(*I(u, "out"))
                    yield

            walk(dve, "dve", (first, layers), (stage_first, stage_layers))


def kernel(**inputs):
    import numpy as _np
    import concourse.bacc as _bacc
    from concourse import mybir as _mybir
    from concourse.bass_utils import run_bass_kernel_spmd as _run

    nc = _bacc.Bacc("TRN2", target_bir_lowering=False, num_devices=1)
    half_idx = _np.arange(0, AD, 2, dtype=_np.float64)
    t = _np.arange(SEQ, dtype=_np.float64)
    inv_freq = (1.0 / 10000.0 ** (half_idx / AD)).astype(_np.float32).astype(_np.float64)
    freqs = (t[:, None] * inv_freq[None, :]).astype(_np.float32).astype(_np.float64)
    freqs = _np.concatenate([freqs, freqs], axis=-1)
    base = (half_idx + 0.4 * AD) / (1.4 * AD)
    scale = base[None, :] ** ((t - SEQ // 2) / 64.0)[:, None]
    scale = _np.concatenate([scale, scale], axis=-1)
    sign = _np.concatenate([-_np.ones(AD // 2), _np.ones(AD // 2)])
    cos, sin = _np.cos(freqs), _np.sin(freqs) * sign
    xpos = _np.concatenate([cos * scale, sin * scale, cos / scale, sin / scale], axis=-1)
    flags = _np.ones((STEPS, P, 4))
    flags[:, :, 3] = 0.0
    flags[::CHUNKS, :, 0] = 0.0
    flags[CHUNKS - 1::CHUNKS, :, 1] = 0.0
    flags[::CHUNKS, 0, 2] = 0.0
    flags[::CHUNKS, :, 3] = MASKED
    table = _np.concatenate([_np.tile(xpos, (BATCH // UNITS, 1)), flags.reshape(STEPS * P, 4)],
                            axis=-1).astype(_np.float32)

    def arr(name):
        return _np.ascontiguousarray(inputs[name])

    data = {
        "x": arr("L0_attn_X").reshape(BATCH * SEQ, D), "table": table,
        "q1T": _np.ascontiguousarray(arr("L0_attn_q1_w").T), "k1T": _np.ascontiguousarray(arr("L0_attn_k1_w").T),
        "k2T": _np.ascontiguousarray(arr("L0_attn_k2_w").T),
        "gw": arr("L0_attn_gw_w"), "sw": arr("L0_attn_sw_w"),
        "cT": _np.ascontiguousarray(arr("L0_attn_c_proj_w").T),
        "wqkv": arr("L0_ffn_wqkv"), "qs": arr("L0_ffn_q_scale"), "ks": arr("L0_ffn_k_scale"),
        "wo": arr("L0_ffn_wo"), "lg": arr("L0_ffn_ln_g"), "lb": arr("L0_ffn_ln_b"),
        "w1": arr("L0_ffn_w1"), "b1": arr("L0_ffn_b1"), "w2": arr("L0_ffn_w2"), "b2": arr("L0_ffn_b2"),
    }
    args = [nc.dram_tensor(n, a.shape, _mybir.dt.from_np(a.dtype), kind="ExternalInput").ap()
            for n, a in data.items()]
    args.append(nc.dram_tensor("out", (BATCH * SEQ, D), F32, kind="ExternalOutput").ap())
    build(nc, *args)
    r = _run(nc, [data], core_ids=[0])
    return r.results[0]["out"].reshape(BATCH, SEQ, D)
```
